# Optimizing a Trainium2 kernel written in Bass

```python
import numpy as np
import jax
import jax.numpy as jnp

def _softmax(x, axis=-1):
    return jax.nn.softmax(x, axis=axis)

def _gelu(x):
    return jax.nn.gelu(x, approximate=True)

def _silu(x):
    return jax.nn.silu(x)

def _sigmoid(x):
    return jax.nn.sigmoid(x)

def _layernorm(x, axis=-1, eps=1e-05):
    m = jnp.mean(x, axis=axis, keepdims=True)
    v = jnp.var(x, axis=axis, keepdims=True)
    return (x - m) / jnp.sqrt(v + eps)

def _scatter_add(tgt, idx, src, axis=0):
    return tgt.at[idx].add(src)

def _segment_sum(src, seg, n):
    return jax.ops.segment_sum(src, seg, n)
kernel_name = 'mk_xattn_ffn_d2_seqx_r4_f7cb9f'

def setup_inputs(seed: int=0):
    np.random.seed(seed)
    _w = jnp.asarray

    def _rec_inputs():
        import jax
        import jax.numpy as jnp
        _rk = jax.random.key(seed)
        x = -0.000929 + 1 * jax.random.normal(jax.random.fold_in(_rk, 1), (16, 128, 512), jnp.float32)
        _lenS = 128 - jax.random.randint(jax.random.fold_in(_rk, 7), (16,), 0, max(1, 128 // 4) + 1, jnp.int32)
        _lenS2 = 128 - jax.random.randint(jax.random.fold_in(_rk, 8), (16,), 0, max(1, 128 // 4) + 1, jnp.int32)
        _ctx_2048P = jax.random.normal(jax.random.fold_in(_rk, 11), (16, 16, 512), jnp.float32)
        _ctx_2048c = jax.random.dirichlet(jax.random.fold_in(_rk, 511), 0.3 * jnp.ones((16,), jnp.float32), (16, 128))
        _ctx_2048t = jnp.einsum('bsk,bkd->bsd', _ctx_2048c, _ctx_2048P)
        _ctx_2048t = _ctx_2048t * jax.lax.rsqrt(jnp.mean(jnp.square(_ctx_2048t)) + 1e-12) * 0.953939
        ctx_2048 = 2.81802e-05 + 1.00001 * (_ctx_2048t + 0.3 * jax.random.normal(jax.random.fold_in(_rk, 611), (16, 128, 512), jnp.float32))
        _validS = jnp.arange(128)[None, :] < _lenS[:, None]
        _validS2 = jnp.arange(128)[None, :] < _lenS2[:, None]
        _causal = jnp.tril(jnp.ones((128, 128), dtype=bool))
        mask_BxS2_bk0 = jnp.logical_not(jnp.broadcast_to(_validS2[:, :], (16, 128)))
        return (x, ctx_2048, mask_BxS2_bk0)
    x, ctx_2048, mask_BxS2_bk0 = _rec_inputs()

    def _L0_xattn_setup():
        import jax, jax.numpy as jnp
        import numpy as np
        from jax import lax
        LN_EPS = 1e-05
        key = jax.random.key(seed)
        ks = jax.random.split(key, 8)
        B, S, T, D = (4, 128, 512, 512)
        scale = 0.02
        return {'Z': jax.random.normal(ks[0], (B, S, D), dtype=jnp.float32), 'kv': jax.random.normal(ks[1], (B, T, D), dtype=jnp.float32), 'decay': jnp.float32(0.9), 'W_in': jax.random.normal(ks[2], (D, D), dtype=jnp.float32) * scale, 'b_in': jnp.zeros((D,), dtype=jnp.float32), 'W_out': jax.random.normal(ks[3], (D, D), dtype=jnp.float32) * scale, 'b_out': jnp.zeros((D,), dtype=jnp.float32), 'gamma': jnp.ones((D,), dtype=jnp.float32), 'beta': jnp.zeros((D,), dtype=jnp.float32)}
    _L0_xattn_all = _L0_xattn_setup()
    _L0_xattn_in = {k: v for k, v in _L0_xattn_all.items() if k in ('decay', 'W_in', 'b_in', 'W_out', 'b_out', 'gamma', 'beta')}
    del _L0_xattn_all

    def _L0_ffn_setup():
        import jax, jax.numpy as jnp
        import numpy as np
        EPS = 1e-05
        RMS_EPS = 1e-06

        def activation_quant(x, num_bits=8):
            qn = -2 ** (num_bits - 1)
            qp = 2 ** (num_bits - 1) - 1
            xf = x.astype(jnp.float32)
            s = qp / jnp.clip(jnp.max(jnp.abs(xf), axis=-1, keepdims=True), EPS, None)
            return (jnp.clip(jnp.round(xf * s), qn, qp) / s).astype(x.dtype)

        def weight_quant(w):
            wf = w.astype(jnp.float32)
            s = 1.0 / jnp.clip(jnp.mean(jnp.abs(wf)), EPS, None)
            return (jnp.clip(jnp.round(wf * s), -1.0, 1.0) / s).astype(w.dtype)

        def bit_linear(x, w):
            qx = x + jax.lax.stop_gradient(activation_quant(x) - x)
            qw = w + jax.lax.stop_gradient(weight_quant(w) - w)
            return jnp.einsum('bsh,oh->bso', qx, qw)

        def rms_norm(x, weight, eps=RMS_EPS):
            xf = x.astype(jnp.float32)
            var = jnp.mean(xf * xf, axis=-1, keepdims=True)
            return weight * (xf * jax.lax.rsqrt(var + eps)).astype(x.dtype)
        key = jax.random.key(seed)
        k1, k2, k3, k4 = jax.random.split(key, 4)
        B, S, H, I = (2, 512, 512, 2048)
        scale = 1.0 / np.sqrt(H)
        return {'x': jax.random.normal(k1, (B, S, H), dtype=jnp.float32), 'w_gate': jax.random.normal(k2, (I, H), dtype=jnp.float32) * scale, 'w_up': jax.random.normal(k3, (I, H), dtype=jnp.float32) * scale, 'w_down': jax.random.normal(k4, (H, I), dtype=jnp.float32) * (1.0 / np.sqrt(I)), 'ln_weight': jnp.ones((I,), dtype=jnp.float32)}
    _L0_ffn_all = _L0_ffn_setup()
    _L0_ffn_in = {k: v for k, v in _L0_ffn_all.items() if k in ('w_gate', 'w_up', 'w_down', 'ln_weight')}
    del _L0_ffn_all

    def _L1_xattn_setup():
        import jax, jax.numpy as jnp
        import numpy as np
        key = jax.random.key(seed)
        k1, k2, k3 = jax.random.split(key, 3)
        B, S, D, M = (8, 512, 512, 128)
        hidden_states = jax.random.normal(k1, (B, S, D), dtype=jnp.float32)
        memory_tokens = jax.random.normal(k2, (B, M, D), dtype=jnp.float32)
        memory_mask = jax.random.randint(k3, (B, M), 0, 2).astype(jnp.bool_)
        return {'hidden_states': hidden_states, 'memory_tokens': memory_tokens, 'memory_mask': memory_mask}
    _L1_xattn_all = _L1_xattn_setup()
    _L1_xattn_in = {k: v for k, v in _L1_xattn_all.items() if k in ()}
    del _L1_xattn_all

    def _L1_ffn_setup():
        import jax, jax.numpy as jnp
        import numpy as np
        N_EXPERTS = 8
        TOP_K = 2
        C = 512
        H = 256
        HS = 512
        B, T = (1, 128)
        SCALE = 0.02
        key = jax.random.key(seed)
        ks = jax.random.split(key, 10)
        x = jax.random.normal(ks[0], (B, T, C), dtype=jnp.float32)
        gate_w = jax.random.normal(ks[1], (N_EXPERTS, C), dtype=jnp.float32) * SCALE
        w_gate = jax.random.normal(ks[2], (N_EXPERTS, H, C), dtype=jnp.float32) * SCALE
        w_up = jax.random.normal(ks[3], (N_EXPERTS, H, C), dtype=jnp.float32) * SCALE
        w_down = jax.random.normal(ks[4], (N_EXPERTS, C, H), dtype=jnp.float32) * SCALE
        sh_gate = jax.random.normal(ks[5], (HS, C), dtype=jnp.float32) * SCALE
        sh_up = jax.random.normal(ks[6], (HS, C), dtype=jnp.float32) * SCALE
        sh_down = jax.random.normal(ks[7], (C, HS), dtype=jnp.float32) * SCALE
        se_gate_w = jax.random.normal(ks[8], (1, C), dtype=jnp.float32) * SCALE
        return {'x': x, 'gate_w': gate_w, 'w_gate': w_gate, 'w_up': w_up, 'w_down': w_down, 'sh_gate': sh_gate, 'sh_up': sh_up, 'sh_down': sh_down, 'se_gate_w': se_gate_w}
    _L1_ffn_all = _L1_ffn_setup()
    _L1_ffn_in = {k: v for k, v in _L1_ffn_all.items() if k in ('gate_w', 'w_gate', 'w_up', 'w_down', 'sh_gate', 'sh_up', 'sh_down', 'se_gate_w')}
    del _L1_ffn_all
    return {'x': x, 'ctx_2048': ctx_2048, 'mask_BxS2_bk0': mask_BxS2_bk0, 'L0_xattn_decay': _L0_xattn_in['decay'], 'L0_xattn_W_in': _L0_xattn_in['W_in'], 'L0_xattn_b_in': _L0_xattn_in['b_in'], 'L0_xattn_W_out': _L0_xattn_in['W_out'], 'L0_xattn_b_out': _L0_xattn_in['b_out'], 'L0_xattn_gamma': _L0_xattn_in['gamma'], 'L0_xattn_beta': _L0_xattn_in['beta'], 'L0_ffn_w_gate': _L0_ffn_in['w_gate'], 'L0_ffn_w_up': _L0_ffn_in['w_up'], 'L0_ffn_w_down': _L0_ffn_in['w_down'], 'L0_ffn_ln_weight': _L0_ffn_in['ln_weight'], 'L1_ffn_gate_w': _L1_ffn_in['gate_w'], 'L1_ffn_w_gate': _L1_ffn_in['w_gate'], 'L1_ffn_w_up': _L1_ffn_in['w_up'], 'L1_ffn_w_down': _L1_ffn_in['w_down'], 'L1_ffn_sh_gate': _L1_ffn_in['sh_gate'], 'L1_ffn_sh_up': _L1_ffn_in['sh_up'], 'L1_ffn_sh_down': _L1_ffn_in['sh_down'], 'L1_ffn_se_gate_w': _L1_ffn_in['se_gate_w']}

def reference(x, ctx_2048, mask_BxS2_bk0, L0_xattn_decay, L0_xattn_W_in, L0_xattn_b_in, L0_xattn_W_out, L0_xattn_b_out, L0_xattn_gamma, L0_xattn_beta, L0_ffn_w_gate, L0_ffn_w_up, L0_ffn_w_down, L0_ffn_ln_weight, L1_ffn_gate_w, L1_ffn_w_gate, L1_ffn_w_up, L1_ffn_w_down, L1_ffn_sh_gate, L1_ffn_sh_up, L1_ffn_sh_down, L1_ffn_se_gate_w):
    import jax
    import jax.numpy as jnp

    def _L0_xattn_ref(Z, kv, decay, W_in, b_in, W_out, b_out, gamma, beta):
        import jax, jax.numpy as jnp
        import numpy as np
        from jax import lax
        LN_EPS = 1e-05
        B, T, D = kv.shape
        K = jax.nn.sigmoid(decay)
        x = jnp.einsum('btd,ed->bte', kv, W_in) + b_in

        def scan_fn(s, xt):
            s = K * s + xt
            return (s, s)
        s0 = jnp.zeros((B, D), dtype=kv.dtype)
        _, states = lax.scan(scan_fn, s0, jnp.swapaxes(x, 0, 1))
        states = jnp.swapaxes(states, 0, 1)
        proj = jnp.einsum('btd,ed->bte', states, W_out) + b_out
        summary = jnp.mean(proj, axis=1, keepdims=True)
        y = Z + summary
        mu = jnp.mean(y, axis=-1, keepdims=True)
        var = jnp.mean((y - mu) ** 2, axis=-1, keepdims=True)
        return (y - mu) / jnp.sqrt(var + LN_EPS) * gamma + beta

    def _L0_ffn_ref(x, w_gate, w_up, w_down, ln_weight):
        import jax, jax.numpy as jnp
        import numpy as np
        EPS = 1e-05
        RMS_EPS = 1e-06

        def activation_quant(x, num_bits=8):
            qn = -2 ** (num_bits - 1)
            qp = 2 ** (num_bits - 1) - 1
            xf = x.astype(jnp.float32)
            s = qp / jnp.clip(jnp.max(jnp.abs(xf), axis=-1, keepdims=True), EPS, None)
            return (jnp.clip(jnp.round(xf * s), qn, qp) / s).astype(x.dtype)

        def weight_quant(w):
            wf = w.astype(jnp.float32)
            s = 1.0 / jnp.clip(jnp.mean(jnp.abs(wf)), EPS, None)
            return (jnp.clip(jnp.round(wf * s), -1.0, 1.0) / s).astype(w.dtype)

        def bit_linear(x, w):
            qx = x + jax.lax.stop_gradient(activation_quant(x) - x)
            qw = w + jax.lax.stop_gradient(weight_quant(w) - w)
            return jnp.einsum('bsh,oh->bso', qx, qw)

        def rms_norm(x, weight, eps=RMS_EPS):
            xf = x.astype(jnp.float32)
            var = jnp.mean(xf * xf, axis=-1, keepdims=True)
            return weight * (xf * jax.lax.rsqrt(var + eps)).astype(x.dtype)
        h = jax.nn.silu(bit_linear(x, w_gate)) * bit_linear(x, w_up)
        h = rms_norm(h, ln_weight)
        return bit_linear(h, w_down)

    def _L1_xattn_ref(hidden_states, memory_tokens, memory_mask):
        import jax, jax.numpy as jnp
        import numpy as np
        B, S, D = hidden_states.shape
        scale = 1.0 / jnp.sqrt(jnp.asarray(D, hidden_states.dtype))
        scores = jnp.einsum('bsd,bmd->bsm', hidden_states, memory_tokens) * scale
        neg_inf = jnp.asarray(-1e+30, scores.dtype)
        scores = jnp.where(memory_mask[:, None, :], scores, neg_inf)
        attn = jax.nn.softmax(scores, axis=-1)
        readout = jnp.einsum('bsm,bmd->bsd', attn, memory_tokens)
        valid_b = jnp.any(memory_mask, axis=-1)
        out = jnp.where(valid_b[:, None, None], readout, jnp.zeros_like(readout))
        return out

    def _L1_ffn_ref(x, gate_w, w_gate, w_up, w_down, sh_gate, sh_up, sh_down, se_gate_w):
        import jax, jax.numpy as jnp
        import numpy as np
        N_EXPERTS = 8
        TOP_K = 2
        C = 512
        H = 256
        HS = 512
        B, T = (1, 128)
        SCALE = 0.02
        Bb, Tt, Cc = x.shape
        xf = x.reshape(-1, Cc)
        scores = xf @ gate_w.T
        ew, ei = jax.lax.top_k(scores, TOP_K)
        ew = jax.nn.softmax(ew, axis=-1)
        x1 = jax.nn.silu(jnp.einsum('td,ehd->teh', xf, w_gate))
        x3 = jnp.einsum('td,ehd->teh', xf, w_up)
        expert_out = jnp.einsum('teh,edh->ted', x1 * x3, w_down)
        onehot = jax.nn.one_hot(ei, N_EXPERTS, dtype=ew.dtype)
        comb = jnp.einsum('ta,tae->te', ew, onehot)
        routed = jnp.einsum('te,ted->td', comb, expert_out)
        shared = jax.nn.silu(xf @ sh_gate.T) * (xf @ sh_up.T) @ sh_down.T
        sgate = jax.nn.sigmoid(xf @ se_gate_w.T)
        return (routed + sgate * shared).reshape(Bb, Tt, Cc)
    x = x + _L0_xattn_ref(_layernorm(x, axis=-1), ctx_2048, L0_xattn_decay, L0_xattn_W_in, L0_xattn_b_in, L0_xattn_W_out, L0_xattn_b_out, L0_xattn_gamma, L0_xattn_beta)
    x = x + _L0_ffn_ref(_layernorm(x, axis=-1), L0_ffn_w_gate, L0_ffn_w_up, L0_ffn_w_down, L0_ffn_ln_weight)
    x = x + _L1_xattn_ref(_layernorm(x, axis=-1), ctx_2048, mask_BxS2_bk0)
    x = x + _L1_ffn_ref(_layernorm(x, axis=-1), L1_ffn_gate_w, L1_ffn_w_gate, L1_ffn_w_up, L1_ffn_w_down, L1_ffn_sh_gate, L1_ffn_sh_up, L1_ffn_sh_down, L1_ffn_se_gate_w)
    return x

_drawn_inputs = setup_inputs


def setup_inputs(seed=0):
    import zlib

    import numpy as np

    out = dict(_drawn_inputs(seed))
    spreads = {'L0_xattn_b_in': (0.0, 0.1),
     'L0_xattn_b_out': (0.0, 0.1),
     'L0_xattn_gamma': (1.0, 0.2),
     'L0_xattn_beta': (0.0, 0.1),
     'L0_ffn_ln_weight': (1.0, 0.2)}
    factors = {'L1_ffn_gate_w': 5.77,
     'L1_ffn_w_gate': 5.11,
     'L1_ffn_w_up': 5.018,
     'L1_ffn_w_down': 5.007,
     'L1_ffn_sh_gate': 5.02,
     'L1_ffn_sh_up': 4.956,
     'L1_ffn_sh_down': 4.942,
     'L1_ffn_se_gate_w': 8.0}
    for name, (base, spread) in spreads.items():
        noise = np.random.default_rng([zlib.crc32(name.encode()), seed]).standard_normal(out[name].shape)
        drawn = base * np.exp(spread * noise) if base else spread * noise
        out[name] = jnp.asarray(drawn.astype(out[name].dtype))
    for name, factor in factors.items():
        out[name] = (out[name] * factor).astype(out[name].dtype)
    return out
```

```python
from contextlib import ExitStack

import numpy as np

import concourse.bass as bass
from concourse import mybir

ALU = mybir.AluOpType
ACT = mybir.ActivationFunctionType
AX = mybir.AxisListType
F32 = mybir.dt.float32
BF16 = mybir.dt.bfloat16
F16 = mybir.dt.float16
U8 = mybir.dt.uint8
U32 = mybir.dt.uint32

P = 128
MAGIC = 1.5 * 2.0 ** 23
LN_EPS = 1e-5
RMS_EPS = 1e-6
QUANT_EPS = 1e-5
QMAX = 127.0
WSCALE = 64.0
MASKED = -1e30


def pipelined(eng, body, tiles):
    body(0, 0, True, False, False)
    body(1, 1, True, True, False)
    with eng.Fori(0, (tiles - 2) // 2) as i:
        for j in range(2):
            body(i * 2 + 2 + j, j, True, True, True)
    body(tiles, tiles % 2, False, True, True)
    body(tiles + 1, (tiles + 1) % 2, False, False, True)


def by_pairs(eng, body, tiles):
    body(0, 0)
    body(1, 1)
    with eng.Fori(0, (tiles - 2) // 2) as i:
        for j in range(2):
            body(i * 2 + 2 + j, j)


def model_kernel(nc, x, ctx_in, ctxT_in, mask, decay, w_inT, b_in, w_outT, b_out, gamma, beta,
                 f_gateT, f_upT, f_downT, ln_weight, routerT, e_gateT, e_upT, e_downT,
                 s_gateT, s_upT, s_downT, se_gateT, out):
    B, S, D = x.shape
    T = B * S // P
    DC = D // P
    I = f_gateT.shape[1]
    IC = I // P
    NE, _, H = e_gateT.shape
    HC = H // P
    NSH = s_gateT.shape[1] // H
    NU = NE + NSH
    CH = 512
    NCH = I // CH
    ATT_SCALE = float(D) ** -0.5
    assert S == P and D == CH and T % 2 == 0

    es = ExitStack()
    with es:
        def sb(name, shape, dt):
            return es.enter_context(nc.sbuf_tensor(name, shape, dt))

        def sem(name):
            return es.enter_context(nc.semaphore(name))

        x_sb = sb("x_sb", [P, T, D], F32)
        reg_a = sb("reg_a", [P, 8192], F32)
        reg_b = sb("reg_b", [P, 8192], F32)
        reg_c = sb("reg_c", [P, 8192], F32)
        wq = sb("wq", [P, 3 * DC * I], BF16)
        reg_x = sb("reg_x", [P, DC * T * P], BF16)
        gamma_b = sb("gamma_b", [P, D], F32)
        beta_b = sb("beta_b", [P, D], F32)
        xq = sb("xq", [P, 2, D], BF16)
        ident_h = sb("ident_h", [P, P], BF16)
        ident = sb("ident", [P, P], F32)
        small = sb("small", [P, 640], F32)

        cols = [0]

        def tiny(n):
            cols[0] += n
            assert cols[0] <= 640
            return small[:, cols[0] - n:cols[0]]

        ctx_sb = reg_a[:].rearrange("p (t d) -> p t d", t=T)
        y_buf = wq[:, DC * I:].bitcast(F32).rearrange("p (t d) -> p t d", t=T)
        w_in_sb = reg_x[:, 0:2 * DC * D].bitcast(F32).rearrange("p (c e) -> p c e", c=DC)
        w_out_sb = reg_x[:, 2 * DC * D:4 * DC * D].bitcast(F32).rearrange("p (c e) -> p c e", c=DC)
        rows = wq[0:1, 0:4096].bitcast(F32)
        b_in_row, b_out_row = rows[:, 0:D], rows[:, D:2 * D]
        decay_row = rows[:, 2 * D:2 * D + 1]
        keep_row = rows[:, 2 * D + 1:2 * D + 2]
        geo_row = rows[:, 2 * D + 128:2 * D + 256]
        ones_row = rows[:, 2 * D + 256:2 * D + 384]
        wsum_row = rows[:, 2 * D + 384:2 * D + 385]
        wsum16_row = rows[:, 2 * D + 400:2 * D + 400 + T]
        summary = w_in_sb[0:T, 0, :]
        ones = tiny(P)
        cbarT = tiny(DC * T)
        y1T = tiny(DC * T)
        wcol = tiny(1)
        xqT = reg_x[:].rearrange("p (c n) -> p c n", c=DC)
        raw_gate, raw_up, raw_down = reg_b, reg_c, reg_a
        wq_gate = wq[:, 0:DC * I].rearrange("p (c i) -> p c i", c=DC)
        wq_up = wq[:, DC * I:2 * DC * I].rearrange("p (c i) -> p c i", c=DC)
        wq_down = wq[:, 2 * DC * I:].rearrange("p (c o) -> p c o", c=IC)
        h_buf = reg_c[:, 0:2 * I].rearrange("p (s i) -> p s i", s=2)
        hl_buf = reg_c[:, 2 * I:4 * I].rearrange("p (s i) -> p s i", s=2)
        sg_buf = reg_b[:, 0:2 * CH].rearrange("p (s i) -> p s i", s=2)
        hq = reg_b[:, 1024:2048].bitcast(BF16)
        hqT = reg_b[:, 2048:3072].bitcast(BF16).rearrange("p (c n) -> p c n", c=IC)
        lnw_b = reg_b[:, 4096:4096 + I]
        junk = reg_b[:, 3072:3072 + I // 2].bitcast(BF16)
        abs_part = tiny(3 * DC)
        wabs = tiny(3)
        wmean = tiny(3)
        wscale = tiny(3)
        stats = tiny(6 * T).rearrange("p (t s) -> p t s", s=6)
        mean2 = tiny(T)
        mean = tiny(T)
        vpe = tiny(T)
        tmp16 = tiny(T)
        rstd = tiny(T)
        neg_half = tiny(T)
        amax = tiny(T)
        s_x = tiny(T)
        dq_gate = tiny(T)
        dq_up = tiny(T)
        sumsq = tiny(2)
        ms = tiny(2)
        rinv = tiny(2)
        hmax = tiny(2)
        rlim = tiny(2)
        rrec = tiny(2)
        s_h = tiny(2)
        dq_h = tiny(2)
        ctxT_sb = reg_b[:].rearrange("p (c n) -> p c n", c=DC)
        mask_sb = reg_x[:, 0:T * P // 2].bitcast(U8)
        negb = reg_x[:, 1024:1024 + 2 * T * P].bitcast(F32).rearrange("p (t m) -> p t m", t=T)
        wq32 = wq[:].bitcast(F32)
        xh = wq32[:, 0:1024].rearrange("p (s d) -> p s d", s=2)
        xhT = wq32[:, 1024:2048].rearrange("p (s d) -> p s d", s=2)
        smx = wq32[:, 2048:2304].rearrange("p (s d) -> p s d", s=2)
        prob = wq32[:, 2304:2560].rearrange("p (s d) -> p s d", s=2)
        probT = wq32[:, 2560:2816].rearrange("p (s d) -> p s d", s=2)
        valid = tiny(T)
        st1 = tiny(12).rearrange("p (s k) -> p s k", s=2)
        mv = tiny(4).rearrange("p (s k) -> p s k", s=2)
        ve1 = tiny(2)
        rs1 = tiny(2)
        nmax = tiny(2)
        rsum = tiny(2)
        rv = tiny(2)
        rv2 = tiny(2)
        xnT_hi = reg_c[:, 0:4096].bitcast(F16).rearrange("p (c n) -> p c n", c=DC)
        xnT_lo = reg_c[:, 4096:8192].bitcast(F16).rearrange("p (c n) -> p c n", c=DC)
        RAW = DC * 2 * H + HC * D
        raw_w = wq32[:, 4096:4096 + 2 * RAW].rearrange("p (s w) -> p s w", s=2)
        w_hi = reg_a[:, 0:RAW].bitcast(F16)
        w_lo = reg_a[:, RAW:2 * RAW].bitcast(F16)
        rt_raw = wq32[:, 10240:10240 + DC * (NE + 1)].rearrange("p (c e) -> p c e", c=DC)
        rt_hi = wq32[:, 10290:10308].bitcast(F16).rearrange("p (c e) -> p c e", c=DC)
        rt_lo = wq32[:, 10310:10328].bitcast(F16).rearrange("p (c e) -> p c e", c=DC)
        TE = T * NE

        def routing(n, w):
            v = wq32[:, 10400 + TE * n:10400 + TE * n + T * w]
            return v.rearrange("p (t e) -> p t e", t=T) if w > 1 else v

        iota8, logit, first, second, cand, scr = [routing(n, NE) for n in range(6)]
        comb = routing(6, NU)
        m1, m2, least1, least2, w1, w2 = [wq32[:, 11424 + T * n:11424 + T * (n + 1)] for n in range(6)]
        e_pair = wq32[:, 11540:11540 + 2 * T].rearrange("p (k t) -> p k t", k=2)
        sgd = reg_b[:, 0:2 * H].rearrange("p (s i) -> p s i", s=2)
        hd = reg_b[:, 2 * H:4 * H].rearrange("p (s i) -> p s i", s=2)
        hT_hi = reg_b[:, 1024:1024 + H].bitcast(F16).rearrange("p (s i) -> p s i", s=2)
        hT_lo = reg_b[:, 1536:1536 + H].bitcast(F16).rearrange("p (s i) -> p s i", s=2)

        psum = es.enter_context(nc.psum_tensor("psum", [P, 8 * CH], F32))
        bank = [psum[:, i * CH:(i + 1) * CH] for i in range(8)]

        consts_ready = sem("consts_ready")
        x_landed = sem("x_landed")
        rows_landed = sem("rows_landed")
        ctx_landed = sem("ctx_landed")
        win_landed = sem("win_landed")
        vec_landed = sem("vec_landed")
        raw_landed = [sem(f"raw{i}_landed") for i in range(3)]
        keep_done = sem("keep_done")
        geo_done = sem("geo_done")
        wcol_mm = sem("wcol_mm")
        wcol_done = sem("wcol_done")
        cbar_mm = sem("cbar_mm")
        cbar_done = sem("cbar_done")
        y1_mm = sem("y1_mm")
        y1_done = sem("y1_done")
        sum_mm = sem("sum_mm")
        sum_done = sem("sum_done")
        bcast_mm = sem("bcast_mm")
        bcast_used = sem("bcast_used")
        dve_a = sem("dve_a")
        var_ready = sem("var_ready")
        rstd_ready = sem("rstd_ready")
        y_done = sem("y_done")
        xb_done = sem("xb_done")
        abs_done = sem("abs_done")
        abs_mm = sem("abs_mm")
        wscale_done = sem("wscale_done")
        shifted = sem("shifted")
        wq_done = sem("wq_done")
        xq_done = sem("xq_done")
        xq_tr = sem("xq_tr")
        xqT_done = sem("xqT_done")
        gate_mm = sem("gate_mm")
        up_mm = sem("up_mm")
        silu_done = sem("silu_done")
        h_done = sem("h_done")
        hl_done = sem("hl_done")
        sq_done = sem("sq_done")
        ms_done = sem("ms_done")
        rinv_done = sem("rinv_done")
        dve_b = sem("dve_b")
        s_h_done = sem("s_h_done")
        hs_done = sem("hs_done")
        hq_done = sem("hq_done")
        hq_tr = sem("hq_tr")
        hqT_a = sem("hqT_a")
        hqT_b = sem("hqT_b")
        down_mm = sem("down_mm")
        x2_done = sem("x2_done")
        mask_landed = sem("mask_landed")
        ctx2_landed = sem("ctx2_landed")
        dve_c = sem("dve_c")
        ve_done = sem("ve_done")
        rs_done = sem("rs_done")
        xh_done = sem("xh_done")
        xh_tr = sem("xh_tr")
        xhT_done = sem("xhT_done")
        score_mm = sem("score_mm")
        nmax_done = sem("nmax_done")
        prob_done = sem("prob_done")
        prob_tr = sem("prob_tr")
        probT_done = sem("probT_done")
        read_mm = sem("read_mm")
        x3_done = sem("x3_done")
        rt_landed = sem("rt_landed")
        rt_done = sem("rt_done")
        iota_done = sem("iota_done")
        dve_d = sem("dve_d")
        vd_done = sem("vd_done")
        rd_done = sem("rd_done")
        xn_done = sem("xn_done")
        xn_tr = sem("xn_tr")
        xn_hi_done = sem("xn_hi_done")
        xn_lo_done = sem("xn_lo_done")
        logit_mm = sem("logit_mm")
        edif_done = sem("edif_done")
        eexp_done = sem("eexp_done")
        comb_done = sem("comb_done")
        w_landed = [sem(f"w{i}_landed") for i in range(2)]
        w_hi_done = sem("w_hi_done")
        w_lo_done = sem("w_lo_done")
        gu_mm = sem("gu_mm")
        silu_d = sem("silu_d")
        hd_done = sem("hd_done")
        hd_tr = sem("hd_tr")
        hT_hi_done = sem("hT_hi_done")
        hT_lo_done = sem("hT_lo_done")
        dn_mm = sem("dn_mm")
        acc_done = sem("acc_done")
        stored = sem("stored")
        lnw_landed = sem("lnw_landed")
        smx_done = sem("smx_done")
        rv_done = sem("rv_done")
        logit_done = sem("logit_done")

        x_v = x.rearrange("b p d -> p b d")
        out_v = out.rearrange("b p d -> p b d")
        ctx_v = ctx_in.rearrange("b p d -> p b d")
        ctxT_v = ctxT_in.rearrange("b (c p) m -> p c b m", p=P)
        raw_v = [f_gateT.rearrange("(c p) i -> p c i", p=P), f_upT.rearrange("(c p) i -> p c i", p=P),
                 f_downT.rearrange("(c p) o -> p c o", p=P)]
        raw_sb = [raw_gate[:].rearrange("p (c i) -> p c i", c=DC), raw_up[:].rearrange("p (c i) -> p c i", c=DC),
                  raw_down[:].rearrange("p (c o) -> p c o", c=IC)]

        block = es.enter_context(nc.Block())

        flat_raw = [reg_b, reg_c, reg_a]

        def alone(eng):
            eng.nop(nofuse=True)

        def raw_piece(m, c):
            return flat_raw[m][:, c * 4 * CH:(c + 1) * 4 * CH]

        @block.sync
        def _(sp):
            for v, r in ((b_in, b_in_row), (b_out, b_out_row)):
                sp.dma_start(r, v.rearrange("(a n) -> a n", a=1)).then_inc(rows_landed, 16)
            sp.dma_start(decay_row, decay).then_inc(rows_landed, 16)
            sp.dma_start(ctx_sb, ctx_v).then_inc(ctx_landed, 16)
            for h in range(2):
                sp.dma_start(x_sb[:, h * T // 2:(h + 1) * T // 2, :],
                             x_v[:, h * T // 2:(h + 1) * T // 2, :]).then_inc(x_landed, 16)
            sp.dma_start(w_in_sb, w_inT.rearrange("(c p) e -> p c e", p=P)).then_inc(win_landed, 16)
            sp.dma_start(w_out_sb, w_outT.rearrange("(c p) e -> p c e", p=P)).then_inc(win_landed, 16)
            for v, r in ((gamma, gamma_b), (beta, beta_b)):
                sp.dma_start(r[:], v.partition_broadcast(P)).then_inc(vec_landed, 16)
            sp.dma_start(raw_sb[0], raw_v[0]).then_inc(raw_landed[0], 16)
            sp.dma_start(raw_sb[1], raw_v[1]).then_inc(raw_landed[1], 16)
            sp.wait_ge(cbar_mm, 1)
            sp.dma_start(raw_sb[2], raw_v[2]).then_inc(raw_landed[2], 16)
            sp.wait_ge(wq_done, 3)
            sp.dma_start(lnw_b, ln_weight.partition_broadcast(P)).then_inc(lnw_landed, 16)
            sp.dma_start(ctx_sb, ctx_v).then_inc(ctx2_landed, 16)
            sp.wait_ge(x2_done, T)
            for c in range(DC):
                sp.dma_start(ctxT_sb[:, c, :].rearrange("p (b m) -> p b m", b=T), ctxT_v[:, c]).then_inc(ctx2_landed, 16)
            sp.dma_start(mask_sb, mask.partition_broadcast(P)).then_inc(mask_landed, 16)
            with nc.allow_non_contiguous_dma(reason="router columns are narrow"):
                sp.dma_start(rt_raw[:, :, 0:NE], routerT.rearrange("(c p) e -> p c e", p=P)).then_inc(rt_landed, 16)
                sp.dma_start(rt_raw[:, :, NE:NE + 1], se_gateT.rearrange("(c p) e -> p c e", p=P)).then_inc(rt_landed, 16)
            for u in range(NU):
                s = u % 2
                if u >= 2:
                    sp.wait_ge(w_lo_done, u - 1)
                gu = raw_w[:, s, 0:DC * 2 * H].rearrange("p (c g i) -> p c g i", c=DC, g=2)
                dn = raw_w[:, s, DC * 2 * H:].rearrange("p (c o) -> p c o", c=HC)
                if u < NE:
                    src = (e_gateT[u], e_upT[u], e_downT[u])
                else:
                    v = u - NE
                    src = (s_gateT[:, v * H:(v + 1) * H], s_upT[:, v * H:(v + 1) * H], s_downT[v * H:(v + 1) * H, :])
                sp.dma_start(gu[:, :, 0, :], src[0].rearrange("(c p) i -> p c i", p=P)).then_inc(w_landed[s], 16)
                sp.dma_start(gu[:, :, 1, :], src[1].rearrange("(c p) i -> p c i", p=P)).then_inc(w_landed[s], 16)
                sp.dma_start(dn, src[2].rearrange("(c p) o -> p c o", p=P)).then_inc(w_landed[s], 16)
            for h in range(2):
                sp.wait_ge(acc_done, (NU - 1) * T + (h + 1) * T // 2)
                sp.dma_start(out_v[:, h * T // 2:(h + 1) * T // 2, :],
                             x_sb[:, h * T // 2:(h + 1) * T // 2, :]).then_inc(stored, 16)
            sp.wait_ge(stored, 32)

        @block.gpsimd
        def _(pool):
            pool.memset(ident[:], 0.0).then_inc(consts_ready, 1)
            pool.memset(ident_h[:], 0.0).then_inc(consts_ready, 1)
            pool.memset(ones, 1.0).then_inc(consts_ready, 1)
            pool.memset(neg_half, -0.5).then_inc(consts_ready, 1)
            pool.memset(ones_row, 1.0).then_inc(consts_ready, 1)
            pool.wait_ge(consts_ready, 2)
            for m in (ident, ident_h):
                pool.affine_select(out=m[:], in_=m[:], compare_op=ALU.not_equal, fill=1.0, base=0,
                                   pattern=[[-1, P]], channel_multiplier=1).then_inc(consts_ready, 1)
            pool.wait_ge(consts_ready, 7)
            pool.wait_ge(var_ready, 1)
            pool.tensor_tensor(rstd, vpe, neg_half, ALU.pow).then_inc(rstd_ready, 1)
            pool.wait_ge(vec_landed, 32)
            with pool.Fori(0, T) as t:
                pool.wait_ge(y_done, t + 1)
                pool.tensor_tensor(x_sb[:, bass.ds(t, 1), :].rearrange("p a d -> p (a d)"),
                                   x_sb[:, bass.ds(t, 1), :].rearrange("p a d -> p (a d)"),
                                   beta_b[:], ALU.add).then_inc(xb_done, 1)
            for n in (2, 3):
                pool.wait_ge(var_ready, n)
                pool.tensor_tensor(rstd, vpe, neg_half, ALU.pow).then_inc(rstd_ready, 1)
            pool.wait_ge(lnw_landed, 16)
            with pool.Fori(0, T // 2) as i:
                for j in range(2):
                    t = i * 2 + j
                    pool.wait_ge(hq_done, t + 1)
                    for c in range(NCH):
                        pool.wait_ge(h_done, t * NCH + c + 3)
                        pool.tensor_tensor(hl_buf[:, j, c * CH:(c + 1) * CH], h_buf[:, j, c * CH:(c + 1) * CH],
                                           lnw_b[:, c * CH:(c + 1) * CH], ALU.mult).then_inc(hl_done, 1)
                    pool.wait_ge(sq_done, t + 1)
                    alone(pool)
                    pool.tensor_scalar(ms[:, j:j + 1], sumsq[:, j:j + 1], 1.0 / I, RMS_EPS, ALU.mult, ALU.add)\
                        .then_inc(ms_done, 1)
                    pool.wait_ge(ms_done, t + 1)
                    pool.tensor_tensor(rinv[:, j:j + 1], ms[:, j:j + 1], neg_half[:, 0:1], ALU.pow)\
                        .then_inc(rinv_done, 1)
            with pool.Fori(0, T // 2) as i:
                for j in range(2):
                    pool.wait_ge(ve_done, i * 2 + j + 1)
                    pool.tensor_tensor(rs1[:, j:j + 1], ve1[:, j:j + 1], neg_half[:, 0:1], ALU.pow)\
                        .then_inc(rs_done, 1)
            pool.wait_ge(x2_done, T)
            pool.iota(iota8, pattern=[[0, T], [1, NE]], base=0, channel_multiplier=0,
                      allow_small_or_imprecise_dtypes=True).then_inc(iota_done, 1)
            with pool.Fori(0, T // 2) as i:
                for j in range(2):
                    pool.wait_ge(vd_done, i * 2 + j + 1)
                    pool.tensor_tensor(rs1[:, j:j + 1], ve1[:, j:j + 1], neg_half[:, 0:1], ALU.pow)\
                        .then_inc(rd_done, 1)

        @block.scalar
        def _(act):
            act.wait_ge(rows_landed, 48)
            act.activation(keep_row, decay_row, ACT.Tanh, scale=0.5).then_inc(keep_done, 1)
            for m in range(3):
                act.wait_ge(raw_landed[m], 16)
                for c in range(4):
                    if m or c:
                        act.wait_ge(abs_done, 4 * m + c)
                    act.activation(psum[:, 4 * CH:8 * CH], raw_piece(m, c), ACT.Abs,
                                   accum_out=abs_part[:, 4 * m + c:4 * m + c + 1]).then_inc(abs_done, 1)

            def shift(m):
                act.wait_ge(wscale_done, m + 1)
                for c in range(4):
                    act.activation(raw_piece(m, c), raw_piece(m, c), ACT.Copy, scale=wscale[:, m:m + 1],
                                   bias=MAGIC).then_inc(shifted, 1)

            shift(0)
            shift(1)

            def evac_xq(t, j):
                act.wait_ge(xq_tr, t + 1)
                alone(act)
                act.activation(xqT[:, :, bass.ds(t * P, P)], bank[2 + j].bitcast(BF16)[:, 0:D]
                               .rearrange("p (c n) -> p c n", c=DC), ACT.Copy).then_inc(xqT_done, 1)

            by_pairs(act, evac_xq, T)
            shift(2)

            def ffn(t, j, now, back1, back2):
                def silu(c):
                    if now:
                        act.wait_ge(gate_mm, t * NCH + c + 1)
                        alone(act)
                        act.activation(sg_buf[:, c % 2, :], bank[c % 2], ACT.Silu,
                                       scale=dq_gate[:, bass.ds(t, 1)]).then_inc(silu_done, 1)

                silu(0)
                if back2:
                    act.wait_ge(hq_tr, (t - 2) * 2 + 1)
                    act.activation(hqT[:, 0:IC // 2, :], bank[4].bitcast(BF16).rearrange("p (c n) -> p c n", n=P),
                                   ACT.Copy).then_inc(hqT_a, 1)
                silu(1)
                silu(2)
                if back1:
                    act.wait_ge(s_h_done, t)
                    act.activation(hl_buf[:, 1 - j, :], hl_buf[:, 1 - j, :], ACT.Copy, bias=MAGIC,
                                   scale=s_h[:, 1 - j:2 - j]).then_inc(hs_done, 1)
                silu(3)
                if now:
                    act.wait_ge(h_done, t * NCH + NCH + 2)
                    act.activation(junk, h_buf[:, j, :], ACT.Square,
                                   accum_out=sumsq[:, j:j + 1]).then_inc(sq_done, 1)

            pipelined(act, ffn, T)

            def attend(t, j, now, back1, back2):
                if now:
                    act.wait_ge(xh_tr, t + 1)
                    act.activation(xhT[:, j, :], bank[j], ACT.Copy).then_inc(xhT_done, 1)
                if back1:
                    act.wait_ge(nmax_done, t)
                    act.activation(prob[:, 1 - j, :], smx[:, 1 - j, :], ACT.Exp, bias=nmax[:, 1 - j:2 - j],
                                   accum_out=rsum[:, 1 - j:2 - j]).then_inc(prob_done, 1)
                    act.wait_ge(prob_tr, t)
                    act.activation(probT[:, 1 - j, :], bank[5 - j][:, 0:P], ACT.Copy).then_inc(probT_done, 1)

            pipelined(act, attend, T)

            act.wait_ge(rt_landed, 32)
            act.activation(rt_hi, rt_raw, ACT.Copy, scale=WSCALE).then_inc(rt_done, 1)

            def high(t, j):
                act.wait_ge(xn_tr, t + 1)
                alone(act)
                act.activation(xnT_hi[:, :, bass.ds(t * P, P)], bank[j].rearrange("p (c n) -> p c n", c=DC),
                               ACT.Copy).then_inc(xn_hi_done, 1)

            by_pairs(act, high, T)
            act.wait_ge(edif_done, 1)
            act.activation(e_pair, e_pair, ACT.Exp).then_inc(eexp_done, 1)

            def split_high(u):
                s = u % 2
                act.wait_ge(w_landed[s], 48 * (u // 2 + 1))
                if u >= 2:
                    act.wait_ge(dn_mm, (u - 1) * T)
                act.activation(w_hi[:, s * RAW:(s + 1) * RAW], raw_w[:, s, :], ACT.Copy, scale=WSCALE)\
                   .then_inc(w_hi_done, 1)

            split_high(0)
            for u in range(NU):
                if u + 1 < NU:
                    split_high(u + 1)

                def expert(t, j, now, back1, back2, n0=u * T):
                    if now:
                        act.wait_ge(gu_mm, t + (n0 + 1))
                        act.activation(sgd[:, j, :], bank[j][:, 0:H], ACT.Silu, scale=1.0 / WSCALE)\
                           .then_inc(silu_d, 1)
                    if back1:
                        act.wait_ge(hd_tr, t + n0)
                        act.activation(hT_hi[:, 1 - j, :], bank[3 - j][:, 0:H], ACT.Copy).then_inc(hT_hi_done, 1)

                pipelined(act, expert, T)

        @block.tensor
        def _(pe):
            pe.wait_ge(consts_ready, 7)
            pe.wait_ge(geo_done, 1)
            pe.matmul(bank[0][:, 0:1], geo_row, ones_row[:, 0:1], start=True, stop=True).then_inc(wcol_mm, 1)
            pe.wait_ge(wcol_done, 1)
            pe.wait_ge(ctx_landed, 16)
            for t in range(T):
                for c in range(DC):
                    last = pe.matmul(bank[1][:, c * T + t:c * T + t + 1], ctx_sb[:, t, c * P:(c + 1) * P], wcol,
                                     start=True, stop=True)
            last.then_inc(cbar_mm, 1)
            pe.wait_ge(cbar_done, 1)
            pe.wait_ge(win_landed, 32)
            for e in range(DC):
                for c in range(DC):
                    pe.matmul(bank[0][:, 64 + e * T:64 + (e + 1) * T], w_in_sb[:, c, e * P:(e + 1) * P],
                              cbarT[:, c * T:(c + 1) * T], start=(c == 0), stop=False)
                last = pe.matmul(bank[0][:, 64 + e * T:64 + (e + 1) * T], b_in_row[:, e * P:(e + 1) * P],
                                 wsum16_row, start=False, stop=True)
            last.then_inc(y1_mm, 1)
            pe.wait_ge(y1_done, 1)
            for c in range(DC):
                pe.matmul(bank[1][0:T, :], y1T[:, c * T:(c + 1) * T], w_out_sb[:, c, :], start=(c == 0), stop=False)
            pe.matmul(bank[1][0:T, :], ones_row[:, 0:T], b_out_row, start=False, stop=True).then_inc(sum_mm, 1)
            pe.wait_ge(sum_done, 1)
            for t in range(T):
                if t >= 2:
                    pe.wait_ge(bcast_used, t - 1)
                pe.matmul(bank[2 + t % 2], ident[0:T, t:t + 1].to_broadcast([T, P]), summary,
                          start=True, stop=True).then_inc(bcast_mm, 1)
            for m in range(2):
                pe.wait_ge(abs_done, 4 * m + 4)
                pe.matmul(bank[0][:, 256 + 4 * m:260 + 4 * m], ones, abs_part[:, 4 * m:4 * m + 4],
                          start=True, stop=True).then_inc(abs_mm, 1)

            def turn_xq(t, j):
                pe.wait_ge(xq_done, t + 1)
                if not isinstance(t, int):
                    pe.wait_ge(xqT_done, t - 1)
                for c in range(DC):
                    last = pe.transpose(bank[2 + j].bitcast(BF16)[:, c * P:(c + 1) * P],
                                        xq[:, j, c * P:(c + 1) * P], ident_h[:])
                last.then_inc(xq_tr, 1)

            by_pairs(pe, turn_xq, T)
            pe.wait_ge(abs_done, 12)
            pe.matmul(bank[7][:, 264:268], ones, abs_part[:, 8:12], start=True, stop=True).then_inc(abs_mm, 1)

            def ffn(t, j, now, back1, back2):
                def gate_up(c):
                    if not now:
                        return
                    pe.wait_ge(h_done, t * NCH + c + 1)
                    for m, w, done in ((0, wq_gate, gate_mm), (2, wq_up, up_mm)):
                        for k in range(DC):
                            last = pe.matmul(bank[m + c % 2], xqT[:, k, bass.ds(t * P, P)],
                                             w[:, k, c * CH:(c + 1) * CH], start=(k == 0), stop=(k == DC - 1))
                        last.then_inc(done, 1)

                if now and isinstance(t, int) and t == 0:
                    pe.wait_ge(xqT_done, T)
                    pe.wait_ge(wq_done, 2)
                gate_up(0)
                if back2:
                    pe.wait_ge(hq_done, t + 1)
                    for half, sem_h in ((0, hqT_a), (1, hqT_b)):
                        for c in range(IC // 2):
                            k = half * IC // 2 + c
                            last = pe.transpose(bank[4 + half].bitcast(BF16)[:, c * P:(c + 1) * P],
                                                hq[:, k * P:(k + 1) * P], ident_h[:])
                        last.then_inc(hq_tr, 1)
                gate_up(1)
                if back2:
                    if isinstance(t, int) and t == 2 or not isinstance(t, int):
                        pe.wait_ge(wq_done, 3)
                    pe.wait_ge(hqT_a, t - 1)
                    pe.wait_ge(hqT_b, t - 1)
                    for k in range(IC):
                        last = pe.matmul(bank[6 + j], hqT[:, k, :], wq_down[:, k, :],
                                         start=(k == 0), stop=(k == IC - 1))
                    last.then_inc(down_mm, 1)
                gate_up(2)
                gate_up(3)

            pipelined(pe, ffn, T)

            def attend(t, j, now, back1, back2):
                if now:
                    if isinstance(t, int) and t == 0:
                        pe.wait_ge(ctx2_landed, 16 * (DC + 1))
                    pe.wait_ge(xh_done, t + 1)
                    for c in range(DC):
                        last = pe.transpose(bank[j][:, c * P:(c + 1) * P], xh[:, j, c * P:(c + 1) * P], ident[:])
                    last.then_inc(xh_tr, 1)
                    pe.wait_ge(xhT_done, t + 1)
                    for c in range(DC):
                        last = pe.matmul(bank[2 + j][:, 0:P], xhT[:, j, c * P:(c + 1) * P],
                                         ctxT_sb[:, c, bass.ds(t * P, P)], start=(c == 0), stop=(c == DC - 1))
                    last.then_inc(score_mm, 1)
                if back1:
                    pe.wait_ge(prob_done, t)
                    pe.transpose(bank[5 - j][:, 0:P], prob[:, 1 - j, :], ident[:]).then_inc(prob_tr, 1)
                    pe.wait_ge(probT_done, t)
                    pe.matmul(bank[7 - j], probT[:, 1 - j, :], ctx_sb[:, bass.ds(t - 1, 1), :]
                              .rearrange("p a d -> p (a d)"), start=True, stop=True).then_inc(read_mm, 1)

            pipelined(pe, attend, T)

            pe.wait_ge(rt_done, 2)

            def route(t, j, now, back1, back2):
                if now:
                    pe.wait_ge(xn_done, t + 1)
                    for c in range(DC):
                        last = pe.transpose(bank[j][:, c * P:(c + 1) * P], xh[:, j, c * P:(c + 1) * P], ident[:])
                    last.then_inc(xn_tr, 1)
                if back1:
                    pe.wait_ge(xn_hi_done, t)
                    pe.wait_ge(xn_lo_done, t)
                    n = 0
                    for xx, ww in ((xnT_hi, rt_hi), (xnT_hi, rt_lo), (xnT_lo, rt_hi)):
                        for c in range(DC):
                            last = pe.matmul(bank[3 - j][:, 0:NE + 1], xx[:, c, bass.ds((t - 1) * P, P)],
                                             ww[:, c, :], start=(n == 0), stop=(n == 3 * DC - 1))
                            n += 1
                    last.then_inc(logit_mm, 1)

            pipelined(pe, route, T)

            for u in range(NU):
                s = u % 2
                gu_w = [w[:, s * RAW:s * RAW + DC * 2 * H].rearrange("p (c i) -> p c i", c=DC) for w in (w_hi, w_lo)]
                dn_w = [w[:, s * RAW + DC * 2 * H:(s + 1) * RAW].rearrange("p (c o) -> p c o", c=HC)
                        for w in (w_hi, w_lo)]
                pe.wait_ge(w_hi_done, u + 1)
                pe.wait_ge(w_lo_done, u + 1)

                def expert(t, j, now, back1, back2, n0=u * T, gu_w=gu_w, dn_w=dn_w):
                    if now:
                        if n0 or not isinstance(t, int) or t >= 2:
                            pe.wait_ge(hd_done, t + (n0 - 1))
                        n = 0
                        for xx, ww in ((xnT_hi, 0), (xnT_hi, 1), (xnT_lo, 0)):
                            for c in range(DC):
                                last = pe.matmul(bank[j], xx[:, c, bass.ds(t * P, P)], gu_w[ww][:, c, :],
                                                 start=(n == 0), stop=(n == 3 * DC - 1))
                                n += 1
                        last.then_inc(gu_mm, 1)
                    if back1:
                        pe.wait_ge(hd_done, t + n0)
                        for c in range(HC):
                            last = pe.transpose(bank[3 - j][:, c * P:(c + 1) * P],
                                                hd[:, 1 - j, c * P:(c + 1) * P], ident[:])
                        last.then_inc(hd_tr, 1)
                    if back2:
                        pe.wait_ge(hT_hi_done, t + (n0 - 1))
                        pe.wait_ge(hT_lo_done, t + (n0 - 1))
                        n = 0
                        for hh, ww in ((hT_hi, 0), (hT_hi, 1), (hT_lo, 0)):
                            for c in range(HC):
                                last = pe.matmul(bank[4 + j], hh[:, j, c * P:(c + 1) * P], dn_w[ww][:, c, :],
                                                 start=(n == 0), stop=(n == 3 * HC - 1))
                                n += 1
                        last.then_inc(dn_mm, 1)

                pipelined(pe, expert, T)

        @block.vector
        def _(dve):
            dve.sem_inc(h_done, 2)
            dve.sem_inc(hq_done, 2)

            def tile(buf, t):
                return buf[:, bass.ds(t, 1), :].rearrange("p a d -> p (a d)")

            dve.wait_ge(consts_ready, 5)
            dve.wait_ge(keep_done, 1)
            dve.tensor_scalar(keep_row, keep_row, 0.5, 0.5, ALU.mult, ALU.add).then_inc(dve_a, 1)
            dve.wait_ge(dve_a, 1)
            dve.tensor_tensor_scan(geo_row[:, ::-1], keep_row.to_broadcast([1, S]), ones_row, 0.0,
                                   ALU.mult, ALU.add).then_inc(geo_done, 1)
            dve.wait_ge(geo_done, 1)
            dve.reduce_sum(wsum_row, geo_row, AX.X).then_inc(dve_a, 1)
            dve.wait_ge(dve_a, 2)
            dve.tensor_scalar(wsum16_row, ones_row[:, 0:T], wsum_row, 1.0 / S, ALU.mult, ALU.mult).then_inc(dve_a, 1)
            dve.wait_ge(wcol_mm, 1)
            dve.tensor_scalar(wcol, bank[0][:, 0:1], 1.0 / S, None, ALU.mult).then_inc(wcol_done, 1)
            dve.wait_ge(cbar_mm, 1)
            dve.tensor_copy(cbarT, bank[1][:, 0:DC * T]).then_inc(cbar_done, 1)
            dve.wait_ge(x_landed, 32)

            def batch_norm(k, st):
                dve.tensor_tensor(mean2, st[:, :, 1], st[:, :, 4], ALU.add).then_inc(dve_a, 1)
                dve.tensor_tensor(tmp16, st[:, :, 1], st[:, :, 4], ALU.subtract).then_inc(dve_a, 1)
                dve.tensor_tensor(vpe, st[:, :, 2], st[:, :, 5], ALU.add).then_inc(dve_a, 1)
                dve.wait_ge(dve_a, k + 3)
                dve.scalar_tensor_tensor(tmp16, tmp16, 0.25, tmp16, ALU.mult, ALU.mult).then_inc(dve_a, 1)
                dve.tensor_scalar(vpe, vpe, 1.0 / D, LN_EPS, ALU.mult, ALU.add).then_inc(dve_a, 1)
                dve.tensor_scalar(mean, mean2, 0.5, None, ALU.mult).then_inc(dve_a, 1)
                dve.wait_ge(dve_a, k + 6)
                dve.tensor_tensor(vpe, vpe, tmp16, ALU.add).then_inc(var_ready, 1)

            def stats_of(buf, count):
                with dve.Fori(0, T) as t:
                    dve.bn_stats(stats[:, bass.ds(t, 1), :].rearrange("p a d -> p (a d)"), tile(buf, t))\
                       .then_inc(dve_a, 1)
                dve.wait_ge(dve_a, count + T)

            stats_of(x_sb, 3)
            batch_norm(3 + T, stats)
            dve.wait_ge(y1_mm, 1)
            dve.tensor_copy(y1T, bank[0][:, 64:64 + DC * T]).then_inc(y1_done, 1)
            dve.wait_ge(sum_mm, 1)
            dve.tensor_copy(summary, bank[1][0:T, :]).then_inc(sum_done, 1)
            dve.wait_ge(rstd_ready, 1)
            with dve.Fori(0, T) as t:
                dve.tensor_scalar(tile(y_buf, t), tile(x_sb, t), mean[:, bass.ds(t, 1)], rstd[:, bass.ds(t, 1)],
                                  ALU.subtract, ALU.mult).then_inc(y_done, 1)
            with dve.Fori(0, T // 2) as i:
                for j in range(2):
                    t = i * 2 + j
                    dve.wait_ge(y_done, t + 1)
                    dve.wait_ge(bcast_mm, t + 1)
                    dve.tensor_tensor(tile(y_buf, t), tile(y_buf, t), bank[2 + j], ALU.add).then_inc(bcast_used, 1)
            dve.wait_ge(bcast_used, T)
            n = 3 + T + 6
            stats_of(y_buf, n)
            batch_norm(n + T, stats)
            n += T + 6
            dve.wait_ge(vec_landed, 32)
            dve.wait_ge(rstd_ready, 2)
            with dve.Fori(0, T) as t:
                dve.scalar_tensor_tensor(tile(y_buf, t), tile(y_buf, t), mean[:, bass.ds(t, 1)], gamma_b[:],
                                         ALU.subtract, ALU.mult).then_inc(dve_a, 1)
            dve.wait_ge(dve_a, n + T)
            n += T
            with dve.Fori(0, T) as t:
                dve.wait_ge(xb_done, t + 1)
                dve.scalar_tensor_tensor(tile(x_sb, t), tile(y_buf, t), rstd[:, bass.ds(t, 1)], tile(x_sb, t),
                                         ALU.mult, ALU.add).then_inc(dve_a, 1)
            dve.wait_ge(dve_a, n + T)
            n += T
            stats_of(x_sb, n)
            batch_norm(n + T, stats)
            n += T + 6
            dve.wait_ge(rstd_ready, 3)
            with dve.Fori(0, T) as t:
                dve.tensor_scalar(tile(y_buf, t), tile(x_sb, t), mean[:, bass.ds(t, 1)], rstd[:, bass.ds(t, 1)],
                                  ALU.subtract, ALU.mult).then_inc(dve_a, 1)
            dve.wait_ge(dve_a, n + T)
            n += T
            with dve.Fori(0, T) as t:
                dve.tensor_reduce(amax[:, bass.ds(t, 1)], tile(y_buf, t), AX.X, ALU.max,
                                  apply_absolute_value=True).then_inc(dve_a, 1)
            dve.wait_ge(dve_a, n + T)
            n += T

            def weight_scale(m):
                dve.wait_ge(abs_mm, max(m + 1, 2))
                dve.reduce_sum(wabs[:, m:m + 1], bank[7 if m == 2 else 0][:, 256 + 4 * m:260 + 4 * m], AX.X).then_inc(dve_a, 1)

            weight_scale(0)
            weight_scale(1)
            dve.tensor_scalar(amax, amax, QUANT_EPS, None, ALU.max).then_inc(dve_a, 1)
            dve.wait_ge(dve_a, n + 3)
            dve.tensor_scalar(wmean[:, 0:2], wabs[:, 0:2], 1.0 / (I * D), QUANT_EPS, ALU.mult, ALU.max).then_inc(dve_a, 1)
            dve.reciprocal(s_x, amax).then_inc(dve_a, 1)
            dve.wait_ge(dve_a, n + 5)
            dve.reciprocal(wscale[:, 0:2], wmean[:, 0:2]).then_inc(wscale_done, 2)
            dve.tensor_scalar(s_x, s_x, QMAX, None, ALU.mult).then_inc(dve_a, 1)
            dve.tensor_scalar(dq_gate, amax, wmean[:, 0:1], 1.0 / QMAX, ALU.mult, ALU.mult).then_inc(dve_a, 1)
            dve.tensor_scalar(dq_up, amax, wmean[:, 1:2], 1.0 / QMAX, ALU.mult, ALU.mult).then_inc(dve_a, 1)
            dve.wait_ge(dve_a, n + 8)
            n += 8
            with dve.Fori(0, T) as t:
                dve.tensor_scalar(tile(y_buf, t), tile(y_buf, t), s_x[:, bass.ds(t, 1)], MAGIC, ALU.mult, ALU.add)\
                   .then_inc(dve_a, 1)
            dve.wait_ge(dve_a, n + T)
            n += T

            def store_xq(t, j):
                if not isinstance(t, int):
                    dve.wait_ge(xq_tr, t - 1)
                dve.tensor_scalar(xq[:, j, :], tile(y_buf, t), MAGIC, None, ALU.subtract).then_inc(xq_done, 1)

            by_pairs(dve, store_xq, T)
            dve.wait_ge(xq_done, T)

            def ternary(m, k):
                dve.wait_ge(shifted, 4 * m + 4)
                for c in range(4):
                    v = raw_piece(m, c)
                    dve.tensor_scalar(v, v, MAGIC + 1.0, MAGIC - 1.0, ALU.min, ALU.max).then_inc(dve_a, 1)
                dve.wait_ge(dve_a, k + 4)
                for c in range(4):
                    last = dve.tensor_scalar(wq[:, (4 * m + c) * 4 * CH:(4 * m + c + 1) * 4 * CH], raw_piece(m, c),
                                             MAGIC, None, ALU.subtract)
                last.then_inc(wq_done, 1)

            ternary(0, n)
            ternary(1, n + 4)
            n += 8
            weight_scale(2)
            dve.wait_ge(dve_a, n + 1)
            dve.tensor_scalar(wmean[:, 2:3], wabs[:, 2:3], 1.0 / (I * D), QUANT_EPS, ALU.mult, ALU.max).then_inc(dve_a, 1)
            dve.wait_ge(dve_a, n + 2)
            dve.reciprocal(wscale[:, 2:3], wmean[:, 2:3]).then_inc(wscale_done, 1)
            dve.tensor_scalar(wmean[:, 0:1], wmean[:, 2:3], 1.0 / QMAX, None, ALU.mult).then_inc(dve_a, 1)
            ternary(2, n + 3)
            dve.wait_ge(wq_done, 3)

            def ffn(t, j, now, back1, back2):
                def hidden(c):
                    if now:
                        dve.wait_ge(up_mm, t * NCH + c + 1)
                        dve.wait_ge(silu_done, t * NCH + c + 1)
                        dve.scalar_tensor_tensor(h_buf[:, j, c * CH:(c + 1) * CH], bank[2 + c % 2],
                                                 dq_up[:, bass.ds(t, 1)], sg_buf[:, c % 2, :],
                                                 ALU.mult, ALU.mult).then_inc(h_done, 1)

                b = 1 - j
                hidden(0)
                if back2:
                    dve.wait_ge(hq_tr, (t - 2) * 2 + 2)
                    dve.tensor_copy(hqT[:, IC // 2:, :], bank[5].bitcast(BF16).rearrange("p (c n) -> p c n", n=P))\
                       .then_inc(hqT_b, 1)
                hidden(1)
                if back1:
                    k = (t - 1) * 4
                    dve.wait_ge(hl_done, t * NCH)
                    dve.tensor_reduce(hmax[:, b:b + 1], hl_buf[:, b, :], AX.X, ALU.max,
                                      apply_absolute_value=True).then_inc(dve_b, 1)
                    dve.wait_ge(rinv_done, t)
                    dve.wait_ge(dve_b, k + 1)
                    dve.tensor_scalar(rlim[:, b:b + 1], hmax[:, b:b + 1], rinv[:, b:b + 1], QUANT_EPS,
                                      ALU.mult, ALU.max).then_inc(dve_b, 1)
                    dve.wait_ge(dve_b, k + 2)
                    dve.reciprocal(rrec[:, b:b + 1], rlim[:, b:b + 1]).then_inc(dve_b, 1)
                    dve.wait_ge(dve_b, k + 3)
                    dve.tensor_scalar(s_h[:, b:b + 1], rrec[:, b:b + 1], rinv[:, b:b + 1], QMAX,
                                      ALU.mult, ALU.mult).then_inc(s_h_done, 1)
                    dve.tensor_scalar(dq_h[:, b:b + 1], rlim[:, b:b + 1], wmean[:, 0:1], None,
                                      ALU.mult).then_inc(dve_b, 1)
                hidden(2)
                hidden(3)
                if back1:
                    dve.wait_ge(hs_done, t)
                    dve.tensor_scalar(hq, hl_buf[:, b, :], MAGIC, None, ALU.subtract).then_inc(hq_done, 1)
                if back2:
                    dve.wait_ge(down_mm, t - 1)
                    dve.scalar_tensor_tensor(tile(x_sb, t - 2), bank[6 + j], dq_h[:, j:j + 1], tile(x_sb, t - 2),
                                             ALU.mult, ALU.add).then_inc(x2_done, 1)

            pipelined(dve, ffn, T)

            dve.wait_ge(mask_landed, 16)
            dve.tensor_reduce(valid, mask_sb.rearrange("p (t m) -> p t m", t=T), AX.X, ALU.max).then_inc(dve_c, 1)
            dve.tensor_scalar(negb.rearrange("p t m -> p (t m)"), mask_sb, -1.0, -MASKED, ALU.add, ALU.mult)\
               .then_inc(dve_c, 1)
            dve.wait_ge(dve_c, 2)
            dve.wait_ge(x2_done, T)

            def norm_start(t, j, k, chain, out_sem):
                dve.bn_stats(st1[:, j, :], tile(x_sb, t)).then_inc(chain, 1)
                dve.wait_ge(chain, k + 1)
                alone(dve)
                dve.bn_aggr(mv[:, j, :], st1[:, j, :]).then_inc(chain, 1)
                dve.wait_ge(chain, k + 2)
                dve.tensor_scalar(ve1[:, j:j + 1], mv[:, j, 1:2], LN_EPS, None, ALU.add).then_inc(out_sem, 1)

            def attend(t, j, now, back1, back2):
                b = 1 - j
                if now:
                    norm_start(t, j, t * 2 + 2, dve_c, ve_done)
                if back1:
                    dve.wait_ge(score_mm, t)
                    dve.scalar_tensor_tensor(smx[:, b, :], bank[3 - j][:, 0:P], ATT_SCALE, tile(negb, t - 1),
                                             ALU.mult, ALU.add).then_inc(smx_done, 1)
                    dve.wait_ge(smx_done, t)
                    dve.tensor_reduce(nmax[:, b:b + 1], smx[:, b, :], AX.X, ALU.max, negate=True)\
                       .then_inc(nmax_done, 1)
                if back2:
                    dve.wait_ge(read_mm, t - 1)
                    dve.reciprocal(rv[:, j:j + 1], rsum[:, j:j + 1]).then_inc(rv_done, 1)
                    dve.wait_ge(rv_done, (t - 2) * 2 + 1)
                    dve.tensor_tensor(rv2[:, j:j + 1], rv[:, j:j + 1], valid[:, bass.ds(t - 2, 1)], ALU.mult)\
                       .then_inc(rv_done, 1)
                    dve.wait_ge(rv_done, (t - 2) * 2 + 2)
                    dve.scalar_tensor_tensor(tile(x_sb, t - 2), bank[6 + j], rv2[:, j:j + 1], tile(x_sb, t - 2),
                                             ALU.mult, ALU.add).then_inc(x3_done, 1)
                if now:
                    dve.wait_ge(rs_done, t + 1)
                    dve.tensor_scalar(xh[:, j, :], tile(x_sb, t), mv[:, j, 0:1], rs1[:, j:j + 1],
                                      ALU.subtract, ALU.mult).then_inc(xh_done, 1)

            pipelined(dve, attend, T)
            dve.wait_ge(x3_done, T)

            dve.wait_ge(rt_done, 1)
            dve.scalar_tensor_tensor(rt_lo, rt_raw, WSCALE, rt_hi, ALU.mult, ALU.subtract).then_inc(rt_done, 1)

            def route(t, j, now, back1, back2):
                b = 1 - j
                if now:
                    norm_start(t, j, t * 2, dve_d, vd_done)
                if back1:
                    dve.wait_ge(xn_hi_done, t)
                    dve.tensor_tensor(xnT_lo[:, :, bass.ds((t - 1) * P, P)],
                                      bank[b].rearrange("p (c n) -> p c n", c=DC),
                                      xnT_hi[:, :, bass.ds((t - 1) * P, P)], ALU.subtract).then_inc(xn_lo_done, 1)
                if back2:
                    dve.wait_ge(logit_mm, t - 1)
                    dve.tensor_scalar(tile(logit, t - 2), bank[2 + j][:, 0:NE], 1.0 / WSCALE, None, ALU.mult)\
                       .then_inc(logit_done, 1)
                    dve.tensor_scalar(e_pair[:, 1, bass.ds(t - 2, 1)], bank[2 + j][:, NE:NE + 1], -1.0 / WSCALE,
                                      None, ALU.mult).then_inc(logit_done, 1)
                if now:
                    dve.wait_ge(rd_done, t + 1)
                    dve.tensor_scalar(xh[:, j, :], tile(x_sb, t), mv[:, j, 0:1], rs1[:, j:j + 1],
                                      ALU.subtract, ALU.mult).then_inc(xn_done, 1)

            pipelined(dve, route, T)
            n = 2 * T
            dve.wait_ge(logit_done, 2 * T)
            dve.wait_ge(iota_done, 1)

            def wide(v):
                return v.unsqueeze(2).to_broadcast([P, T, NE])

            def step(ins):
                ins.then_inc(dve_d, 1)

            for a, (src, m, least, hot) in enumerate(((logit, m1, least1, first), (scr, m2, least2, second))):
                step(dve.tensor_reduce(m, src, AX.X, ALU.max))
                dve.wait_ge(dve_d, n + 1)
                step(dve.tensor_tensor(cand, src, wide(m), ALU.is_ge))
                dve.wait_ge(dve_d, n + 2)
                step(dve.scalar_tensor_tensor(cand, cand, -2.0 * NE, iota8, ALU.mult, ALU.add))
                dve.wait_ge(dve_d, n + 3)
                step(dve.tensor_reduce(least, cand, AX.X, ALU.min))
                dve.wait_ge(dve_d, n + 4)
                step(dve.tensor_tensor(hot, cand, wide(least), ALU.is_equal))
                dve.wait_ge(dve_d, n + 5)
                n += 5
                if a == 0:
                    step(dve.scalar_tensor_tensor(scr, first, MASKED, logit, ALU.mult, ALU.add))
                    dve.wait_ge(dve_d, n + 1)
                    n += 1
            dve.tensor_tensor(e_pair[:, 0, :], m2, m1, ALU.subtract).then_inc(edif_done, 1)
            dve.wait_ge(eexp_done, 1)
            step(dve.tensor_scalar(w1, e_pair[:, 0, :], 1.0, None, ALU.add))
            step(dve.tensor_scalar(w2, e_pair[:, 1, :], 1.0, None, ALU.add))
            dve.wait_ge(dve_d, n + 2)
            step(dve.reciprocal(w1, w1))
            step(dve.reciprocal(w2, w2))
            dve.wait_ge(dve_d, n + 4)
            step(dve.tensor_scalar(w1, w1, 1.0 / WSCALE, None, ALU.mult))
            for u in range(NSH):
                step(dve.tensor_scalar(comb[:, :, NE + u], w2, 1.0 / WSCALE, None, ALU.mult))
            dve.wait_ge(dve_d, n + 5 + NSH)
            step(dve.tensor_tensor(w2, e_pair[:, 0, :], w1, ALU.mult))
            step(dve.tensor_tensor(first, first, wide(w1), ALU.mult))
            dve.wait_ge(dve_d, n + 7 + NSH)
            step(dve.tensor_tensor(second, second, wide(w2), ALU.mult))
            dve.wait_ge(dve_d, n + 8 + NSH)
            dve.tensor_tensor(comb[:, :, 0:NE], first, second, ALU.add).then_inc(comb_done, 1)
            dve.wait_ge(comb_done, 1)

            def split_low(u):
                s = u % 2
                dve.wait_ge(w_hi_done, u + 1)
                dve.scalar_tensor_tensor(w_lo[:, s * RAW:(s + 1) * RAW], raw_w[:, s, :], WSCALE,
                                         w_hi[:, s * RAW:(s + 1) * RAW], ALU.mult, ALU.subtract).then_inc(w_lo_done, 1)

            split_low(0)
            for u in range(NU):
                if u + 1 < NU:
                    split_low(u + 1)

                def expert(t, j, now, back1, back2, n0=u * T, u=u):
                    b = 1 - j
                    if now:
                        dve.wait_ge(silu_d, t + (n0 + 1))
                        if n0 or not isinstance(t, int) or t >= 2:
                            dve.wait_ge(hd_tr, t + (n0 - 1))
                        dve.scalar_tensor_tensor(hd[:, j, :], bank[j][:, H:2 * H],
                                                 comb[:, bass.ds(t, 1), u:u + 1].rearrange("p a b -> p (a b)"),
                                                 sgd[:, j, :], ALU.mult, ALU.mult).then_inc(hd_done, 1)
                    if back1:
                        dve.wait_ge(hT_hi_done, t + n0)
                        dve.tensor_tensor(hT_lo[:, b, :], bank[3 - j][:, 0:H], hT_hi[:, b, :], ALU.subtract)\
                           .then_inc(hT_lo_done, 1)
                    if back2:
                        dve.wait_ge(dn_mm, t + (n0 - 1))
                        dve.scalar_tensor_tensor(tile(x_sb, t - 2), bank[4 + j], 1.0 / WSCALE, tile(x_sb, t - 2),
                                                 ALU.mult, ALU.add).then_inc(acc_done, 1)

                pipelined(dve, expert, T)


def kernel(x, ctx_2048, mask_BxS2_bk0, L0_xattn_decay, L0_xattn_W_in, L0_xattn_b_in, L0_xattn_W_out, L0_xattn_b_out,
           L0_xattn_gamma, L0_xattn_beta, L0_ffn_w_gate, L0_ffn_w_up, L0_ffn_w_down, L0_ffn_ln_weight, L1_ffn_gate_w,
           L1_ffn_w_gate, L1_ffn_w_up, L1_ffn_w_down, L1_ffn_sh_gate, L1_ffn_sh_up, L1_ffn_sh_down, L1_ffn_se_gate_w):
    import concourse.bacc as bacc
    from concourse.bass_utils import run_bass_kernel_spmd

    def lay(a, *perm):
        a = np.asarray(a)
        return np.ascontiguousarray(a.transpose(perm) if perm else a)

    arrays = {
        "x": lay(x), "ctx": lay(ctx_2048), "ctxT": lay(ctx_2048, 0, 2, 1),
        "mask": lay(mask_BxS2_bk0).reshape(-1), "decay": lay(L0_xattn_decay).reshape(1, 1),
        "w_inT": lay(L0_xattn_W_in, 1, 0), "b_in": lay(L0_xattn_b_in),
        "w_outT": lay(L0_xattn_W_out, 1, 0), "b_out": lay(L0_xattn_b_out),
        "gamma": lay(L0_xattn_gamma), "beta": lay(L0_xattn_beta),
        "f_gateT": lay(L0_ffn_w_gate, 1, 0), "f_upT": lay(L0_ffn_w_up, 1, 0), "f_downT": lay(L0_ffn_w_down, 1, 0),
        "ln_weight": lay(L0_ffn_ln_weight), "routerT": lay(L1_ffn_gate_w, 1, 0),
        "e_gateT": lay(L1_ffn_w_gate, 0, 2, 1), "e_upT": lay(L1_ffn_w_up, 0, 2, 1),
        "e_downT": lay(L1_ffn_w_down, 0, 2, 1),
        "s_gateT": lay(L1_ffn_sh_gate, 1, 0), "s_upT": lay(L1_ffn_sh_up, 1, 0), "s_downT": lay(L1_ffn_sh_down, 1, 0),
        "se_gateT": lay(L1_ffn_se_gate_w, 1, 0),
    }
    nc = bacc.Bacc("TRN2", target_bir_lowering=False, num_devices=1)
    args = [nc.dram_tensor(f"in_{k}", a.shape, mybir.dt.from_np(a.dtype), kind="ExternalInput").ap()
            for k, a in arrays.items()]
    out = nc.dram_tensor("out_x", np.asarray(x).shape, F32, kind="ExternalOutput").ap()
    model_kernel(nc, *args, out)
    r = run_bass_kernel_spmd(nc, [{f"in_{k}": a for k, a in arrays.items()}], core_ids=[0])
    return r.results[0]["out_x"]
```

```python
from contextlib import ExitStack

import numpy as np

import concourse.bass as bass
from concourse import mybir

ALU = mybir.AluOpType
ACT = mybir.ActivationFunctionType
AX = mybir.AxisListType
F32 = mybir.dt.float32
BF16 = mybir.dt.bfloat16
F16 = mybir.dt.float16
U8 = mybir.dt.uint8
U32 = mybir.dt.uint32

P = 128
MAGIC = 1.5 * 2.0 ** 23
LN_EPS = 1e-5
RMS_EPS = 1e-6
QUANT_EPS = 1e-5
QMAX = 127.0
WSCALE = 64.0
MASKED = -1e30


def pipelined(eng, body, tiles, first=0, before_last=None):
    if first == 0:
        body(0, 0, True, False, False)
    body(1, 1, True, True, False)
    with eng.Fori(0, (tiles - 2) // 2) as i:
        for j in range(2):
            body(i * 2 + 2 + j, j, True, True, True)
    if tiles % 2:
        body(tiles - 1, 0, True, True, True)
    body(tiles, tiles % 2, False, True, True)
    if before_last:
        before_last()
    body(tiles + 1, (tiles + 1) % 2, False, False, True)


def staged(eng, body, tiles, depth, first=0):
    head = depth + depth % 2
    for n in range(first, head):
        body(n, n % 2, lambda k: n - k >= 0)
    with eng.Fori(0, (tiles - head) // 2) as i:
        for j in range(2):
            body(i * 2 + (head + j), j, lambda k: True)
    for n in range(tiles, tiles + depth):
        body(n, n % 2, lambda k: n - k < tiles)


def by_pairs(eng, body, tiles):
    body(0, 0)
    body(1, 1)
    with eng.Fori(0, (tiles - 2) // 2) as i:
        for j in range(2):
            body(i * 2 + 2 + j, j)
    if tiles % 2:
        body(tiles - 1, 0)


def model_kernel(nc, x, ctx_in, ctxT_in, mask, decay, w_inT, b_in, w_outT, b_out, gamma, beta,
                 f_gateT, f_upT, f_downT, ln_weight, routerT, e_gateT, e_upT, e_downT,
                 s_gateT, s_upT, s_downT, se_gateT, out):
    B, S, D = x.shape
    T = B * S // P
    DC = D // P
    I = f_gateT.shape[1]
    IC = I // P
    NE, _, H = e_gateT.shape
    HC = H // P
    NSH = s_gateT.shape[1] // H
    HT = T // 2
    NBLK = 2 * T + NE - 1
    CH = 512
    NCH = I // CH
    RAW = DC * 2 * H + HC * D
    ATT_SCALE = float(D) ** -0.5
    assert S == P and D == CH and T % 2 == 0

    es = ExitStack()
    with es:
        def sb(name, shape, dt):
            return es.enter_context(nc.sbuf_tensor(name, shape, dt))

        def sem(name):
            return es.enter_context(nc.semaphore(name))

        x_sb = sb("x_sb", [P, T, D], F32)
        big = sb("big", [P, 28672], F32)
        wq = big[:, 0:12288].bitcast(BF16)
        reg_a = big[:, 12288:20480]
        reg_b = big[:, 20480:28672]
        reg_c = sb("reg_c", [P, 8192], F32)
        reg_x = sb("reg_x", [P, DC * T * P], BF16)
        pair = sb("pair", [P, 2 * D], F32)
        gamma_b, beta_b = pair[:, 0:D], pair[:, D:2 * D]
        extra = sb("extra", [P, 1296], F32)
        xq = sb("xq", [P, 2, D], BF16)
        ident_h = sb("ident_h", [P, P], BF16)
        ident16 = sb("ident16", [P, P], F16)
        ident = sb("ident", [P, P], F32)
        small = sb("small", [P, 960], F32)

        cols = [0]

        def tiny(n):
            cols[0] += n
            assert cols[0] <= 960
            return small[:, cols[0] - n:cols[0]]

        ctx_sb = reg_a[:].rearrange("p (t d) -> p t d", t=T)
        y_buf = wq[:, DC * I:].bitcast(F32).rearrange("p (t d) -> p t d", t=T)
        w_in_sb = reg_x[:, 0:2 * DC * D].bitcast(F32).rearrange("p (c e) -> p c e", c=DC)
        w_out_sb = reg_x[:, 2 * DC * D:4 * DC * D].bitcast(F32).rearrange("p (c e) -> p c e", c=DC)
        rows = wq[0:1, 0:4096].bitcast(F32)
        b_in_row, b_out_row = rows[:, 0:D], rows[:, D:2 * D]
        decay_row = rows[:, 2 * D:2 * D + 1]
        keep_row = rows[:, 2 * D + 1:2 * D + 2]
        geo_row = rows[:, 2 * D + 128:2 * D + 256]
        ones_row = rows[:, 2 * D + 256:2 * D + 384]
        wsum_row = rows[:, 2 * D + 384:2 * D + 385]
        wsum16_row = rows[:, 2 * D + 400:2 * D + 400 + T]
        ones = tiny(P)
        cbarT = tiny(DC * T)
        y1T = tiny(DC * T)
        wcols = extra[:, 0:T * T].rearrange("p (t k) -> p t k", t=T)
        cbar = extra[0:T, 256:256 + D]
        y1 = extra[0:T, 768:768 + D]
        sum_f = w_in_sb[0:T, 0, :]
        sum_rest = w_in_sb[0:T, 1, :]
        sum_mid = w_in_sb[0:T, 3, :].bitcast(BF16)[:, 0:D]
        sum_parts = w_in_sb[:, 2, :].bitcast(BF16)[0:96, 0:D]
        pick = xq[0:96, 0, 0:T]
        xqT = reg_x[:].rearrange("p (c n) -> p c n", c=DC)
        raw_gate, raw_up, raw_down = reg_b, reg_c, reg_a
        wq_gate = wq[:, 0:DC * I].rearrange("p (c i) -> p c i", c=DC)
        wq_up = wq[:, DC * I:2 * DC * I].rearrange("p (c i) -> p c i", c=DC)
        wq_down = wq[:, 2 * DC * I:].rearrange("p (c o) -> p c o", c=IC)
        h_buf = reg_c[:, 0:2 * I].rearrange("p (s i) -> p s i", s=2)
        hl_buf = reg_c[:, 2 * I:4 * I].rearrange("p (s i) -> p s i", s=2)
        sg_buf = reg_b[:, 0:2 * CH].rearrange("p (s i) -> p s i", s=2)
        hq = reg_b[:, 1024:2048].bitcast(BF16)
        hqT = reg_b[:, 2048:3072].bitcast(BF16).rearrange("p (c n) -> p c n", c=IC)
        lnw_b = reg_b[:, 4096:4096 + I]
        whole = [wq[:, 0:DC * I], reg_b[:, 0:DC * I // 2].bitcast(BF16)]
        junk = reg_b[:, 3072:3072 + I // 2].bitcast(BF16)
        abs_part = tiny(3 * DC)
        wabs = tiny(3)
        wmean = tiny(3)
        wscale = tiny(3)
        stats_flat = tiny(6 * T)
        stats = stats_flat.rearrange("p (t s) -> p t s", s=6)
        mean2 = tiny(T)
        neg_mean = tiny(T)
        vpe = tiny(T)
        tmp16 = tiny(T)
        rstd = tiny(T)
        neg_half = tiny(T)
        nmr = tiny(T)
        amax = tiny(T)
        s_x = tiny(T)
        dq_gate = tiny(T)
        dq_up = tiny(T)
        sumsq = tiny(2)
        ms = tiny(2)
        rinv = tiny(2)
        hmax = tiny(2)
        rlim = tiny(2)
        rrec = tiny(2)
        s_h = tiny(2)
        dq_h = tiny(2)
        ctxT_at = lambda t: 3 * DC * T * P // 4 + t * D if isinstance(t, int) and t < T // 4 else (t - T // 4) * D
        mask_sb = extra[:, 0:T * P // 4].bitcast(U8)
        negb = reg_x[:, 0:2 * T * P].bitcast(F32).rearrange("p (t m) -> p t m", t=T)
        xh = pair[:].rearrange("p (s d) -> p s d", s=2)
        c_work = big[:, 3 * RAW:4 * RAW]
        xhT = c_work[:, 0:1024].rearrange("p (s d) -> p s d", s=2)
        xn = c_work[:, 1024:2048].rearrange("p (s d) -> p s d", s=2)
        smx = c_work[:, 2048:2304].rearrange("p (s d) -> p s d", s=2)
        prob = c_work[:, 2304:2560].rearrange("p (s d) -> p s d", s=2)
        probT = c_work[:, 2560:2816].rearrange("p (s d) -> p s d", s=2)
        valid = tiny(T)
        st1 = tiny(12).rearrange("p (s k) -> p s k", s=2)
        mv = tiny(4).rearrange("p (s k) -> p s k", s=2)
        ve1 = tiny(2)
        rs1 = tiny(2)
        nmax = tiny(2)
        rsum = tiny(2)
        rv = tiny(2)
        rv2 = tiny(2)
        st2 = stats_flat[:, 0:12].rearrange("p (s k) -> p s k", s=2)
        mv2 = stats_flat[:, 12:16].rearrange("p (s k) -> p s k", s=2)
        ve2 = stats_flat[:, 16:18]
        rs2 = stats_flat[:, 18:20]
        xnT = reg_c[:].bitcast(F16).rearrange("p (c n) -> p c n", c=2 * DC)
        tail = big[:, 9 * RAW:9 * RAW + 1024]
        RS = 1024
        NPC = RAW // RS
        SUMS = [0, 0, 2, 4, 6, 9, 11, 14, 16]
        EARLY = 8
        SPLITS = [NPC + 1, 6, 8, 12, 16, 20, 24, 27, 27]

        def splits_beside(m, part):
            ahead = 1 if m >= 2 and SPLITS[m + 1] > SPLITS[m] else 0
            return range(SPLITS[m], SPLITS[m] + ahead) if part == 0 else range(SPLITS[m] + ahead, SPLITS[m + 1])

        def wait_low(eng, n):
            eng.wait_ge(w_lo_early, min(n, EARLY))
            if n > EARLY:
                eng.wait_ge(w_lo_done, n - EARLY)

        stage = reg_x[:, 0:2 * RAW].bitcast(F32)
        last_x = reg_x[:, 2 * NPC * RS:2 * NPC * RS + 2048].bitcast(F32)
        xhl = last_x.bitcast(F16).rearrange("p (s n) -> p s n", s=2)
        w_all = big[:, 0:(NE + 1) * RAW].bitcast(F16).rearrange("p (e w) -> p e w", e=NE + 1)
        lower_h = extra[:, 1024:1024 + P // 2].bitcast(BF16)
        ones_h = extra[:, 1088:1088 + P // 2].bitcast(BF16)
        rt_raw = extra[:, 1152:1152 + DC * (NE + 1)].rearrange("p (c e) -> p c e", c=DC)
        rt_hi = extra[:, 1190:1208].bitcast(F16).rearrange("p (c e) -> p c e", c=DC)
        rt_lo = extra[:, 1208:1226].bitcast(F16).rearrange("p (c e) -> p c e", c=DC)
        TE = T * NE
        routed_h = extra[:, 1228:1228 + TE // 2].bitcast(BF16)
        cmp_row = extra[0:1, 0:NBLK * NE].rearrange("p (n e) -> p n e", n=NBLK)

        def routing(n):
            return extra[:, TE * n:TE * (n + 1)].rearrange("p (t e) -> p t e", t=T)

        logit, first, second, cand, scr, iota8 = [routing(n) for n in range(6)]
        carry, before = routing(6), routing(7)
        m1, m2, least1, least2, w1, w2, sgate = [tiny(T) for _ in range(7)]
        e_pair = tiny(2 * T).rearrange("p (k t) -> p k t", k=2)
        blocks, ends, begins = tiny(NE), tiny(NE), tiny(NE)
        ones8 = ones[:, 0:NE]
        slot, place = [xq[:, 1, 4 * T * k:4 * T * (k + 1)].bitcast(F32).rearrange("p (a t) -> p a t", a=2)
                       for k in range(2)]
        slot_u = tiny(2 * T).bitcast(U32).rearrange("p (a t) -> p a t", a=2)
        place_u = tiny(2 * T).bitcast(U32).rearrange("p (a t) -> p a t", a=2)
        token_id = tiny(T).bitcast(U32)
        zeros = xq[:, 0, 0:2 * NBLK].bitcast(U32)
        iota_n = xq[:, 0, 2 * NBLK:4 * NBLK].bitcast(F32)
        expert_f = xq[:, 0, 4 * NBLK:6 * NBLK].bitcast(F32)
        tokens_of = tiny(NBLK).bitcast(U32)
        expert_of = tiny(NBLK).bitcast(U32)
        token_now = tiny(2).bitcast(U32)
        GT = CH // P
        NG = T // GT
        sg_s = pair[:].rearrange("p (s n) -> p s n", s=2)
        hT_s = [v.bitcast(F16).rearrange("p (k c n) -> p k c n", k=2, c=HC) for v in (tail, last_x)]
        xg = extra[:, 0:1024].bitcast(F16).rearrange("p (s n) -> p s n", s=2)
        xgT = tail.bitcast(F16).rearrange("p (s n) -> p s n", s=2)
        sg_r = pair[:, 0:2 * H].rearrange("p (s n) -> p s n", s=2)
        h_hl = pair[:, 2 * H:4 * H].bitcast(F16).rearrange("p (s n) -> p s n", s=2)
        hT_r = xq
        y_out = last_x.rearrange("p (s n) -> p s n", s=2)
        ya = stage.rearrange("p (s n) -> p s n", n=D)

        psum = es.enter_context(nc.psum_tensor("psum", [P, 8 * CH], F32))
        bank = [psum[:, i * CH:(i + 1) * CH] for i in range(8)]

        consts_ready = sem("consts_ready")
        x_landed = [sem(f"x{i}_landed") for i in range(2)]
        wout_landed = sem("wout_landed")
        y0_done = sem("y0_done")
        cols_cleared = sem("cols_cleared")
        z_done = sem("z_done")
        zg_done = sem("zg_done")
        quant_ready = sem("quant_ready")
        xs_done = sem("xs_done")
        rows_landed = sem("rows_landed")
        ctx_landed = [sem(f"ctx_part{i}_landed") for i in range(4)]
        win_landed = sem("win_landed")
        vec_landed = sem("vec_landed")
        raw_landed = [sem(f"raw{i}_landed") for i in range(3)]
        keep_done = sem("keep_done")
        geo_done = sem("geo_done")
        wcol_mm = sem("wcol_mm")
        wcol_done = sem("wcol_done")
        chain_mm = sem("chain_mm")
        chain_done = sem("chain_done")
        bcast_mm = sem("bcast_mm")
        bcast_used = sem("bcast_used")
        dve_a = sem("dve_a")
        var_ready = sem("var_ready")
        rstd_ready = sem("rstd_ready")
        rstd_done = sem("rstd_done")
        xb_done = sem("xb_done")
        abs_done = sem("abs_done")
        abs_mm = sem("abs_mm")
        wscale_done = sem("wscale_done")
        shifted = sem("shifted")
        whole_done = sem("whole_done")
        wq_done = sem("wq_done")
        xq_done = sem("xq_done")
        xq_tr = sem("xq_tr")
        xqT_done = sem("xqT_done")
        gate_mm = sem("gate_mm")
        up_mm = sem("up_mm")
        silu_done = sem("silu_done")
        h_done = sem("h_done")
        hl_done = sem("hl_done")
        sq_done = sem("sq_done")
        ms_done = sem("ms_done")
        rinv_done = sem("rinv_done")
        dve_b = sem("dve_b")
        s_h_done = sem("s_h_done")
        hs_done = sem("hs_done")
        hq_done = sem("hq_done")
        hq_tr = sem("hq_tr")
        hqT_a = sem("hqT_a")
        hqT_b = sem("hqT_b")
        down_mm = sem("down_mm")
        x2_done = sem("x2_done")
        mask_landed = sem("mask_landed")
        ctx2_landed = sem("ctx2_landed")
        dve_c = sem("dve_c")
        ve_done = sem("ve_done")
        rs_done = sem("rs_done")
        xh_done = sem("xh_done")
        xh_tr = sem("xh_tr")
        xhT_done = sem("xhT_done")
        score_mm = sem("score_mm")
        nmax_done = sem("nmax_done")
        prob_done = sem("prob_done")
        prob_tr = sem("prob_tr")
        probT_done = sem("probT_done")
        read_mm = sem("read_mm")
        x3_done = sem("x3_done")
        rt_landed = sem("rt_landed")
        rt_done = sem("rt_done")
        iota_done = sem("iota_done")
        dve_d = sem("dve_d")
        vd_done = sem("vd_done")
        rd_done = sem("rd_done")
        xn_done = sem("xn_done")
        xn_tr = sem("xn_tr")
        xnT_done = sem("xnT_done")
        logit_mm = sem("logit_mm")
        edif_done = sem("edif_done")
        eexp_done = sem("eexp_done")
        w_landed = [sem(f"w{i}_landed") for i in range(NE + 2)]
        ctxT_landed = [sem(f"ctxT{i}_landed") for i in range(4)]
        xhl_hi_done = sem("xhl_hi_done")
        xhl_done = sem("xhl_done")
        xn_stored = [sem(f"xn{i}_stored") for i in range(2)]
        hot_done = sem("hot_done")
        rank_mm = sem("rank_mm")
        rank_read = sem("rank_read")
        place_done = sem("place_done")
        table_cleared = sem("table_cleared")
        table_written = sem("table_written")
        table_landed = sem("table_landed")
        tokens_copied = sem("tokens_copied")
        experts_known = sem("experts_known")
        s_gate_mm = sem("s_gate_mm")
        s_up_mm = sem("s_up_mm")
        s_silu = sem("s_silu")
        s_hid = sem("s_hid")
        s_hi = sem("s_hi")
        s_lo = sem("s_lo")
        s_down_mm = sem("s_down_mm")
        xg_landed = [sem(f"xg{i}_landed") for i in range(2)]
        xg_tr = sem("xg_tr")
        xgT_hi = sem("xgT_hi")
        xgT_lo = sem("xgT_lo")
        hr_hi = sem("hr_hi")
        hr_lo = sem("hr_lo")
        hT_done = sem("hT_done")
        y_ready = sem("y_ready")
        y_stored = [sem(f"y{i}_stored") for i in range(2)]
        ya_landed = [sem(f"ya{i}_landed") for i in range(2 * NPC)]
        ya_used = sem("ya_used")
        w_hi_done = sem("w_hi_done")
        w_scaled = sem("w_scaled")
        w_lo_early = sem("w_lo_early")
        w_lo_done = sem("w_lo_done")
        gu_mm = sem("gu_mm")
        silu_d = sem("silu_d")
        hd_done = sem("hd_done")
        hd_tr = sem("hd_tr")
        dn_mm = sem("dn_mm")
        acc_done = sem("acc_done")
        stored = sem("stored")
        lnw_landed = sem("lnw_landed")
        smx_done = sem("smx_done")
        mask_done = sem("mask_done")
        rv_done = sem("rv_done")
        logit_done = sem("logit_done")

        xn_dram = nc.dram_tensor("xn_rows", [T * P, 2 * D], F16).ap()
        table = nc.dram_tensor("token_table", [P * NBLK, 1], U32).ap()
        y_dram = nc.dram_tensor("expert_rows", [NBLK * P, D], F32).ap()

        x_v = x.rearrange("b p d -> p b d")
        out_v = out.rearrange("b p d -> p b d")
        ctx_v = ctx_in.rearrange("b p d -> p b d")
        ctxT_v = ctxT_in.rearrange("b (c p) m -> p c b m", p=P)
        raw_v = [f_gateT.rearrange("(c p) i -> p c i", p=P), f_upT.rearrange("(c p) i -> p c i", p=P),
                 f_downT.rearrange("(c p) o -> p c o", p=P)]
        raw_sb = [raw_gate[:].rearrange("p (c i) -> p c i", c=DC), raw_up[:].rearrange("p (c i) -> p c i", c=DC),
                  raw_down[:].rearrange("p (c o) -> p c o", c=IC)]

        block = es.enter_context(nc.Block())

        flat_raw = [reg_b, reg_c, reg_a]

        def alone(eng):
            eng.nop(nofuse=True)

        def slot_count(t):
            return (t // 2) * 16

        def raw_unit(u):
            return big[:, (u + 1) * RAW:(u + 2) * RAW] if u < NE else stage

        def piece_of(n, part):
            u, k = divmod(n, NPC)
            at = part * RAW + k * RS
            return w_all[:, u % (NE + 1), at:at + RS]

        def raw_piece_of(n):
            return raw_unit(n // NPC)[:, n % NPC * RS:(n % NPC + 1) * RS]

        def tile(buf, t):
            return buf[:, bass.ds(t, 1), :].rearrange("p a d -> p (a d)")

        def raw_piece(m, c):
            return flat_raw[m][:, c * 4 * CH:(c + 1) * 4 * CH]

        @block.sync
        def _(sp):
            for v, r in ((b_in, b_in_row), (b_out, b_out_row)):
                sp.dma_start(r, v.rearrange("(a n) -> a n", a=1)).then_inc(rows_landed, 16)
            sp.dma_start(decay_row, decay).then_inc(rows_landed, 16)
            for q in range(4):
                sp.dma_start(ctx_sb[:, q * T // 4:(q + 1) * T // 4, :],
                             ctx_v[:, q * T // 4:(q + 1) * T // 4, :]).then_inc(ctx_landed[q], 16)
            halves = [slice(h * HT, (h + 1) * HT) for h in range(2)]
            sp.dma_start(x_sb[:, halves[0], :], x_v[:, halves[0], :]).then_inc(x_landed[0], 16)
            sp.dma_start(w_in_sb, w_inT.rearrange("(c p) e -> p c e", p=P)).then_inc(win_landed, 16)
            sp.dma_start(w_out_sb, w_outT.rearrange("(c p) e -> p c e", p=P)).then_inc(wout_landed, 16)
            sp.dma_start(x_sb[:, halves[1], :], x_v[:, halves[1], :]).then_inc(x_landed[1], 16)
            for v, r in ((gamma, gamma_b), (beta, beta_b)):
                sp.dma_start(r[:], v.partition_broadcast(P)).then_inc(vec_landed, 16)
            sp.dma_start(raw_sb[0], raw_v[0]).then_inc(raw_landed[0], 16)
            sp.dma_start(raw_sb[1], raw_v[1]).then_inc(raw_landed[1], 16)
            sp.wait_ge(chain_mm, 1)
            sp.dma_start(raw_sb[2], raw_v[2]).then_inc(raw_landed[2], 16)
            sp.wait_ge(wq_done, 2)
            sp.dma_start(lnw_b, ln_weight.partition_broadcast(P)).then_inc(lnw_landed, 16)
            sp.wait_ge(wq_done, 6)
            sp.dma_start(ctx_sb, ctx_v).then_inc(ctx2_landed, 16)
            sp.dma_start(mask_sb, mask.partition_broadcast(P)).then_inc(mask_landed, 16)
            with nc.allow_non_contiguous_dma(reason="router columns are narrow"):
                sp.dma_start(rt_raw[:, :, 0:NE], routerT.rearrange("(c p) e -> p c e", p=P)).then_inc(rt_landed, 16)
                sp.dma_start(rt_raw[:, :, NE:NE + 1], se_gateT.rearrange("(c p) e -> p c e", p=P)).then_inc(rt_landed, 16)
            for q in range(4):
                if q == 1:
                    sp.wait_ge(x2_done, T)
                for c in range(DC):
                    at = ctxT_at(q * T // 4)
                    sp.dma_start(reg_b[:, at:at + T // 4 * D].rearrange("p (b c m) -> p b c m", b=T // 4, c=DC)[:, :, c, :],
                                 ctxT_v[:, c, q * T // 4:(q + 1) * T // 4, :]).then_inc(ctxT_landed[q], 16)
            sp.wait_ge(iota_done, 3)
            sp.dma_start(table.rearrange("(p n) a -> p (n a)", n=NBLK), zeros).then_inc(table_cleared, 16)

            def load_weights(u):
                if 1 <= u <= NE:
                    gate_w, up_w, down_w = e_gateT[u - 1], e_upT[u - 1], e_downT[u - 1]
                else:
                    v = u // NE
                    gate_w, up_w, down_w = [s_gateT[:, v * H:(v + 1) * H], s_upT[:, v * H:(v + 1) * H],
                                            s_downT[v * H:(v + 1) * H, :]]
                raw = raw_unit(u)
                gu = raw[:, 0:DC * 2 * H].rearrange("p (c g i) -> p c g i", c=DC, g=2)
                for g, w in ((0, gate_w), (1, up_w)):
                    sp.dma_start(gu[:, :, g, :], w.rearrange("(c p) i -> p c i", p=P)).then_inc(w_landed[u], 16)
                sp.dma_start(raw[:, DC * 2 * H:].rearrange("p (c o) -> p c o", c=HC),
                             down_w.rearrange("(c p) o -> p c o", p=P)).then_inc(w_landed[u], 16)

            for u in range(2):
                load_weights(u)
            for t in range(T):
                sp.wait_ge(xhl_done, t + 1)
                sp.dma_start(xn_dram[t * P:(t + 1) * P, :], xhl[:, t % 2, :]).then_inc(xn_stored[t % 2], 16)
            sp.wait_ge(x3_done, T)
            for u in range(2, NE + 1):
                load_weights(u)
            sp.wait_ge(table_written, 2 * T * 16)
            sp.dma_start(tokens_of, table.rearrange("(p n) a -> p (n a)", n=NBLK)).then_inc(table_landed, 16)
            wait_low(sp, (NE + 1) * NPC)
            load_weights(NE + 1)

            def store_rows(n, j):
                sp.wait_ge(y_ready, n + 3)
                sp.dma_start(y_dram[bass.ds(n * P, P), :], y_out[:, j, :]).then_inc(y_stored[j], 16)

            by_pairs(sp, store_rows, NBLK)
            for t in range(0, T, 2):
                sp.wait_ge(acc_done, T + t + 2)
                sp.dma_start(out_v[:, t:t + 2, :], x_sb[:, t:t + 2, :]).then_inc(stored, 16)
            sp.wait_ge(stored, 16 * T // 2)

        @block.gpsimd
        def _(pool):
            pool.memset(ident[:], 0.0).then_inc(consts_ready, 1)
            pool.memset(ident_h[:], 0.0).then_inc(consts_ready, 1)
            pool.memset(ident16[:], 0.0).then_inc(consts_ready, 1)
            pool.memset(ones, 1.0).then_inc(consts_ready, 1)
            pool.memset(neg_half, -0.5).then_inc(consts_ready, 1)
            pool.memset(ones_row, 1.0).then_inc(consts_ready, 1)
            pool.wait_ge(consts_ready, 6)
            for m in (ident, ident_h, ident16):
                pool.affine_select(out=m[:], in_=m[:], compare_op=ALU.not_equal, fill=1.0, base=0,
                                   pattern=[[-1, P]], channel_multiplier=1).then_inc(consts_ready, 1)
            pool.memset(extra[:, 0:T * T], 0.0).then_inc(cols_cleared, 1)
            pool.wait_ge(consts_ready, 9)

            def deviations(k, h):
                pool.wait_ge(var_ready, 2 * k + h + 1)
                pool.tensor_tensor(rstd[:, h * HT:(h + 1) * HT], vpe[:, h * HT:(h + 1) * HT],
                                   neg_half[:, 0:HT], ALU.pow).then_inc(rstd_done, 1)
                pool.wait_ge(rstd_done, 2 * k + h + 1)
                pool.tensor_tensor(nmr[:, h * HT:(h + 1) * HT], neg_mean[:, h * HT:(h + 1) * HT],
                                   rstd[:, h * HT:(h + 1) * HT], ALU.mult).then_inc(rstd_ready, 1)

            def add_beta(h):
                with pool.Fori(h * HT // 4, (h + 1) * HT // 4) as i:
                    for t in (i * 4, i * 4 + 1, i * 4 + 2, i * 4 + 3):
                        pool.wait_ge(y0_done, t + 1)
                        pool.tensor_tensor(tile(x_sb, t), tile(x_sb, t), beta_b, ALU.add).then_inc(xb_done, 1)

            def times_gamma(h):
                with pool.Fori(h * HT // 4, (h + 1) * HT // 4) as i:
                    for t in (i * 4, i * 4 + 1, i * 4 + 2, i * 4 + 3):
                        pool.wait_ge(z_done, t + 1)
                        pool.tensor_tensor(tile(y_buf, t), tile(y_buf, t), gamma_b, ALU.mult).then_inc(zg_done, 1)

            deviations(0, 0)
            deviations(0, 1)
            pool.wait_ge(vec_landed, 32)
            add_beta(0)
            add_beta(1)
            deviations(1, 0)
            times_gamma(0)
            deviations(1, 1)
            times_gamma(1)
            deviations(2, 0)
            deviations(2, 1)
            pool.wait_ge(lnw_landed, 16)
            with pool.Fori(0, T // 2) as i:
                for j in range(2):
                    t = i * 2 + j
                    pool.wait_ge(hq_done, t + 1)
                    for c in range(NCH):
                        pool.wait_ge(h_done, t * NCH + c + 3)
                        pool.tensor_tensor(hl_buf[:, j, c * CH:(c + 1) * CH], h_buf[:, j, c * CH:(c + 1) * CH],
                                           lnw_b[:, c * CH:(c + 1) * CH], ALU.mult).then_inc(hl_done, 1)
                    pool.wait_ge(sq_done, t + 1)
                    alone(pool)
                    pool.tensor_scalar(ms[:, j:j + 1], sumsq[:, j:j + 1], 1.0 / I, RMS_EPS, ALU.mult, ALU.add)\
                        .then_inc(ms_done, 1)
                    pool.wait_ge(ms_done, t + 1)
                    pool.tensor_tensor(rinv[:, j:j + 1], ms[:, j:j + 1], neg_half[:, 0:1], ALU.pow)\
                        .then_inc(rinv_done, 1)
            pool.iota(iota8, pattern=[[0, T], [1, NE]], base=0, channel_multiplier=0,
                      allow_small_or_imprecise_dtypes=True).then_inc(iota_done, 1)
            pool.iota(iota_n, pattern=[[1, NBLK]], base=0, channel_multiplier=0,
                      allow_small_or_imprecise_dtypes=True).then_inc(iota_done, 1)
            pool.memset(zeros, 0).then_inc(iota_done, 1)
            pool.iota(token_id, pattern=[[P, T]], base=0, channel_multiplier=1).then_inc(iota_done, 1)
            pool.memset(lower_h, 1.0).then_inc(iota_done, 1)
            pool.memset(ones_h, 1.0).then_inc(iota_done, 1)
            pool.wait_ge(iota_done, 6)
            pool.affine_select(out=lower_h, in_=lower_h, compare_op=ALU.is_gt, fill=0.0, base=0,
                               pattern=[[1, P]], channel_multiplier=-1).then_inc(iota_done, 1)

            def early_low(n):
                pool.wait_ge(w_hi_done, n + 1)
                pool.tensor_tensor(piece_of(n, 1), raw_piece_of(n), piece_of(n, 0), ALU.subtract).then_inc(w_lo_early, 1)

            def attend(n, j, on):
                if on(0):
                    pool.wait_ge(ve_done, n + 1)
                    pool.tensor_tensor(rs1[:, j:j + 1], ve1[:, j:j + 1], neg_half[:, 0:1], ALU.pow).then_inc(rs_done, 1)
                b = 1 - j
                if on(3):
                    pool.wait_ge(vd_done, n - 2)
                    pool.tensor_tensor(rs2[:, b:b + 1], ve2[:, b:b + 1], neg_half[:, 0:1], ALU.pow).then_inc(rd_done, 1)
                    pool.wait_ge(xhl_hi_done, n - 2)
                    pool.tensor_tensor(xhl[:, b, D:2 * D], xn[:, b, :], xhl[:, b, 0:D], ALU.subtract).then_inc(xhl_done, 1)
                if isinstance(n, int) and T < n <= T + NPC:
                    early_low(n - T - 1)

            staged(pool, attend, T, 5)
            for n in range(NPC, EARLY):
                early_low(n)
            pool.wait_ge(table_cleared, 16)
            pool.wait_ge(place_done, 1)
            for a in range(2):
                for t in range(T):
                    pool.indirect_dma_start(table, bass.IndirectOffsetOnAxis(place_u[:, a, t:t + 1], 0),
                                            token_id[:, t:t + 1], None).then_inc(table_written, 16)
            pool.wait_ge(table_landed, 16)
            pool.wait_ge(experts_known, 1)
            for j in range(2):
                pool.wait_ge(xn_stored[j], T // 2 * 16)

            def gather_tokens(n, j):
                if not isinstance(n, int) or n >= 2:
                    pool.wait_ge(xg_tr, n - 1)
                    alone(pool)
                pool.tensor_copy(token_now[:, j:j + 1], tokens_of[:, bass.ds(n, 1)]).then_inc(tokens_copied, 1)
                pool.wait_ge(tokens_copied, n + 1)
                alone(pool)
                pool.indirect_dma_start(xg[:, j, :], None, xn_dram,
                                        bass.IndirectOffsetOnAxis(token_now[:, j:j + 1], 0)).then_inc(xg_landed[j], 16)

            by_pairs(pool, gather_tokens, NBLK)
            pool.wait_ge(y_stored[0], (NBLK + 1) // 2 * 16)
            pool.wait_ge(y_stored[1], NBLK // 2 * 16)
            wait_low(pool, (NE + 2) * NPC)
            for n in range(2 * T):
                s = n % (2 * NPC)
                if n >= 2 * NPC:
                    pool.wait_ge(ya_used, n - 2 * NPC + 1)
                pool.indirect_dma_start(ya[:, s, :], None, y_dram,
                                        bass.IndirectOffsetOnAxis(slot_u[:, n % 2, n // 2:n // 2 + 1], 0))\
                    .then_inc(ya_landed[s], 16)

        @block.scalar
        def _(act):
            act.wait_ge(rows_landed, 48)
            act.activation(keep_row, decay_row, ACT.Tanh, scale=0.5).then_inc(keep_done, 1)
            def norm_tiles(dst, src, k, h, done):
                act.wait_ge(rstd_ready, 2 * k + h + 1)
                with act.Fori(h * HT // 4, (h + 1) * HT // 4) as i:
                    for t in (i * 4, i * 4 + 1, i * 4 + 2, i * 4 + 3):
                        act.activation(tile(dst, t), tile(src, t), ACT.Identity, scale=rstd[:, bass.ds(t, 1)],
                                       bias=nmr[:, bass.ds(t, 1)]).then_inc(done, 1)

            def abs_sums(m):
                act.wait_ge(raw_landed[m], 16)
                for c in range(4):
                    if m or c:
                        act.wait_ge(abs_done, 4 * m + c)
                    act.activation(psum[:, 4 * CH:8 * CH], raw_piece(m, c), ACT.Abs,
                                   accum_out=abs_part[:, 4 * m + c:4 * m + c + 1]).then_inc(abs_done, 1)

            def shift_piece(m, c):
                act.activation(raw_piece(m, c), raw_piece(m, c), ACT.Copy, scale=wscale[:, m:m + 1],
                               bias=MAGIC).then_inc(shifted, 1)

            def shift(m):
                act.wait_ge(wscale_done, m + 1)
                for c in range(4):
                    shift_piece(m, c)

            def quantise(h):
                act.wait_ge(quant_ready, h + 1)
                with act.Fori(h * HT // 4, (h + 1) * HT // 4) as i:
                    for t in (i * 4, i * 4 + 1, i * 4 + 2, i * 4 + 3):
                        act.activation(tile(y_buf, t), tile(y_buf, t), ACT.Copy, scale=s_x[:, bass.ds(t, 1)],
                                       bias=MAGIC).then_inc(xs_done, 1)

            norm_tiles(y_buf, x_sb, 0, 0, y0_done)
            norm_tiles(y_buf, x_sb, 0, 1, y0_done)
            abs_sums(0)
            abs_sums(1)
            norm_tiles(y_buf, y_buf, 1, 0, z_done)
            norm_tiles(y_buf, y_buf, 1, 1, z_done)
            shift(0)
            shift(1)
            abs_sums(2)

            def evac_xq(t, j):
                act.wait_ge(xq_tr, t + 3)
                alone(act)
                act.activation(xqT[:, :, bass.ds(t * P, P)], bank[2 + j].bitcast(BF16)[:, 0:D]
                               .rearrange("p (c n) -> p c n", c=DC), ACT.Copy).then_inc(xqT_done, 1)

            def shift_back(m):
                act.wait_ge(shifted, 4 * m + 4)
                for c in range(4):
                    act.activation(whole[m][:, c * 4 * CH:(c + 1) * 4 * CH], raw_piece(m, c), ACT.Copy,
                                   bias=-MAGIC).then_inc(whole_done, 1)

            shift_back(0)
            quantise(0)
            act.wait_ge(whole_done, 4)
            shift_back(1)
            by_pairs(act, evac_xq, T)

            def ffn(t, j, now, back1, back2):
                def silu(c):
                    if now:
                        act.wait_ge(gate_mm, t * NCH + c + 1)
                        alone(act)
                        act.activation(sg_buf[:, c % 2, :], bank[c % 2], ACT.Silu,
                                       scale=dq_gate[:, bass.ds(t, 1)]).then_inc(silu_done, 1)
                        if isinstance(t, int) and t == 0:
                            shift_piece(2, c)

                silu(0)
                silu(1)
                if back2:
                    act.wait_ge(hq_tr, (t - 2) * 2 + 1)
                    act.activation(hqT[:, 0:IC // 2, :], bank[4].bitcast(BF16).rearrange("p (c n) -> p c n", n=P),
                                   ACT.Copy).then_inc(hqT_a, 1)
                silu(2)
                if back1:
                    act.wait_ge(s_h_done, t)
                    act.activation(hl_buf[:, 1 - j, :], hl_buf[:, 1 - j, :], ACT.Copy, bias=MAGIC,
                                   scale=s_h[:, 1 - j:2 - j]).then_inc(hs_done, 1)
                silu(3)
                if now:
                    act.wait_ge(h_done, t * NCH + NCH + 2)
                    act.activation(junk, h_buf[:, j, :], ACT.Square,
                                   accum_out=sumsq[:, j:j + 1]).then_inc(sq_done, 1)


            def router_high():
                act.wait_ge(rt_landed, 32)
                act.activation(rt_hi, rt_raw, ACT.Copy, scale=WSCALE).then_inc(rt_done, 1)

            def split_high(n):
                if n % NPC == 0:
                    act.wait_ge(w_landed[n // NPC], 48)
                    if n >= NPC:
                        wait_low(act, n)
                if n < EARLY:
                    act.activation(raw_piece_of(n), raw_piece_of(n), ACT.Copy, scale=WSCALE).then_inc(w_scaled, 1)
                    act.wait_ge(w_scaled, n + 1)
                act.activation(piece_of(n, 0), raw_piece_of(n), ACT.Copy, scale=1.0 if n < EARLY else WSCALE)\
                   .then_inc(w_hi_done, 1)

            def attend(n, j, on):
                b = 1 - j
                if isinstance(n, int) and T < n <= T + NPC:
                    split_high(n - T - 1)
                if on(1):
                    act.wait_ge(xh_tr, n)
                    act.activation(xhT[:, b, :], bank[7 * b], ACT.Copy).then_inc(xhT_done, 1)
                if on(2):
                    act.wait_ge(prob_tr, n - 1)
                    act.activation(probT[:, j, :], bank[2][:, 0:P], ACT.Copy).then_inc(probT_done, 1)
                if on(4):
                    act.wait_ge(xn_tr, n - 3)
                    alone(act)
                    act.activation(xnT[:, :, bass.ds((n - 4) * P, P)],
                                   bank[5].bitcast(F16).rearrange("p (c n) -> p c n", c=2 * DC),
                                   ACT.Copy).then_inc(xnT_done, 1)
                if on(3):
                    act.wait_ge(xn_done, n - 2)
                    if not isinstance(n, int) or n - 3 >= 2:
                        act.wait_ge(xn_tr, n - 4)
                        act.wait_ge(xn_stored[b], (n - 3) // 2 * 16)
                    act.activation(xhl[:, b, 0:D], xn[:, b, :], ACT.Copy).then_inc(xhl_hi_done, 1)
                if on(1):
                    act.wait_ge(nmax_done, n)
                    act.activation(prob[:, b, :], smx[:, b, :], ACT.Exp, bias=nmax[:, b:b + 1],
                                   accum_out=rsum[:, b:b + 1]).then_inc(prob_done, 1)

            pipelined(act, ffn, T, before_last=router_high)
            staged(act, attend, T, 5, first=1)

            def shared(v):
                for g in range(NG):
                    for c in range(HC):
                        m = (v * NG + g) * HC + c
                        act.wait_ge(s_gate_mm, m + 1)
                        if m >= 2:
                            act.wait_ge(s_lo, m - 1)
                        act.activation(sg_s[:, m % 2, :], bank[m % 2], ACT.Silu, scale=1.0 / WSCALE).then_inc(s_silu, 1)
                        if v == 0:
                            for n in splits_beside(m, 0):
                                split_high(n)
                        act.wait_ge(s_hid, m + 1)
                        if g >= 2:
                            act.wait_ge(s_down_mm, (v * NG + g - 1) * GT)
                        act.activation(hT_s[g % 2][:, 0, c, :], sg_s[:, m % 2, :], ACT.Copy).then_inc(s_hi, 1)
                        if v == 0:
                            for n in splits_beside(m, 1):
                                split_high(n)
                if v == 0:
                    routed(0, 0, True, False, False)

            for j in range(2):
                act.wait_ge(xn_stored[j], T // 2 * 16)

            def routed(t, j, now, back1, back2):
                b = 1 - j
                if isinstance(t, int) and NBLK - 1 <= t < NBLK - 1 + NPC:
                    split_high((NE + 1) * NPC + t - NBLK + 1)
                if back1:
                    act.wait_ge(gu_mm, t)
                    act.activation(sg_r[:, b, :], bank[b][:, 0:H], ACT.Silu, scale=1.0 / WSCALE).then_inc(silu_d, 1)
                if now:
                    act.wait_ge(xg_tr, t + 1)
                    act.activation(xgT[:, j, 0:D], bank[2].bitcast(F16)[:, 0:D], ACT.Copy).then_inc(xgT_hi, 1)
                if back1:
                    act.wait_ge(hd_done, t)
                    act.activation(h_hl[:, b, 0:H], sg_r[:, b, :], ACT.Copy).then_inc(hr_hi, 1)
                if back2:
                    act.wait_ge(dn_mm, t - 1)
                    if not isinstance(t, int) or t >= 4:
                        act.wait_ge(y_stored[j], slot_count(t - 2))
                    act.activation(y_out[:, j, :], bank[4 + j], ACT.Copy).then_inc(y_ready, 1)

            split_high(NPC)
            act.wait_ge(edif_done, 1)
            act.activation(e_pair, e_pair, ACT.Exp).then_inc(eexp_done, 1)
            shared(0)
            act.sem_inc(y_ready, 2)
            pipelined(act, routed, NBLK, first=1)
            for j in range(2):
                act.wait_ge(y_stored[j], (NBLK + 1 - j) // 2 * 16)
            shared(1)

        @block.tensor
        def _(pe):
            pe.wait_ge(consts_ready, 9)
            pe.wait_ge(geo_done, 1)
            pe.matmul(bank[0][:, 0:1], geo_row, ones_row[:, 0:1], start=True, stop=True).then_inc(wcol_mm, 1)
            pe.wait_ge(wcol_done, 1)
            for t in range(T):
                if t % (T // 4) == 0:
                    pe.wait_ge(ctx_landed[t // (T // 4)], 16)
                last = pe.matmul(bank[1][0:T, :], wcols[:, t, :], ctx_sb[:, t, :], start=(t == 0), stop=(t == T - 1))
            last.then_inc(chain_mm, 1)
            pe.wait_ge(chain_done, 1)
            for c in range(DC):
                last = pe.transpose(bank[0][:, 64 + c * T:64 + (c + 1) * T], cbar[:, c * P:(c + 1) * P], ident[0:T, 0:T])
            last.then_inc(chain_mm, 1)
            pe.wait_ge(chain_done, 2)
            pe.wait_ge(win_landed, 16)
            for c in range(DC):
                pe.matmul(bank[1][0:T, :], cbarT[:, c * T:(c + 1) * T], w_in_sb[:, c, :], start=(c == 0), stop=False)
            pe.matmul(bank[1][0:T, :], wsum16_row, b_in_row, start=False, stop=True).then_inc(chain_mm, 1)
            pe.wait_ge(chain_done, 3)
            for c in range(DC):
                last = pe.transpose(bank[0][:, 128 + c * T:128 + (c + 1) * T], y1[:, c * P:(c + 1) * P], ident[0:T, 0:T])
            last.then_inc(chain_mm, 1)
            pe.wait_ge(chain_done, 4)
            pe.wait_ge(wout_landed, 16)
            for c in range(DC):
                pe.matmul(bank[1][0:T, :], y1T[:, c * T:(c + 1) * T], w_out_sb[:, c, :], start=(c == 0), stop=False)
            pe.matmul(bank[1][0:T, :], ones_row[:, 0:T], b_out_row, start=False, stop=True).then_inc(chain_mm, 1)
            pe.wait_ge(chain_done, 6)
            for t in range(T):
                if t >= 2:
                    pe.wait_ge(bcast_used, t - 1)
                pe.matmul(bank[2 + t % 2], pick[:, t:t + 1].to_broadcast([96, P]), sum_parts,
                          start=True, stop=True).then_inc(bcast_mm, 1)
            for m in range(3):
                pe.wait_ge(abs_done, 4 * m + 4)
                if m == 2:
                    pe.wait_ge(wscale_done, 1)
                pe.matmul(bank[m % 2][:, 256 + 4 * m:260 + 4 * m], ones, abs_part[:, 4 * m:4 * m + 4],
                          start=True, stop=True).then_inc(abs_mm, 1)

            def turn_xq(t, j):
                pe.wait_ge(xq_done, t + 1)
                if not isinstance(t, int):
                    pe.wait_ge(xqT_done, t - 1)
                for c in range(DC):
                    last = pe.transpose(bank[2 + j].bitcast(BF16)[:, c * P:(c + 1) * P],
                                        xq[:, j, c * P:(c + 1) * P], ident_h[:])
                last.then_inc(xq_tr, 1)

            by_pairs(pe, turn_xq, T)

            def ffn(t, j, now, back1, back2):
                def gate_up(c):
                    if not now:
                        return
                    pe.wait_ge(h_done, t * NCH + c + 1)
                    for m, w, done in ((0, wq_gate, gate_mm), (2, wq_up, up_mm)):
                        for k in range(DC):
                            last = pe.matmul(bank[m + c % 2], xqT[:, k, bass.ds(t * P, P)],
                                             w[:, k, c * CH:(c + 1) * CH], start=(k == 0), stop=(k == DC - 1))
                        last.then_inc(done, 1)

                if now and isinstance(t, int) and t == 0:
                    pe.wait_ge(xqT_done, T)
                    pe.wait_ge(wscale_done, 3)
                    pe.wait_ge(wq_done, 2)
                gate_up(0)
                gate_up(1)
                if back2:
                    pe.wait_ge(hq_done, t + 1)
                    for half, sem_h in ((0, hqT_a), (1, hqT_b)):
                        for c in range(IC // 2):
                            k = half * IC // 2 + c
                            last = pe.transpose(bank[4 + half].bitcast(BF16)[:, c * P:(c + 1) * P],
                                                hq[:, k * P:(k + 1) * P], ident_h[:])
                        last.then_inc(hq_tr, 1)
                gate_up(2)
                if back2:
                    if isinstance(t, int) and t == 2 or not isinstance(t, int):
                        pe.wait_ge(wq_done, 6)
                    pe.wait_ge(hqT_a, t - 1)
                    pe.wait_ge(hqT_b, t - 1)
                    for k in range(IC):
                        last = pe.matmul(bank[6 + j], hqT[:, k, :], wq_down[:, k, :],
                                         start=(k == 0), stop=(k == IC - 1))
                    last.then_inc(down_mm, 1)
                gate_up(3)

            pipelined(pe, ffn, T)

            pe.wait_ge(rt_done, 2)
            pe.wait_ge(ctx2_landed, 16)
            pe.wait_ge(ctxT_landed[0], 16 * DC)

            def attend(n, j, on):
                b = 1 - j
                if on(1):
                    pe.wait_ge(xh_done, n)
                    for c in range(DC):
                        last = pe.transpose(bank[7 * b][:, c * P:(c + 1) * P], xh[:, b, c * P:(c + 1) * P], ident[:])
                    last.then_inc(xh_tr, 1)
                if on(2):
                    pe.wait_ge(prob_done, n - 1)
                    pe.transpose(bank[2][:, 0:P], prob[:, j, :], ident[:]).then_inc(prob_tr, 1)
                if on(4):
                    pe.wait_ge(xhl_done, n - 3)
                    for c in range(2 * DC):
                        last = pe.transpose(bank[5].bitcast(F16)[:, c * P:(c + 1) * P],
                                            xhl[:, j, c * P:(c + 1) * P], ident16[:])
                    last.then_inc(xn_tr, 1)
                if on(1):
                    if isinstance(n, int) and n == T // 4 + 1:
                        for q in range(1, 4):
                            pe.wait_ge(ctxT_landed[q], 16 * DC)
                    pe.wait_ge(xhT_done, n)
                    for c in range(DC):
                        last = pe.matmul(bank[1][:, 0:P], xhT[:, b, c * P:(c + 1) * P],
                                         reg_b[:, bass.ds(ctxT_at(n - 1) + c * P, P)],
                                         start=(c == 0), stop=(c == DC - 1))
                    last.then_inc(score_mm, 1)
                if on(5):
                    pe.wait_ge(xnT_done, n - 4)
                    if not isinstance(n, int) or n > 5:
                        pe.wait_ge(logit_done, n * 2 - 10)
                    i = 0
                    for part, ww in ((0, rt_hi), (0, rt_lo), (1, rt_hi)):
                        for c in range(DC):
                            last = pe.matmul(bank[6][:, 0:NE + 1], xnT[:, part * DC + c, bass.ds((n - 5) * P, P)],
                                             ww[:, c, :], start=(i == 0), stop=(i == 3 * DC - 1))
                            i += 1
                    last.then_inc(logit_mm, 1)
                if on(2):
                    pe.wait_ge(probT_done, n - 1)
                    pe.matmul(bank[3 + j], probT[:, j, :], ctx_sb[:, bass.ds(n - 2, 1), :]
                              .rearrange("p a d -> p (a d)"), start=True, stop=True).then_inc(read_mm, 1)

            staged(pe, attend, T, 5, first=1)
            def rank():
                pe.wait_ge(hot_done, 1)
                pe.matmul(bank[6][:, 0:TE], lower_h, routed_h, start=True, stop=True)
                pe.matmul(bank[7][:, 0:TE], ones_h, routed_h, start=True, stop=True).then_inc(rank_mm, 1)

            def shared_down(v, g, dn):
                done = (v * NG + g) * HC
                for c in range(HC):
                    pe.wait_ge(s_hi, done + c + 1)
                    pe.wait_ge(s_lo, done + c + 1)
                    for k in range(GT):
                        n = (v * NG + g) * GT + k
                        if c == 0 and n == 0:
                            pe.wait_ge(rank_read, 1)
                        if c == 0 and n >= GT:
                            pe.wait_ge(acc_done, n - GT + 1)
                        for i, (part, ww) in enumerate(((0, 0), (0, 1), (1, 0))):
                            last = pe.matmul(bank[4 + k], hT_s[g % 2][:, part, c, k * P:(k + 1) * P], dn[ww][:, c, :],
                                             start=(c == 0 and i == 0), stop=(c == HC - 1 and i == 2))
                        if c == HC - 1:
                            last.then_inc(s_down_mm, 1)

            def shared(v):
                gu, dn = weights_of(0)
                wait_low(pe, NPC if v == 0 else (NE + 2) * NPC)
                for g in range(NG):
                    for c in range(HC):
                        m = (v * NG + g) * HC + c
                        if m >= 2:
                            pe.wait_ge(s_hid, m - 1)
                        for x_or_y, at, done in ((0, 0, s_gate_mm), (2, H, s_up_mm)):
                            i = 0
                            for part, ww in ((0, 0), (0, 1), (1, 0)):
                                for k in range(DC):
                                    last = pe.matmul(bank[x_or_y + m % 2],
                                                     gu[ww][:, k, at + c * P:at + (c + 1) * P],
                                                     xnT[:, part * DC + k, g * CH:(g + 1) * CH],
                                                     start=(i == 0), stop=(i == 3 * DC - 1))
                                    i += 1
                            last.then_inc(done, 1)
                        if m == 1:
                            rank()
                        if c == 0 and g:
                            shared_down(v, g - 1, dn)
                shared_down(v, NG - 1, dn)

            def weights_of(e):
                w = w_all[:, e, :] if isinstance(e, int) else w_all[:, bass.ds(e, 1), :].rearrange("p a w -> p (a w)")
                gu = [w[:, p * RAW:p * RAW + DC * 2 * H].rearrange("p (c i) -> p c i", c=DC) for p in range(2)]
                dn = [w[:, p * RAW + DC * 2 * H:(p + 1) * RAW].rearrange("p (c o) -> p c o", c=HC) for p in range(2)]
                return gu, dn

            def routed(t, j, now, back1, back2):
                b = 1 - j
                if isinstance(t, int) and t == 1:
                    wait_low(pe, (NE + 1) * NPC)
                    pe.wait_ge(experts_known, 1)
                    alone(pe)
                if back1:
                    gu, _ = weights_of(pe.value_load(expert_of[0:1, bass.ds(t - 1, 1)], min_val=1, max_val=NE))
                if back2:
                    _, dn = weights_of(pe.value_load(expert_of[0:1, bass.ds(t - 2, 1)], min_val=1, max_val=NE))
                if back1:
                    pe.wait_ge(xgT_hi, t)
                    if not isinstance(t, int) or t >= 3:
                        pe.wait_ge(hd_done, t - 2)
                    n = 0
                    for part, ww in ((0, 0), (0, 1), (1, 0)):
                        if part == 1:
                            pe.wait_ge(xgT_lo, t)
                        for c in range(DC):
                            at = (part * DC + c) * P
                            last = pe.matmul(bank[b], xgT[:, b, at:at + P], gu[ww][:, c, :],
                                             start=(n == 0), stop=(n == 3 * DC - 1))
                            n += 1
                        if n == DC and back2:
                            turn_hidden(t, j)
                    last.then_inc(gu_mm, 1)
                elif back2:
                    turn_hidden(t, j)
                if now:
                    pe.wait_ge(xg_landed[j], slot_count(t) + 16)
                    if not isinstance(t, int) or t >= 1:
                        pe.wait_ge(xgT_lo, t)
                        pe.wait_ge(xgT_hi, t)
                    for c in range(2 * DC):
                        last = pe.transpose(bank[2 + c // DC].bitcast(F16)[:, c % DC * P:(c % DC + 1) * P],
                                            xg[:, j, c * P:(c + 1) * P], ident16[:])
                    last.then_inc(xg_tr, 1)
                if back2:
                    pe.wait_ge(hT_done, t - 1)
                    pe.wait_ge(y_ready, t - 1)
                    n = 0
                    for part, ww in ((0, 0), (0, 1), (1, 0)):
                        for c in range(HC):
                            at = (part * HC + c) * P
                            last = pe.matmul(bank[4 + j], hT_r[:].bitcast(F16)[:, j, at:at + P], dn[ww][:, c, :],
                                             start=(n == 0), stop=(n == 3 * HC - 1))
                            n += 1
                    last.then_inc(dn_mm, 1)

            def turn_hidden(t, j):
                pe.wait_ge(hr_hi, t - 1)
                pe.wait_ge(hr_lo, t - 1)
                for c in range(2 * HC):
                    last = pe.transpose(bank[6 + j].bitcast(F16)[:, c * P:(c + 1) * P],
                                        h_hl[:, j, c * P:(c + 1) * P], ident16[:])
                last.then_inc(hd_tr, 1)

            pe.wait_ge(xnT_done, T)
            shared(0)

            pipelined(pe, routed, NBLK)
            shared(1)

        @block.vector
        def _(dve):
            dve.sem_inc(h_done, 2)
            dve.sem_inc(hq_done, 2)

            dve.wait_ge(consts_ready, 9)
            dve.wait_ge(keep_done, 1)
            dve.tensor_scalar(keep_row, keep_row, 0.5, 0.5, ALU.mult, ALU.add).then_inc(dve_a, 1)
            dve.wait_ge(dve_a, 1)
            dve.tensor_tensor_scan(geo_row[:, ::-1], keep_row.to_broadcast([1, S]), ones_row, 0.0,
                                   ALU.mult, ALU.add).then_inc(geo_done, 1)
            dve.wait_ge(geo_done, 1)
            dve.reduce_sum(wsum_row, geo_row, AX.X).then_inc(dve_a, 1)
            dve.wait_ge(dve_a, 2)
            dve.tensor_scalar(wsum16_row, ones_row[:, 0:T], wsum_row, 1.0 / S, ALU.mult, ALU.mult).then_inc(dve_a, 1)
            dve.wait_ge(wcol_mm, 1)
            dve.wait_ge(cols_cleared, 1)
            dve.tensor_scalar(extra[:, 0:T * T:T + 1], bank[0][:, 0:1].to_broadcast([P, T]), 1.0 / S, None, ALU.mult)\
               .then_inc(wcol_done, 1)
            dve.wait_ge(chain_mm, 1)
            dve.tensor_copy(cbar, bank[1][0:T, :]).then_inc(chain_done, 1)
            dve.wait_ge(chain_mm, 2)
            dve.tensor_copy(cbarT, bank[0][:, 64:64 + DC * T]).then_inc(chain_done, 1)
            count = [3]

            def step(ins, times=1):
                ins.then_inc(dve_a, 1)
                count[0] += times

            def settle():
                dve.wait_ge(dve_a, count[0])

            def stats_of(buf, h):
                with dve.Fori(h * HT // 4, (h + 1) * HT // 4) as i:
                    for t in (i * 4, i * 4 + 1, i * 4 + 2, i * 4 + 3):
                        ins = dve.bn_stats(stats[:, bass.ds(t, 1), :].rearrange("p a d -> p (a d)"), tile(buf, t))
                        ins.then_inc(dve_a, 1)
                count[0] += HT
                settle()
                r = slice(h * HT, (h + 1) * HT)
                step(dve.tensor_tensor(mean2[:, r], stats[:, r, 1], stats[:, r, 4], ALU.add))
                step(dve.tensor_tensor(tmp16[:, r], stats[:, r, 1], stats[:, r, 4], ALU.subtract))
                step(dve.tensor_tensor(vpe[:, r], stats[:, r, 2], stats[:, r, 5], ALU.add))
                settle()
                step(dve.scalar_tensor_tensor(tmp16[:, r], tmp16[:, r], 0.25, tmp16[:, r], ALU.mult, ALU.mult))
                step(dve.tensor_scalar(vpe[:, r], vpe[:, r], 1.0 / D, LN_EPS, ALU.mult, ALU.add))
                step(dve.tensor_scalar(neg_mean[:, r], mean2[:, r], -0.5, None, ALU.mult))
                settle()
                dve.tensor_tensor(vpe[:, r], vpe[:, r], tmp16[:, r], ALU.add).then_inc(var_ready, 1)

            def add_summary(h):
                with dve.Fori(h * HT // 4, (h + 1) * HT // 4) as i:
                    for t, j in ((i * 4, 0), (i * 4 + 1, 1), (i * 4 + 2, 0), (i * 4 + 3, 1)):
                        dve.wait_ge(y0_done, t + 1)
                        dve.wait_ge(bcast_mm, t + 1)
                        dve.tensor_tensor(tile(y_buf, t), tile(y_buf, t), bank[2 + j], ALU.add).then_inc(bcast_used, 1)
                dve.wait_ge(bcast_used, (h + 1) * HT)

            def add_norm(h):
                with dve.Fori(h * HT // 4, (h + 1) * HT // 4) as i:
                    for t in (i * 4, i * 4 + 1, i * 4 + 2, i * 4 + 3):
                        dve.wait_ge(xb_done, t + 1)
                        dve.wait_ge(zg_done, t + 1)
                        ins = dve.tensor_tensor(tile(x_sb, t), tile(y_buf, t), tile(x_sb, t), ALU.add)
                        ins.then_inc(dve_a, 1)
                count[0] += HT
                settle()

            def norm_and_largest(h):
                r = slice(h * HT, (h + 1) * HT)
                dve.wait_ge(rstd_ready, 4 + h + 1)
                with dve.Fori(h * HT // 4, (h + 1) * HT // 4) as i:
                    for t in (i * 4, i * 4 + 1, i * 4 + 2, i * 4 + 3):
                        dve.tensor_scalar(tile(y_buf, t), tile(x_sb, t), neg_mean[:, bass.ds(t, 1)], rstd[:, bass.ds(t, 1)],
                                          ALU.add, ALU.mult).then_inc(dve_a, 1)
                count[0] += HT
                settle()
                with dve.Fori(h * HT // 4, (h + 1) * HT // 4) as i:
                    for t in (i * 4, i * 4 + 1, i * 4 + 2, i * 4 + 3):
                        dve.tensor_reduce(amax[:, bass.ds(t, 1)], tile(y_buf, t), AX.X, ALU.max,
                                          apply_absolute_value=True).then_inc(dve_a, 1)
                count[0] += HT
                settle()
                step(dve.tensor_scalar(amax[:, r], amax[:, r], QUANT_EPS, None, ALU.max))
                settle()
                step(dve.reciprocal(s_x[:, r], amax[:, r]))
                settle()
                dve.tensor_scalar(s_x[:, r], s_x[:, r], QMAX, None, ALU.mult).then_inc(quant_ready, 1)

            def weight_scale(m):
                dve.wait_ge(abs_mm, m + 1)
                step(dve.reduce_sum(wabs[:, m:m + 1], bank[m % 2][:, 256 + 4 * m:260 + 4 * m], AX.X))
                settle()
                step(dve.tensor_scalar(wmean[:, m:m + 1], wabs[:, m:m + 1], 1.0 / (I * D), QUANT_EPS, ALU.mult, ALU.max))
                settle()
                dve.reciprocal(wscale[:, m:m + 1], wmean[:, m:m + 1]).then_inc(wscale_done, 1)

            def hold(m):
                dve.wait_ge(whole_done, 4 * m + 4)
                for c in range(4):
                    last = dve.tensor_scalar(wq[:, (4 * m + c) * 4 * CH:(4 * m + c + 1) * 4 * CH],
                                             whole[m][:, c * 4 * CH:(c + 1) * 4 * CH], 1.0, -1.0, ALU.min, ALU.max)
                last.then_inc(wq_done, 1)

            def store_xq(h):
                with dve.Fori(h * HT // 4, (h + 1) * HT // 4) as i:
                    for t, j in ((i * 4, 0), (i * 4 + 1, 1), (i * 4 + 2, 0), (i * 4 + 3, 1)):
                        if h == 0:
                            dve.wait_ge(xs_done, t + 1)
                        dve.wait_ge(xq_tr, t + 1)
                        dve.tensor_scalar(xq[:, j, :], tile(y_buf, t), MAGIC, None, ALU.subtract).then_inc(xq_done, 1)

            dve.sem_inc(xq_tr, 2)
            dve.wait_ge(x_landed[0], 16)
            stats_of(x_sb, 0)
            dve.wait_ge(chain_mm, 3)
            dve.tensor_copy(y1, bank[1][0:T, :]).then_inc(chain_done, 1)
            dve.wait_ge(chain_mm, 4)
            dve.tensor_copy(y1T, bank[0][:, 128:128 + DC * T]).then_inc(chain_done, 1)
            dve.wait_ge(x_landed[1], 16)
            stats_of(x_sb, 1)
            dve.wait_ge(chain_mm, 3)
            step(dve.memset(sum_parts, 0.0))
            step(dve.tensor_tensor(pick, ident_h[0:96, 0:T], ident_h[0:96, 32:32 + T], ALU.add))
            settle()
            step(dve.tensor_tensor(pick, pick, ident_h[0:96, 64:64 + T], ALU.add))
            dve.wait_ge(chain_mm, 5)
            step(dve.tensor_copy(sum_f, bank[1][0:T, :]))
            settle()
            step(dve.tensor_copy(sum_parts[0:T], sum_f))
            settle()
            step(dve.tensor_tensor(sum_rest, sum_f, sum_parts[0:T], ALU.subtract))
            settle()
            step(dve.tensor_copy(sum_mid, sum_rest))
            settle()
            dve.tensor_copy(sum_parts[32:32 + T], sum_mid).then_inc(chain_done, 1)
            dve.tensor_tensor(sum_parts[64:64 + T], sum_rest, sum_mid, ALU.subtract).then_inc(chain_done, 1)
            for h in range(2):
                add_summary(h)
                stats_of(y_buf, h)
            weight_scale(0)
            weight_scale(1)
            for h in range(2):
                add_norm(h)
                stats_of(x_sb, h)
            norm_and_largest(0)
            weight_scale(2)
            norm_and_largest(1)
            step(dve.tensor_scalar(dq_gate, amax, wmean[:, 0:1], 1.0 / QMAX, ALU.mult, ALU.mult))
            step(dve.tensor_scalar(dq_up, amax, wmean[:, 1:2], 1.0 / QMAX, ALU.mult, ALU.mult))
            hold(0)
            dve.wait_ge(quant_ready, 2)
            with dve.Fori(HT // 4, 2 * HT // 4) as i:
                for t in (i * 4, i * 4 + 1, i * 4 + 2, i * 4 + 3):
                    dve.tensor_scalar(tile(y_buf, t), tile(y_buf, t), s_x[:, bass.ds(t, 1)], MAGIC,
                                      ALU.mult, ALU.add).then_inc(dve_a, 1)
            count[0] += HT
            store_xq(0)
            settle()
            store_xq(1)
            dve.wait_ge(xq_done, T)
            hold(1)
            dve.wait_ge(wq_done, 2)

            def ffn(t, j, now, back1, back2):
                def hidden(c):
                    if now:
                        dve.wait_ge(up_mm, t * NCH + c + 1)
                        dve.wait_ge(silu_done, t * NCH + c + 1)
                        dve.scalar_tensor_tensor(h_buf[:, j, c * CH:(c + 1) * CH], bank[2 + c % 2],
                                                 dq_up[:, bass.ds(t, 1)], sg_buf[:, c % 2, :],
                                                 ALU.mult, ALU.mult).then_inc(h_done, 1)

                def down_weights(c):
                    if isinstance(t, int) and t == 0:
                        if c == 0:
                            step(dve.tensor_scalar(wmean[:, 0:1], wmean[:, 2:3], 1.0 / QMAX, None, ALU.mult))
                        dve.wait_ge(shifted, 4 * 2 + c + 1)
                        v = raw_piece(2, c)
                        step(dve.tensor_scalar(v, v, MAGIC + 1.0, MAGIC - 1.0, ALU.min, ALU.max))
                        settle()
                        dve.tensor_scalar(wq[:, (4 * 2 + c) * 4 * CH:(4 * 2 + c + 1) * 4 * CH], v,
                                          MAGIC, None, ALU.subtract).then_inc(wq_done, 1)

                b = 1 - j
                hidden(0)
                down_weights(0)
                hidden(1)
                down_weights(1)
                if back2:
                    dve.wait_ge(hq_tr, (t - 2) * 2 + 2)
                    dve.tensor_copy(hqT[:, IC // 2:, :], bank[5].bitcast(BF16).rearrange("p (c n) -> p c n", n=P))\
                       .then_inc(hqT_b, 1)
                    if isinstance(t, int) and t == T + 1:
                        attend(0, 0, lambda k: k == 0)
                if back1:
                    k = (t - 1) * 4
                    dve.wait_ge(hl_done, t * NCH)
                    dve.tensor_reduce(hmax[:, b:b + 1], hl_buf[:, b, :], AX.X, ALU.max,
                                      apply_absolute_value=True).then_inc(dve_b, 1)
                    dve.wait_ge(rinv_done, t)
                    dve.wait_ge(dve_b, k + 1)
                    dve.tensor_scalar(rlim[:, b:b + 1], hmax[:, b:b + 1], rinv[:, b:b + 1], QUANT_EPS,
                                      ALU.mult, ALU.max).then_inc(dve_b, 1)
                    dve.wait_ge(dve_b, k + 2)
                    dve.reciprocal(rrec[:, b:b + 1], rlim[:, b:b + 1]).then_inc(dve_b, 1)
                    dve.wait_ge(dve_b, k + 3)
                    dve.tensor_scalar(s_h[:, b:b + 1], rrec[:, b:b + 1], rinv[:, b:b + 1], QMAX,
                                      ALU.mult, ALU.mult).then_inc(s_h_done, 1)
                    dve.tensor_scalar(dq_h[:, b:b + 1], rlim[:, b:b + 1], wmean[:, 0:1], None,
                                      ALU.mult).then_inc(dve_b, 1)
                hidden(2)
                down_weights(2)
                hidden(3)
                down_weights(3)
                if back1:
                    dve.wait_ge(hs_done, t)
                    dve.tensor_scalar(hq, hl_buf[:, b, :], MAGIC, None, ALU.subtract).then_inc(hq_done, 1)
                if back2:
                    dve.wait_ge(down_mm, t - 1)
                    dve.scalar_tensor_tensor(tile(x_sb, t - 2), bank[6 + j], dq_h[:, j:j + 1], tile(x_sb, t - 2),
                                             ALU.mult, ALU.add).then_inc(x2_done, 1)


            def start_stats(todo):
                for t, st, mv, ve, chain, k, out_sem in todo:
                    alone(dve)
                    dve.bn_stats(st, tile(x_sb, t)).then_inc(chain, 1)

            def join_stats(todo):
                for t, st, mv, ve, chain, k, out_sem in todo:
                    dve.wait_ge(chain, k + 1)
                    alone(dve)
                    dve.bn_aggr(mv, st).then_inc(chain, 1)

            def end_stats(todo):
                for t, st, mv, ve, chain, k, out_sem in todo:
                    dve.wait_ge(chain, k + 2)
                    dve.tensor_scalar(ve, mv[:, 1:2], LN_EPS, None, ALU.add).then_inc(out_sem, 1)

            def split_low(n):
                dve.wait_ge(w_hi_done, n + 1)
                dve.scalar_tensor_tensor(piece_of(n, 1), raw_piece_of(n), WSCALE, piece_of(n, 0),
                                         ALU.mult, ALU.subtract).then_inc(w_lo_done, 1)

            def attend(n, j, on):
                b = 1 - j
                first, second_norm = [], []
                if on(0):
                    first = [(n, st1[:, j, :], mv[:, j, :], ve1[:, j:j + 1], dve_c, n * 2, ve_done)]
                if on(3):
                    second_norm = [(n - 3, st2[:, b, :], mv2[:, b, :], ve2[:, b:b + 1], dve_d, (n - 3) * 2, vd_done)]
                start_stats(first)
                if on(2):
                    dve.wait_ge(prob_done, n - 1)
                    dve.reciprocal(rv[:, j:j + 1], rsum[:, j:j + 1]).then_inc(rv_done, 1)
                if on(3):
                    dve.wait_ge(x3_done, n - 2)
                    start_stats(second_norm)
                if isinstance(n, int) and n == 0:
                    dve.wait_ge(mask_landed, 16)
                    dve.tensor_reduce(valid, mask_sb.rearrange("p (t m) -> p t m", t=T), AX.X, ALU.max)\
                       .then_inc(mask_done, 1)
                    dve.tensor_scalar(negb.rearrange("p t m -> p (t m)"), mask_sb, -1.0, -MASKED, ALU.add, ALU.mult)\
                       .then_inc(mask_done, 1)
                    dve.wait_ge(rt_done, 1)
                    dve.scalar_tensor_tensor(rt_lo, rt_raw, WSCALE, rt_hi, ALU.mult, ALU.subtract).then_inc(rt_done, 1)
                    dve.wait_ge(mask_done, 2)
                join_stats(first + second_norm)
                if on(2):
                    dve.wait_ge(rv_done, n * 2 - 3)
                    dve.tensor_tensor(rv2[:, j:j + 1], rv[:, j:j + 1], valid[:, bass.ds(n - 2, 1)], ALU.mult)\
                       .then_inc(rv_done, 1)
                end_stats(first + second_norm)
                if on(1):
                    dve.wait_ge(score_mm, n)
                    dve.scalar_tensor_tensor(smx[:, b, :], bank[1][:, 0:P], ATT_SCALE, tile(negb, n - 1),
                                             ALU.mult, ALU.add).then_inc(smx_done, 1)
                if on(1):
                    dve.wait_ge(smx_done, n)
                    dve.tensor_reduce(nmax[:, b:b + 1], smx[:, b, :], AX.X, ALU.max, negate=True)\
                       .then_inc(nmax_done, 1)
                if on(3):
                    dve.wait_ge(rd_done, n - 2)
                    dve.tensor_scalar(xn[:, b, :], tile(x_sb, n - 3), mv2[:, b, 0:1], rs2[:, b:b + 1],
                                      ALU.subtract, ALU.mult).then_inc(xn_done, 1)
                if on(0):
                    dve.wait_ge(rs_done, n + 1)
                    dve.tensor_scalar(xh[:, j, :], tile(x_sb, n), mv[:, j, 0:1], rs1[:, j:j + 1],
                                      ALU.subtract, ALU.mult).then_inc(xh_done, 1)
                if on(5):
                    dve.wait_ge(logit_mm, n - 4)
                    dve.tensor_scalar(tile(logit, n - 5), bank[6][:, 0:NE], 1.0 / WSCALE, None, ALU.mult)\
                       .then_inc(logit_done, 1)
                    dve.tensor_scalar(e_pair[:, 1, bass.ds(n - 5, 1)], bank[6][:, NE:NE + 1], -1.0 / WSCALE,
                                      None, ALU.mult).then_inc(logit_done, 1)
                if on(2):
                    dve.wait_ge(rv_done, n * 2 - 2)
                    dve.wait_ge(read_mm, n - 1)
                    dve.scalar_tensor_tensor(tile(x_sb, n - 2), bank[3 + j], rv2[:, j:j + 1], tile(x_sb, n - 2),
                                             ALU.mult, ALU.add).then_inc(x3_done, 1)

            pipelined(dve, ffn, T)
            dve.wait_ge(x2_done, T)
            staged(dve, attend, T, 5, first=1)

            n = 2 * T
            dve.wait_ge(logit_done, 2 * T)
            dve.wait_ge(iota_done, 1)

            def wide(v):
                return v.unsqueeze(2).to_broadcast([P, T, NE])

            def step(ins):
                ins.then_inc(dve_d, 1)

            for a, (src, m, least, hot) in enumerate(((logit, m1, least1, first), (scr, m2, least2, second))):
                step(dve.tensor_reduce(m, src, AX.X, ALU.max))
                dve.wait_ge(dve_d, n + 1)
                step(dve.tensor_tensor(cand, src, wide(m), ALU.is_ge))
                dve.wait_ge(dve_d, n + 2)
                step(dve.scalar_tensor_tensor(cand, cand, -2.0 * NE, iota8, ALU.mult, ALU.add))
                dve.wait_ge(dve_d, n + 3)
                step(dve.tensor_reduce(least, cand, AX.X, ALU.min))
                dve.wait_ge(dve_d, n + 4)
                step(dve.tensor_tensor(hot, cand, wide(least), ALU.is_equal))
                dve.wait_ge(dve_d, n + 5)
                n += 5
                if a == 0:
                    step(dve.scalar_tensor_tensor(scr, first, MASKED, logit, ALU.mult, ALU.add))
                    dve.wait_ge(dve_d, n + 1)
                    n += 1
            dve.tensor_tensor(e_pair[:, 0, :], m2, m1, ALU.subtract).then_inc(edif_done, 1)
            dve.wait_ge(eexp_done, 1)
            step(dve.tensor_scalar(w1, e_pair[:, 0, :], 1.0, None, ALU.add))
            step(dve.tensor_scalar(w2, e_pair[:, 1, :], 1.0, None, ALU.add))
            dve.wait_ge(dve_d, n + 2)
            step(dve.reciprocal(w1, w1))
            step(dve.reciprocal(w2, w2))
            dve.wait_ge(dve_d, n + 4)
            step(dve.tensor_scalar(w1, w1, 1.0 / WSCALE, None, ALU.mult))
            step(dve.tensor_scalar(sgate, w2, 1.0 / WSCALE, None, ALU.mult))
            dve.wait_ge(dve_d, n + 6)
            step(dve.tensor_tensor(w2, e_pair[:, 0, :], w1, ALU.mult))
            dve.tensor_tensor(routed_h.rearrange("p (e t) -> p t e", e=NE), first, second, ALU.add).then_inc(hot_done, 1)
            step(dve.memset(carry.rearrange("p t e -> p (t e)"), 1.0))
            n += 8
            dve.wait_ge(dve_d, n)
            carry_v = carry.rearrange("p t e -> p (t e)").rearrange("p (e t) -> p e t", e=NE)
            step(dve.memset(carry_v[:, :, 0:1], 0.0))

            def split_pieces(m, part):
                for n in splits_beside(m, part):
                    if n >= EARLY:
                        split_low(n)

            def shared_hidden(v, m):
                g, c = m // HC % NG, m % HC
                dve.wait_ge(s_up_mm, m + 1)
                dve.wait_ge(s_silu, m + 1)
                dve.scalar_tensor_tensor(sg_s[:, m % 2, :], bank[2 + m % 2], 1.0 / WSCALE, sg_s[:, m % 2, :],
                                         ALU.mult, ALU.mult).then_inc(s_hid, 1)
                if v == 0 and 2 <= m:
                    split_pieces(m, 0)
                dve.wait_ge(s_hi, m + 1)
                dve.tensor_tensor(hT_s[g % 2][:, 1, c, :], sg_s[:, m % 2, :], hT_s[g % 2][:, 0, c, :],
                                  ALU.subtract).then_inc(s_lo, 1)

            shared_hidden(0, 0)
            shared_hidden(0, 1)
            dve.wait_ge(rank_mm, 1)
            flat = lambda v: v.rearrange("p t e -> p (t e)")
            step(dve.tensor_copy(flat(cand), bank[7][:, 0:TE]))
            dve.tensor_copy(flat(iota8), bank[6][:, 0:TE]).then_inc(rank_read, 1)
            dve.wait_ge(dve_d, n + 2)
            step(dve.tensor_tensor_scan(flat(scr), flat(carry), flat(cand), 0.0, ALU.mult, ALU.add))
            dve.wait_ge(dve_d, n + 3)
            n += 3
            total = flat(scr).rearrange("p (e t) -> p e t", e=NE)[:, :, T - 1:T].rearrange("p e t -> p (e t)")
            step(dve.tensor_scalar(blocks, total, 1.0 / P, 0.5 - 0.5 / P, ALU.mult, ALU.add))
            step(dve.tensor_tensor(flat(before), flat(scr), flat(cand), ALU.subtract))
            dve.wait_ge(dve_d, n + 2)
            step(dve.tensor_scalar(blocks, blocks, MAGIC, None, ALU.add))
            dve.wait_ge(rank_read, 1)
            step(dve.tensor_tensor(flat(before), flat(before), flat(iota8), ALU.add))
            dve.wait_ge(dve_d, n + 4)
            step(dve.tensor_scalar(blocks, blocks, MAGIC, None, ALU.subtract))
            dve.wait_ge(dve_d, n + 5)
            step(dve.tensor_tensor_scan(ends, ones8, blocks, 0.0, ALU.mult, ALU.add))
            dve.wait_ge(dve_d, n + 6)
            step(dve.tensor_tensor(begins, ends, blocks, ALU.subtract))
            dve.wait_ge(dve_d, n + 7)
            n += 7
            before_v = flat(before).rearrange("p (e t) -> p e t", e=NE)
            step(dve.scalar_tensor_tensor(before_v, begins.unsqueeze(2).to_broadcast([P, NE, T]), float(P), before_v,
                                          ALU.mult, ALU.add))
            dve.wait_ge(dve_d, n + 1)
            before_t = flat(before).rearrange("p (e t) -> p t e", e=NE)
            step(dve.tensor_tensor(first, first, before_t, ALU.mult))
            step(dve.tensor_tensor(second, second, before_t, ALU.mult))
            dve.wait_ge(dve_d, n + 3)
            step(dve.reduce_sum(slot[:, 0, :], first, AX.X))
            step(dve.reduce_sum(slot[:, 1, :], second, AX.X))
            dve.wait_ge(dve_d, n + 5)
            n += 5
            step(dve.tensor_scalar(place, slot, 1.0 / P, 0.5 / P - 0.5, ALU.mult, ALU.add))
            step(dve.tensor_copy(slot_u, slot))
            dve.wait_ge(dve_d, n + 2)
            step(dve.tensor_scalar(place, place, MAGIC, None, ALU.add))
            dve.wait_ge(dve_d, n + 3)
            step(dve.tensor_scalar(place, place, MAGIC, None, ALU.subtract))
            step(dve.tensor_scalar(slot, slot, float(NBLK), None, ALU.mult))
            dve.wait_ge(dve_d, n + 5)
            step(dve.scalar_tensor_tensor(place, place, 1.0 - NBLK * P, slot, ALU.mult, ALU.add))
            dve.wait_ge(dve_d, n + 6)
            dve.tensor_copy(place_u, place).then_inc(place_done, 1)
            n += 6
            step(dve.tensor_tensor(cmp_row, iota_n[0:1, :].unsqueeze(2).to_broadcast([1, NBLK, NE]),
                                   ends[0:1, :].unsqueeze(1).to_broadcast([1, NBLK, NE]), ALU.is_ge))
            dve.wait_ge(dve_d, n + 1)
            step(dve.reduce_sum(expert_f[0:1, :], cmp_row, AX.X))
            dve.wait_ge(dve_d, n + 2)
            dve.tensor_scalar(expert_of[0:1, :], expert_f[0:1, :], float(NE - 1), 1.0, ALU.min, ALU.add).then_inc(experts_known, 1)
            n += 2

            def shared_sum(v, g):
                for k in range(GT):
                    t = g * GT + k
                    m = v * T + t
                    dve.wait_ge(s_down_mm, m + 1)
                    if v:
                        dve.wait_ge(ya_used, 2 * t + 2)
                    dve.scalar_tensor_tensor(x_sb[:, t, :], bank[4 + k], sgate[:, t:t + 1], x_sb[:, t, :],
                                             ALU.mult, ALU.add).then_inc(acc_done, 1)

            def routed_sum(t):
                for a, w in ((0, w1), (1, w2)):
                    i = 2 * t + a
                    dve.wait_ge(ya_landed[i % (2 * NPC)], 16 * (i // (2 * NPC) + 1))
                    if a:
                        dve.wait_ge(ya_used, i)
                    dve.scalar_tensor_tensor(x_sb[:, t, :], ya[:, i % (2 * NPC), :], w[:, t:t + 1], x_sb[:, t, :],
                                             ALU.mult, ALU.add).then_inc(ya_used, 1)

            def shared(v):
                for g in range(NG):
                    for c in range(HC):
                        m = (v * NG + g) * HC + c
                        if v:
                            for t in range(SUMS[m - NG * HC], SUMS[m - NG * HC + 1]):
                                routed_sum(t)
                        if v or m >= 2:
                            shared_hidden(v, m)
                        if v == 0:
                            if m < 2:
                                split_pieces(m, 0)
                            split_pieces(m, 1)
                        if c == 0 and g:
                            shared_sum(v, g - 1)
                if v == 0:
                    routed(0, 0, True, False, False)
                shared_sum(v, NG - 1)

            def routed(t, j, now, back1, back2):
                b = 1 - j
                if isinstance(t, int) and NBLK - 1 <= t < NBLK - 1 + NPC:
                    split_low((NE + 1) * NPC + t - NBLK + 1)
                if back2:
                    dve.wait_ge(hd_tr, t - 1)
                    dve.tensor_copy(hT_r[:].bitcast(F16)[:, j, :], bank[6 + j].bitcast(F16)[:, 0:2 * H])\
                       .then_inc(hT_done, 1)
                if back1:
                    dve.wait_ge(silu_d, t)
                    dve.scalar_tensor_tensor(sg_r[:, b, :], bank[b][:, H:2 * H], 1.0 / WSCALE, sg_r[:, b, :],
                                             ALU.mult, ALU.mult).then_inc(hd_done, 1)
                if now:
                    dve.wait_ge(xg_tr, t + 1)
                    dve.tensor_copy(xgT[:, j, D:2 * D], bank[3].bitcast(F16)[:, 0:D]).then_inc(xgT_lo, 1)
                if back1:
                    dve.wait_ge(hr_hi, t)
                    dve.tensor_tensor(h_hl[:, b, H:2 * H], sg_r[:, b, :], h_hl[:, b, 0:H], ALU.subtract)\
                       .then_inc(hr_lo, 1)

            shared(0)
            pipelined(dve, routed, NBLK, first=1)
            shared(1)


def kernel(x, ctx_2048, mask_BxS2_bk0, L0_xattn_decay, L0_xattn_W_in, L0_xattn_b_in, L0_xattn_W_out, L0_xattn_b_out,
           L0_xattn_gamma, L0_xattn_beta, L0_ffn_w_gate, L0_ffn_w_up, L0_ffn_w_down, L0_ffn_ln_weight, L1_ffn_gate_w,
           L1_ffn_w_gate, L1_ffn_w_up, L1_ffn_w_down, L1_ffn_sh_gate, L1_ffn_sh_up, L1_ffn_sh_down, L1_ffn_se_gate_w):
    import concourse.bacc as bacc
    from concourse.bass_utils import run_bass_kernel_spmd

    def lay(a, *perm):
        a = np.asarray(a)
        return np.ascontiguousarray(a.transpose(perm) if perm else a)

    arrays = {
        "x": lay(x), "ctx": lay(ctx_2048), "ctxT": lay(ctx_2048, 0, 2, 1),
        "mask": lay(mask_BxS2_bk0).reshape(-1), "decay": lay(L0_xattn_decay).reshape(1, 1),
        "w_inT": lay(L0_xattn_W_in, 1, 0), "b_in": lay(L0_xattn_b_in),
        "w_outT": lay(L0_xattn_W_out, 1, 0), "b_out": lay(L0_xattn_b_out),
        "gamma": lay(L0_xattn_gamma), "beta": lay(L0_xattn_beta),
        "f_gateT": lay(L0_ffn_w_gate, 1, 0), "f_upT": lay(L0_ffn_w_up, 1, 0), "f_downT": lay(L0_ffn_w_down, 1, 0),
        "ln_weight": lay(L0_ffn_ln_weight), "routerT": lay(L1_ffn_gate_w, 1, 0),
        "e_gateT": lay(L1_ffn_w_gate, 0, 2, 1), "e_upT": lay(L1_ffn_w_up, 0, 2, 1),
        "e_downT": lay(L1_ffn_w_down, 0, 2, 1),
        "s_gateT": lay(L1_ffn_sh_gate, 1, 0), "s_upT": lay(L1_ffn_sh_up, 1, 0), "s_downT": lay(L1_ffn_sh_down, 1, 0),
        "se_gateT": lay(L1_ffn_se_gate_w, 1, 0),
    }
    nc = bacc.Bacc("TRN2", target_bir_lowering=False, num_devices=1)
    args = [nc.dram_tensor(f"in_{k}", a.shape, mybir.dt.from_np(a.dtype), kind="ExternalInput").ap()
            for k, a in arrays.items()]
    out = nc.dram_tensor("out_x", np.asarray(x).shape, F32, kind="ExternalOutput").ap()
    model_kernel(nc, *args, out)
    r = run_bass_kernel_spmd(nc, [{f"in_{k}": a for k, a in arrays.items()}], core_ids=[0])
    return r.results[0]["out_x"]
```

```python
from contextlib import ExitStack

import numpy as np

import concourse.bass as bass
from concourse import mybir

ALU = mybir.AluOpType
ACT = mybir.ActivationFunctionType
AX = mybir.AxisListType
F32 = mybir.dt.float32
BF16 = mybir.dt.bfloat16
F16 = mybir.dt.float16
U8 = mybir.dt.uint8
U32 = mybir.dt.uint32

P = 128
MAGIC = 1.5 * 2.0 ** 23
LN_EPS = 1e-5
RMS_EPS = 1e-6
QUANT_EPS = 1e-5
QMAX = 127.0
WSCALE = 64.0
MASKED = -1e30


def pipelined(eng, body, tiles, first=0, before_last=None):
    if first == 0:
        body(0, 0, True, False, False)
    body(1, 1, True, True, False)
    with eng.Fori(0, (tiles - 2) // 2) as i:
        for j in range(2):
            body(i * 2 + 2 + j, j, True, True, True)
    if tiles % 2:
        body(tiles - 1, 0, True, True, True)
    body(tiles, tiles % 2, False, True, True)
    if before_last:
        before_last()
    body(tiles + 1, (tiles + 1) % 2, False, False, True)


def staged(eng, body, tiles, depth, first=0, before={}):
    head = depth + depth % 2
    for n in range(first, head):
        body(n, n % 2, lambda k: n - k >= 0)
    starts = [head] + sorted(before)
    for start, end in zip(starts, starts[1:] + [tiles]):
        if start in before:
            before[start]()
        with eng.Fori(0, (end - start) // 2) as i:
            for j in range(2):
                body(i * 2 + (start + j), j, lambda k: True)
    for n in range(tiles, tiles + depth):
        body(n, n % 2, lambda k: n - k < tiles)


def by_pairs(eng, body, tiles):
    body(0, 0)
    body(1, 1)
    with eng.Fori(0, (tiles - 2) // 2) as i:
        for j in range(2):
            body(i * 2 + 2 + j, j)
    if tiles % 2:
        body(tiles - 1, 0)


def norms_of(on):
    return 0 if on(0) else 1, 2 if on(3) else 1


def model_kernel(nc, x, ctx_in, ctxT_in, mask, decay, w_inT, b_in, w_outT, b_out, gamma, beta,
                 f_gateT, f_upT, f_downT, ln_weight, routerT, e_gateT, e_upT, e_downT,
                 s_gateT, s_upT, s_downT, se_gateT, out):
    B, S, D = x.shape
    T = B * S // P
    DC = D // P
    I = f_gateT.shape[1]
    IC = I // P
    NE, _, H = e_gateT.shape
    HC = H // P
    NSH = s_gateT.shape[1] // H
    HT = T // 2
    NBLK = 2 * T + NE - 1
    CH = 512
    NCH = I // CH
    RAW = DC * 2 * H + HC * D
    ATT_SCALE = float(D) ** -0.5
    assert S == P and D == CH and T % 2 == 0

    es = ExitStack()
    with es:
        def sb(name, shape, dt):
            return es.enter_context(nc.sbuf_tensor(name, shape, dt))

        def sem(name):
            return es.enter_context(nc.semaphore(name))

        x_sb = sb("x_sb", [P, T, D], F32)
        big = sb("big", [P, 28672], F32)
        wq = big[:, 0:12288].bitcast(BF16)
        reg_a = big[:, 12288:20480]
        reg_b = big[:, 20480:28672]
        reg_c = sb("reg_c", [P, 8192], F32)
        reg_x = sb("reg_x", [P, DC * T * P], BF16)
        pair = sb("pair", [P, 2 * D], F32)
        gamma_b, beta_b = pair[:, 0:D], pair[:, D:2 * D]
        extra = sb("extra", [P, 1296], F32)
        xq = sb("xq", [P, 2, D], BF16)
        ident_h = sb("ident_h", [P, P], BF16)
        ident16 = sb("ident16", [P, P], F16)
        ident = sb("ident", [P, P], F32)
        small = sb("small", [P, 960], F32)

        cols = [0]

        def tiny(n):
            cols[0] += n
            assert cols[0] <= 960
            return small[:, cols[0] - n:cols[0]]

        ctx_sb = reg_a[:].rearrange("p (t d) -> p t d", t=T)
        y_buf = wq[:, DC * I:].bitcast(F32).rearrange("p (t d) -> p t d", t=T)
        w_in_sb = reg_x[:, 0:2 * DC * D].bitcast(F32).rearrange("p (c e) -> p c e", c=DC)
        w_out_sb = reg_x[:, 2 * DC * D:4 * DC * D].bitcast(F32).rearrange("p (c e) -> p c e", c=DC)
        rows = wq[0:1, 0:4096].bitcast(F32)
        b_in_row, b_out_row = rows[:, 0:D], rows[:, D:2 * D]
        decay_row = rows[:, 2 * D:2 * D + 1]
        keep_row = rows[:, 2 * D + 1:2 * D + 2]
        geo_row = rows[:, 2 * D + 128:2 * D + 256]
        ones_row = rows[:, 2 * D + 256:2 * D + 384]
        wsum_row = rows[:, 2 * D + 384:2 * D + 385]
        wsum16_row = rows[:, 2 * D + 400:2 * D + 400 + T]
        ones = tiny(P)
        cbarT = tiny(DC * T)
        y1T = tiny(DC * T)
        wcols = extra[:, 0:T * T].rearrange("p (t k) -> p t k", t=T)
        cbar = extra[0:T, 256:256 + D]
        y1 = extra[0:T, 768:768 + D]
        sum_f = w_in_sb[0:T, 0, :]
        sum_rest = w_in_sb[0:T, 1, :]
        sum_mid = w_in_sb[0:T, 3, :].bitcast(BF16)[:, 0:D]
        sum_parts = w_in_sb[:, 2, :].bitcast(BF16)[0:96, 0:D]
        pick = xq[0:96, 0, 0:T]
        xqT = reg_x[:].rearrange("p (c n) -> p c n", c=DC)
        raw_gate, raw_up, raw_down = reg_b, reg_c, reg_a
        wq_gate = wq[:, 0:DC * I].rearrange("p (c i) -> p c i", c=DC)
        wq_up = wq[:, DC * I:2 * DC * I].rearrange("p (c i) -> p c i", c=DC)
        wq_down = wq[:, 2 * DC * I:].rearrange("p (c o) -> p c o", c=IC)
        h_buf = reg_c[:, 0:2 * I].rearrange("p (s i) -> p s i", s=2)
        hl_buf = reg_c[:, 2 * I:4 * I].rearrange("p (s i) -> p s i", s=2)
        sg_buf = reg_b[:, 0:2 * CH].rearrange("p (s i) -> p s i", s=2)
        hq = reg_b[:, 1024:2048].bitcast(BF16)
        hqT = reg_b[:, 2048:3072].bitcast(BF16).rearrange("p (c n) -> p c n", c=IC)
        lnw_b = reg_b[:, 4096:4096 + I]
        whole = [wq[:, 0:DC * I], reg_b[:, 0:DC * I // 2].bitcast(BF16), reg_c[:, 0:DC * I // 2].bitcast(BF16)]
        junk = reg_b[:, 3072:3072 + I // 2].bitcast(BF16)
        abs_part = tiny(3 * DC)
        wabs = tiny(3)
        wmean = tiny(3)
        wscale = tiny(3)
        stats_flat = tiny(6 * T)
        stats = stats_flat.rearrange("p (t s) -> p t s", s=6)
        mean2 = tiny(T)
        neg_mean = tiny(T)
        vpe = tiny(T)
        tmp16 = tiny(T)
        rstd = tiny(T)
        neg_half = tiny(T)
        nmr = tiny(T)
        amax = tiny(T)
        s_x = tiny(T)
        dq_gate = tiny(T)
        dq_up = tiny(T)
        sumsq = tiny(2)
        ms = tiny(2)
        rinv = tiny(2)
        hmax = tiny(2)
        rlim = tiny(2)
        rrec = tiny(2)
        s_h = tiny(2)
        dq_h = tiny(2)
        ctxT_at = lambda t: 3 * DC * T * P // 4 + t * D if isinstance(t, int) and t < T // 4 else (t - T // 4) * D
        mask_sb = extra[:, 0:T * P // 4].bitcast(U8)
        negb = reg_x[:, 0:2 * T * P].bitcast(F32).rearrange("p (t m) -> p t m", t=T)
        xh = pair[:].rearrange("p (s d) -> p s d", s=2)
        c_work = big[:, 3 * RAW:4 * RAW]
        xhT = c_work[:, 0:1024].rearrange("p (s d) -> p s d", s=2)
        xn = c_work[:, 1024:2048].rearrange("p (s d) -> p s d", s=2)
        smx = c_work[:, 2048:2304].rearrange("p (s d) -> p s d", s=2)
        prob = c_work[:, 2304:2560].rearrange("p (s d) -> p s d", s=2)
        probT = c_work[:, 2560:2816].rearrange("p (s d) -> p s d", s=2)
        valid = tiny(T)
        nmax = tiny(2)
        rsum = tiny(2)
        rv = tiny(2)
        rv2 = tiny(2)
        st = stats_flat[:, 0:24].rearrange("p (s w k) -> p s w k", s=2, w=2)
        mv = stats_flat[:, 24:32].rearrange("p (s w k) -> p s w k", s=2, w=2)
        ve = stats_flat[:, 32:36].rearrange("p (s w) -> p s w", s=2)
        rs = stats_flat[:, 36:40].rearrange("p (s w) -> p s w", s=2)
        xnT = reg_c[:].bitcast(F16).rearrange("p (c n) -> p c n", c=2 * DC)
        tail = big[:, 9 * RAW:9 * RAW + 1024]
        RS = 1024
        NPC = RAW // RS
        SUMS = [0, 0, 2, 4, 6, 9, 11, 14, 16]
        EARLY = 8
        TAIL_PIECES = ((), (0, 1), (2,))
        SPLITS = [NPC + 1, 6, 8, 12, 16, 20, 24, 27, 27]

        def splits_beside(m, part):
            ahead = 1 if m >= 2 and SPLITS[m + 1] > SPLITS[m] else 0
            return range(SPLITS[m], SPLITS[m] + ahead) if part == 0 else range(SPLITS[m] + ahead, SPLITS[m + 1])

        def wait_low(eng, n):
            eng.wait_ge(w_lo_done, min(n, NPC) + max(n - EARLY, 0))
            if n > NPC:
                eng.wait_ge(w_lo_early, min(n, EARLY) - NPC)

        stage = reg_x[:, 0:2 * RAW].bitcast(F32)
        last_x = reg_x[:, 2 * NPC * RS:2 * NPC * RS + 2048].bitcast(F32)
        xhl = last_x.bitcast(F16).rearrange("p (s n) -> p s n", s=2)
        w_all = big[:, 0:(NE + 1) * RAW].bitcast(F16).rearrange("p (e w) -> p e w", e=NE + 1)
        lower_h = extra[:, 1024:1024 + P // 2].bitcast(BF16)
        ones_h = extra[:, 1088:1088 + P // 2].bitcast(BF16)
        rt_raw = extra[:, 1152:1152 + DC * (NE + 1)].rearrange("p (c e) -> p c e", c=DC)
        rt_hi = extra[:, 1190:1208].bitcast(F16).rearrange("p (c e) -> p c e", c=DC)
        rt_lo = extra[:, 1208:1226].bitcast(F16).rearrange("p (c e) -> p c e", c=DC)
        TE = T * NE
        routed_h = extra[:, 1228:1228 + TE // 2].bitcast(BF16)
        cmp_row = extra[0:1, 0:NBLK * NE].rearrange("p (n e) -> p n e", n=NBLK)

        def routing(n):
            return extra[:, TE * n:TE * (n + 1)].rearrange("p (t e) -> p t e", t=T)

        logit, first, second, cand, scr, iota8 = [routing(n) for n in range(6)]
        carry, before = routing(6), routing(7)
        m1, m2, least1, least2, w1, w2, sgate = [tiny(T) for _ in range(7)]
        e_pair = tiny(2 * T).rearrange("p (k t) -> p k t", k=2)
        blocks, ends, begins = tiny(NE), tiny(NE), tiny(NE)
        ones8 = ones[:, 0:NE]
        slot, place = [xq[:, 1, 4 * T * k:4 * T * (k + 1)].bitcast(F32).rearrange("p (a t) -> p a t", a=2)
                       for k in range(2)]
        slot_u = tiny(2 * T).bitcast(U32).rearrange("p (a t) -> p a t", a=2)
        place_u = tiny(2 * T).bitcast(U32).rearrange("p (a t) -> p a t", a=2)
        token_id = tiny(T).bitcast(U32)
        zeros = xq[:, 0, 0:2 * NBLK].bitcast(U32)
        iota_n = xq[:, 0, 2 * NBLK:4 * NBLK].bitcast(F32)
        expert_f = xq[:, 0, 4 * NBLK:6 * NBLK].bitcast(F32)
        tokens_of = tiny(NBLK).bitcast(U32)
        expert_of = tiny(NBLK).bitcast(U32)
        token_now = tiny(2).bitcast(U32)
        GT = CH // P
        NG = T // GT
        sg_s = pair[:].rearrange("p (s n) -> p s n", s=2)
        hT_s = [v.bitcast(F16).rearrange("p (k c n) -> p k c n", k=2, c=HC) for v in (tail, last_x)]
        xg = extra[:, 0:1024].bitcast(F16).rearrange("p (s n) -> p s n", s=2)
        xgT = tail.bitcast(F16).rearrange("p (s n) -> p s n", s=2)
        sg_r = pair[:, 0:2 * H].rearrange("p (s n) -> p s n", s=2)
        h_hl = pair[:, 2 * H:4 * H].bitcast(F16).rearrange("p (s n) -> p s n", s=2)
        hT_r = xq
        y_out = last_x.rearrange("p (s n) -> p s n", s=2)
        ya = stage.rearrange("p (s n) -> p s n", n=D)

        psum = es.enter_context(nc.psum_tensor("psum", [P, 8 * CH], F32))
        bank = [psum[:, i * CH:(i + 1) * CH] for i in range(8)]

        consts_ready = sem("consts_ready")
        x_landed = [sem(f"x{i}_landed") for i in range(3)]
        wout_landed = sem("wout_landed")
        normed = sem("normed")
        cols_cleared = sem("cols_cleared")
        zg_done = sem("zg_done")
        quant_ready = sem("quant_ready")
        xs_done = sem("xs_done")
        xs_ready = sem("xs_ready")
        pool_shifted = sem("pool_shifted")
        norm_done = sem("norm_done")
        down_whole = sem("down_whole")
        down_shifted = sem("down_shifted")
        rows_landed = sem("rows_landed")
        ctx_landed = [sem(f"ctx_part{i}_landed") for i in range(4)]
        win_landed = sem("win_landed")
        vec_landed = sem("vec_landed")
        raw_landed = [sem(f"raw{i}_landed") for i in range(3)]
        keep_done = sem("keep_done")
        geo_done = sem("geo_done")
        wcol_mm = sem("wcol_mm")
        wcol_done = sem("wcol_done")
        chain_mm = sem("chain_mm")
        chain_done = sem("chain_done")
        bcast_mm = sem("bcast_mm")
        bcast_used = sem("bcast_used")
        dve_a = sem("dve_a")
        var_ready = sem("var_ready")
        rstd_ready = sem("rstd_ready")
        rstd_done = sem("rstd_done")
        xb_done = sem("xb_done")
        abs_done = sem("abs_done")
        abs_mm = sem("abs_mm")
        wscale_done = sem("wscale_done")
        whole_done = sem("whole_done")
        wq_done = sem("wq_done")
        xq_done = sem("xq_done")
        xq_tr = sem("xq_tr")
        xqT_done = sem("xqT_done")
        gate_mm = sem("gate_mm")
        up_mm = sem("up_mm")
        silu_done = sem("silu_done")
        h_done = sem("h_done")
        hl_done = sem("hl_done")
        sq_done = sem("sq_done")
        ms_done = sem("ms_done")
        rinv_done = sem("rinv_done")
        dve_b = sem("dve_b")
        s_h_done = sem("s_h_done")
        hs_done = sem("hs_done")
        hq_done = sem("hq_done")
        hq_tr = sem("hq_tr")
        hqT_a = sem("hqT_a")
        hqT_b = sem("hqT_b")
        down_mm = sem("down_mm")
        x2_done = sem("x2_done")
        mask_landed = sem("mask_landed")
        ctx2_landed = sem("ctx2_landed")
        stats_a = sem("stats_a")
        stats_b = sem("stats_b")
        ve_done = sem("ve_done")
        rs_done = sem("rs_done")
        xh_done = sem("xh_done")
        xh_tr = sem("xh_tr")
        xhT_done = sem("xhT_done")
        score_mm = sem("score_mm")
        nmax_done = sem("nmax_done")
        prob_done = sem("prob_done")
        prob_tr = sem("prob_tr")
        probT_done = sem("probT_done")
        read_mm = sem("read_mm")
        x3_done = sem("x3_done")
        rt_landed = sem("rt_landed")
        rt_done = sem("rt_done")
        iota_done = sem("iota_done")
        dve_d = sem("dve_d")
        xn_done = sem("xn_done")
        xn_tr = sem("xn_tr")
        xnT_done = sem("xnT_done")
        logit_mm = sem("logit_mm")
        edif_done = sem("edif_done")
        eexp_done = sem("eexp_done")
        w_landed = [sem(f"w{i}_landed") for i in range(NE + 2)]
        ctxT_landed = [sem(f"ctxT{i}_landed") for i in range(4)]
        xhl_hi_done = sem("xhl_hi_done")
        xhl_done = sem("xhl_done")
        xn_stored = [sem(f"xn{i}_stored") for i in range(2)]
        hot_done = sem("hot_done")
        rank_mm = sem("rank_mm")
        rank_read = sem("rank_read")
        place_done = sem("place_done")
        table_cleared = sem("table_cleared")
        table_written = sem("table_written")
        table_landed = sem("table_landed")
        tokens_copied = sem("tokens_copied")
        experts_known = sem("experts_known")
        s_gate_mm = sem("s_gate_mm")
        s_up_mm = sem("s_up_mm")
        s_silu = sem("s_silu")
        s_hid = sem("s_hid")
        s_hi = sem("s_hi")
        s_lo = sem("s_lo")
        s_down_mm = sem("s_down_mm")
        xg_landed = [sem(f"xg{i}_landed") for i in range(2)]
        xg_tr = sem("xg_tr")
        xgT_hi = sem("xgT_hi")
        xgT_lo = sem("xgT_lo")
        hr_hi = sem("hr_hi")
        hr_lo = sem("hr_lo")
        hT_done = sem("hT_done")
        y_ready = sem("y_ready")
        y_stored = [sem(f"y{i}_stored") for i in range(2)]
        ya_landed = [sem(f"ya{i}_landed") for i in range(2 * NPC)]
        ya_used = sem("ya_used")
        w_hi_done = sem("w_hi_done")
        w_scaled = sem("w_scaled")
        w_lo_early = sem("w_lo_early")
        w_lo_done = sem("w_lo_done")
        gu_mm = sem("gu_mm")
        silu_d = sem("silu_d")
        hd_done = sem("hd_done")
        hd_tr = sem("hd_tr")
        dn_mm = sem("dn_mm")
        acc_done = sem("acc_done")
        stored = sem("stored")
        lnw_landed = sem("lnw_landed")
        smx_done = sem("smx_done")
        mask_done = sem("mask_done")
        rv_done = sem("rv_done")
        logit_done = sem("logit_done")

        xn_dram = nc.dram_tensor("xn_rows", [T * P, 2 * D], F16).ap()
        table = nc.dram_tensor("token_table", [P * NBLK, 1], U32).ap()
        y_dram = nc.dram_tensor("expert_rows", [NBLK * P, D], F32).ap()

        x_v = x.rearrange("b p d -> p b d")
        out_v = out.rearrange("b p d -> p b d")
        ctx_v = ctx_in.rearrange("b p d -> p b d")
        ctxT_v = ctxT_in.rearrange("b (c p) m -> p c b m", p=P)
        raw_v = [f_gateT.rearrange("(c p) i -> p c i", p=P), f_upT.rearrange("(c p) i -> p c i", p=P),
                 f_downT.rearrange("(c p) o -> p c o", p=P)]
        raw_sb = [raw_gate[:].rearrange("p (c i) -> p c i", c=DC), raw_up[:].rearrange("p (c i) -> p c i", c=DC),
                  raw_down[:].rearrange("p (c o) -> p c o", c=IC)]

        block = es.enter_context(nc.Block())

        flat_raw = [reg_b, reg_c, reg_a]

        def alone(eng):
            eng.nop(nofuse=True)

        def slot_count(t):
            return (t // 2) * 16

        def raw_unit(u):
            return big[:, (u + 1) * RAW:(u + 2) * RAW] if u < NE else stage

        def piece_of(n, part):
            u, k = divmod(n, NPC)
            at = part * RAW + k * RS
            return w_all[:, u % (NE + 1), at:at + RS]

        def raw_piece_of(n):
            return raw_unit(n // NPC)[:, n % NPC * RS:(n % NPC + 1) * RS]

        def tile(buf, t):
            return buf[:, bass.ds(t, 1), :].rearrange("p a d -> p (a d)")

        def raw_piece(m, c):
            return flat_raw[m][:, c * 4 * CH:(c + 1) * 4 * CH]

        DOWN_BY_POOL = 2

        def wait_down(eng, c):
            if c < DOWN_BY_POOL:
                eng.wait_ge(pool_shifted, 8 + c + 1)
            else:
                eng.wait_ge(down_shifted, c - DOWN_BY_POOL + 1)

        @block.sync
        def _(sp):
            for v, r in ((b_in, b_in_row), (b_out, b_out_row)):
                sp.dma_start(r, v.rearrange("(a n) -> a n", a=1)).then_inc(rows_landed, 16)
            sp.dma_start(decay_row, decay).then_inc(rows_landed, 16)
            for q in range(4):
                sp.dma_start(ctx_sb[:, q * T // 4:(q + 1) * T // 4, :],
                             ctx_v[:, q * T // 4:(q + 1) * T // 4, :]).then_inc(ctx_landed[q], 16)
            halves = [slice(h * HT, (h + 1) * HT) for h in range(2)]
            sp.dma_start(x_sb[:, halves[0], :], x_v[:, halves[0], :]).then_inc(x_landed[0], 16)
            sp.dma_start(w_in_sb, w_inT.rearrange("(c p) e -> p c e", p=P)).then_inc(win_landed, 16)
            sp.dma_start(w_out_sb, w_outT.rearrange("(c p) e -> p c e", p=P)).then_inc(wout_landed, 16)
            for v, r in ((gamma, gamma_b), (beta, beta_b)):
                sp.dma_start(r[:], v.partition_broadcast(P)).then_inc(vec_landed, 16)
            for i, r in ((1, slice(HT, HT + HT // 2)), (2, slice(HT + HT // 2, T))):
                sp.dma_start(x_sb[:, r, :], x_v[:, r, :]).then_inc(x_landed[i], 16)
            sp.dma_start(raw_sb[0], raw_v[0]).then_inc(raw_landed[0], 16)
            sp.dma_start(raw_sb[1], raw_v[1]).then_inc(raw_landed[1], 16)
            sp.wait_ge(chain_mm, 1)
            sp.dma_start(raw_sb[2], raw_v[2]).then_inc(raw_landed[2], 16)
            sp.wait_ge(wq_done, 2)
            sp.dma_start(lnw_b, ln_weight.partition_broadcast(P)).then_inc(lnw_landed, 16)
            sp.wait_ge(wq_done, 3)
            sp.dma_start(ctx_sb, ctx_v).then_inc(ctx2_landed, 16)
            sp.dma_start(mask_sb, mask.partition_broadcast(P)).then_inc(mask_landed, 16)
            with nc.allow_non_contiguous_dma(reason="router columns are narrow"):
                sp.dma_start(rt_raw[:, :, 0:NE], routerT.rearrange("(c p) e -> p c e", p=P)).then_inc(rt_landed, 16)
                sp.dma_start(rt_raw[:, :, NE:NE + 1], se_gateT.rearrange("(c p) e -> p c e", p=P)).then_inc(rt_landed, 16)
            for q in range(4):
                if q == 1:
                    sp.wait_ge(x2_done, T)
                for c in range(DC):
                    at = ctxT_at(q * T // 4)
                    sp.dma_start(reg_b[:, at:at + T // 4 * D].rearrange("p (b c m) -> p b c m", b=T // 4, c=DC)[:, :, c, :],
                                 ctxT_v[:, c, q * T // 4:(q + 1) * T // 4, :]).then_inc(ctxT_landed[q], 16)
            sp.wait_ge(iota_done, 3)
            sp.dma_start(table.rearrange("(p n) a -> p (n a)", n=NBLK), zeros).then_inc(table_cleared, 16)

            def load_weights(u):
                if 1 <= u <= NE:
                    gate_w, up_w, down_w = e_gateT[u - 1], e_upT[u - 1], e_downT[u - 1]
                else:
                    v = u // NE
                    gate_w, up_w, down_w = [s_gateT[:, v * H:(v + 1) * H], s_upT[:, v * H:(v + 1) * H],
                                            s_downT[v * H:(v + 1) * H, :]]
                raw = raw_unit(u)
                gu = raw[:, 0:DC * 2 * H].rearrange("p (c g i) -> p c g i", c=DC, g=2)
                for g, w in ((0, gate_w), (1, up_w)):
                    sp.dma_start(gu[:, :, g, :], w.rearrange("(c p) i -> p c i", p=P)).then_inc(w_landed[u], 16)
                sp.dma_start(raw[:, DC * 2 * H:].rearrange("p (c o) -> p c o", c=HC),
                             down_w.rearrange("(c p) o -> p c o", p=P)).then_inc(w_landed[u], 16)

            for u in range(2):
                load_weights(u)
            for t in range(T):
                sp.wait_ge(xhl_done, t + 1)
                sp.dma_start(xn_dram[t * P:(t + 1) * P, :], xhl[:, t % 2, :]).then_inc(xn_stored[t % 2], 16)
            sp.wait_ge(x3_done, T)
            for u in range(2, NE + 1):
                load_weights(u)
            sp.wait_ge(table_written, 2 * T * 16)
            sp.dma_start(tokens_of, table.rearrange("(p n) a -> p (n a)", n=NBLK)).then_inc(table_landed, 16)
            wait_low(sp, (NE + 1) * NPC)
            load_weights(NE + 1)

            def store_rows(n, j):
                sp.wait_ge(y_ready, n + 3)
                sp.dma_start(y_dram[bass.ds(n * P, P), :], y_out[:, j, :]).then_inc(y_stored[j], 16)

            by_pairs(sp, store_rows, NBLK)
            for t in range(0, T, 2):
                sp.wait_ge(acc_done, T + t + 2)
                sp.dma_start(out_v[:, t:t + 2, :], x_sb[:, t:t + 2, :]).then_inc(stored, 16)
            sp.wait_ge(stored, 16 * T // 2)

        @block.gpsimd
        def _(pool):
            pool.memset(ident[:], 0.0).then_inc(consts_ready, 1)
            pool.memset(ident_h[:], 0.0).then_inc(consts_ready, 1)
            pool.memset(ident16[:], 0.0).then_inc(consts_ready, 1)
            pool.memset(ones, 1.0).then_inc(consts_ready, 1)
            pool.memset(neg_half, -0.5).then_inc(consts_ready, 1)
            pool.memset(ones_row, 1.0).then_inc(consts_ready, 1)
            pool.wait_ge(consts_ready, 6)
            for m in (ident, ident_h, ident16):
                pool.affine_select(out=m[:], in_=m[:], compare_op=ALU.not_equal, fill=1.0, base=0,
                                   pattern=[[-1, P]], channel_multiplier=1).then_inc(consts_ready, 1)
            pool.memset(extra[:, 0:T * T], 0.0).then_inc(cols_cleared, 1)
            pool.wait_ge(consts_ready, 9)

            def deviations(k, h):
                pool.wait_ge(var_ready, 2 * k + h + 1)
                pool.tensor_tensor(rstd[:, h * HT:(h + 1) * HT], vpe[:, h * HT:(h + 1) * HT],
                                   neg_half[:, 0:HT], ALU.pow).then_inc(rstd_ready if k == 2 else rstd_done, 1)
                if k == 2:
                    return
                pool.wait_ge(rstd_done, 2 * k + h + 1)
                pool.tensor_tensor(nmr[:, h * HT:(h + 1) * HT], neg_mean[:, h * HT:(h + 1) * HT],
                                   rstd[:, h * HT:(h + 1) * HT], ALU.mult).then_inc(rstd_ready, 1)

            def add_beta(first, end):
                with pool.Fori(first, end) as i:
                    for t in (i * 4, i * 4 + 1, i * 4 + 2, i * 4 + 3):
                        pool.wait_ge(normed, t + 1)
                        pool.tensor_tensor(tile(x_sb, t), tile(x_sb, t), beta_b, ALU.add).then_inc(xb_done, 1)

            def times_gamma(first, end):
                with pool.Fori(first, end) as i:
                    for t in (i * 4, i * 4 + 1, i * 4 + 2, i * 4 + 3):
                        pool.wait_ge(normed, t + (T + 1))
                        pool.tensor_tensor(tile(y_buf, t), tile(y_buf, t), gamma_b, ALU.mult).then_inc(zg_done, 1)

            deviations(0, 0)
            pool.wait_ge(vec_landed, 32)
            add_beta(0, 1)
            deviations(0, 1)
            for q in range(1, T // 4):
                add_beta(q, q + 1)
            deviations(1, 0)
            times_gamma(0, 2)
            deviations(1, 1)
            times_gamma(2, 3)
            deviations(2, 0)
            times_gamma(3, T // 4)

            def shift(m, pieces=range(4)):
                pool.wait_ge(raw_landed[m], 16)
                pool.wait_ge(wscale_done, m + 1)
                for c in pieces:
                    pool.tensor_scalar(raw_piece(m, c), raw_piece(m, c), wscale[:, m:m + 1], MAGIC, ALU.mult, ALU.add)\
                        .then_inc(pool_shifted, 1)

            shift(0)
            shift(1)
            shift(2, range(1))
            deviations(2, 1)
            pool.wait_ge(rstd_ready, 6)
            for t in range(HT, T):
                pool.tensor_scalar(tile(y_buf, t), tile(x_sb, t), neg_mean[:, t:t + 1], rstd[:, t:t + 1],
                                   ALU.add, ALU.mult).then_inc(norm_done, 1)

            def shift_back_down(c):
                wait_down(pool, c)
                pool.tensor_scalar(whole[2][:, c * 4 * CH:(c + 1) * 4 * CH], raw_piece(2, c), 1.0, -MAGIC,
                                   ALU.mult, ALU.add).then_inc(down_whole, 1)

            shift(2, range(1, DOWN_BY_POOL))
            pool.wait_ge(quant_ready, 2)
            pool.wait_ge(norm_done, HT)
            for t in range(HT, T):
                pool.tensor_scalar(tile(y_buf, t), tile(y_buf, t), s_x[:, t:t + 1], MAGIC,
                                   ALU.mult, ALU.add).then_inc(xs_ready, 1)
            pool.wait_ge(whole_done, 8)
            for c in range(1, 4):
                shift_back_down(c)
            pool.wait_ge(lnw_landed, 16)
            with pool.Fori(0, T // 2) as i:
                for j in range(2):
                    t = i * 2 + j
                    pool.wait_ge(hq_done, t + 1)
                    for c in range(NCH):
                        pool.wait_ge(h_done, t * NCH + c + 3)
                        pool.tensor_tensor(hl_buf[:, j, c * CH:(c + 1) * CH], h_buf[:, j, c * CH:(c + 1) * CH],
                                           lnw_b[:, c * CH:(c + 1) * CH], ALU.mult).then_inc(hl_done, 1)
                    pool.wait_ge(sq_done, t + 1)
                    alone(pool)
                    pool.tensor_scalar(ms[:, j:j + 1], sumsq[:, j:j + 1], 1.0 / I, RMS_EPS, ALU.mult, ALU.add)\
                        .then_inc(ms_done, 1)
                    pool.wait_ge(ms_done, t + 1)
                    pool.tensor_tensor(rinv[:, j:j + 1], ms[:, j:j + 1], neg_half[:, 0:1], ALU.pow)\
                        .then_inc(rinv_done, 1)
            pool.iota(iota8, pattern=[[0, T], [1, NE]], base=0, channel_multiplier=0,
                      allow_small_or_imprecise_dtypes=True).then_inc(iota_done, 1)
            pool.iota(iota_n, pattern=[[1, NBLK]], base=0, channel_multiplier=0,
                      allow_small_or_imprecise_dtypes=True).then_inc(iota_done, 1)
            pool.memset(zeros, 0).then_inc(iota_done, 1)
            pool.iota(token_id, pattern=[[P, T]], base=0, channel_multiplier=1).then_inc(iota_done, 1)
            pool.memset(lower_h, 1.0).then_inc(iota_done, 1)
            pool.memset(ones_h, 1.0).then_inc(iota_done, 1)
            pool.wait_ge(iota_done, 6)
            pool.affine_select(out=lower_h, in_=lower_h, compare_op=ALU.is_gt, fill=0.0, base=0,
                               pattern=[[1, P]], channel_multiplier=-1).then_inc(iota_done, 1)

            def early_low(n):
                pool.wait_ge(w_hi_done, n + 1)
                pool.tensor_tensor(piece_of(n, 1), raw_piece_of(n), piece_of(n, 0), ALU.subtract).then_inc(w_lo_early, 1)

            def attend(n, j, on):
                lo, hi = norms_of(on)
                b = 1 - j
                if lo < hi:
                    pool.wait_ge(ve_done, n + 1)
                    pool.tensor_tensor(rs[:, j, lo:hi], ve[:, j, lo:hi], neg_half[:, lo:hi], ALU.pow).then_inc(rs_done, 1)
                if on(3):
                    pool.wait_ge(xhl_hi_done, n - 2)
                    pool.tensor_tensor(xhl[:, b, D:2 * D], xn[:, b, :], xhl[:, b, 0:D], ALU.subtract).then_inc(xhl_done, 1)

            staged(pool, attend, T, 5)
            for n in range(NPC, EARLY):
                early_low(n)
            pool.wait_ge(table_cleared, 16)
            pool.wait_ge(place_done, 1)
            for a in range(2):
                for t in range(T):
                    pool.indirect_dma_start(table, bass.IndirectOffsetOnAxis(place_u[:, a, t:t + 1], 0),
                                            token_id[:, t:t + 1], None).then_inc(table_written, 16)
            pool.wait_ge(table_landed, 16)
            pool.wait_ge(experts_known, 1)
            for j in range(2):
                pool.wait_ge(xn_stored[j], T // 2 * 16)

            def gather_tokens(n, j):
                if not isinstance(n, int) or n >= 2:
                    pool.wait_ge(xg_tr, n - 1)
                    alone(pool)
                pool.tensor_copy(token_now[:, j:j + 1], tokens_of[:, bass.ds(n, 1)]).then_inc(tokens_copied, 1)
                pool.wait_ge(tokens_copied, n + 1)
                alone(pool)
                pool.indirect_dma_start(xg[:, j, :], None, xn_dram,
                                        bass.IndirectOffsetOnAxis(token_now[:, j:j + 1], 0)).then_inc(xg_landed[j], 16)

            by_pairs(pool, gather_tokens, NBLK)
            pool.wait_ge(y_stored[0], (NBLK + 1) // 2 * 16)
            pool.wait_ge(y_stored[1], NBLK // 2 * 16)
            wait_low(pool, (NE + 2) * NPC)
            for n in range(2 * T):
                s = n % (2 * NPC)
                if n >= 2 * NPC:
                    pool.wait_ge(ya_used, n - 2 * NPC + 1)
                pool.indirect_dma_start(ya[:, s, :], None, y_dram,
                                        bass.IndirectOffsetOnAxis(slot_u[:, n % 2, n // 2:n // 2 + 1], 0))\
                    .then_inc(ya_landed[s], 16)

        @block.scalar
        def _(act):
            act.wait_ge(rows_landed, 48)
            act.activation(keep_row, decay_row, ACT.Tanh, scale=0.5).then_inc(keep_done, 1)
            def norm_tiles(dst, src, k, h, done):
                act.wait_ge(rstd_ready, 2 * k + h + 1)
                with act.Fori(h * HT // 4, (h + 1) * HT // 4) as i:
                    for t in (i * 4, i * 4 + 1, i * 4 + 2, i * 4 + 3):
                        act.activation(tile(dst, t), tile(src, t), ACT.Identity, scale=rstd[:, bass.ds(t, 1)],
                                       bias=nmr[:, bass.ds(t, 1)]).then_inc(done, 1)

            def abs_sums(m):
                act.wait_ge(raw_landed[m], 16)
                for c in range(4):
                    if m or c:
                        act.wait_ge(abs_done, 4 * m + c)
                    act.activation(psum[:, 4 * CH:8 * CH], raw_piece(m, c), ACT.Abs,
                                   accum_out=abs_part[:, 4 * m + c:4 * m + c + 1]).then_inc(abs_done, 1)

            def quantise():
                act.wait_ge(quant_ready, 1)
                with act.Fori(0, HT // 4) as i:
                    for t in (i * 4, i * 4 + 1, i * 4 + 2, i * 4 + 3):
                        act.activation(tile(y_buf, t), tile(y_buf, t), ACT.Copy, scale=s_x[:, bass.ds(t, 1)],
                                       bias=MAGIC).then_inc(xs_done, 1)

            act.wait_ge(chain_mm, 1)
            act.activation(cbar, bank[1][0:T, :], ACT.Copy).then_inc(chain_done, 1)
            act.wait_ge(chain_mm, 2)
            act.activation(cbarT, bank[0][:, 64:64 + DC * T], ACT.Copy).then_inc(chain_done, 1)
            act.wait_ge(chain_mm, 3)
            act.activation(y1, bank[1][0:T, :], ACT.Copy).then_inc(chain_done, 1)
            act.wait_ge(chain_mm, 4)
            act.activation(y1T, bank[0][:, 128:128 + DC * T], ACT.Copy).then_inc(chain_done, 1)
            norm_tiles(y_buf, x_sb, 0, 0, normed)
            norm_tiles(y_buf, x_sb, 0, 1, normed)
            abs_sums(0)
            norm_tiles(y_buf, y_buf, 1, 0, normed)
            abs_sums(1)
            norm_tiles(y_buf, y_buf, 1, 1, normed)
            abs_sums(2)

            def evac_xq(t, j):
                act.wait_ge(xq_tr, t + 3)
                alone(act)
                act.activation(xqT[:, :, bass.ds(t * P, P)], bank[2 + j].bitcast(BF16)[:, 0:D]
                               .rearrange("p (c n) -> p c n", c=DC), ACT.Copy).then_inc(xqT_done, 1)

            def shift_back(m):
                for c in range(4):
                    act.wait_ge(pool_shifted, 4 * m + c + 1)
                    act.activation(whole[m][:, c * 4 * CH:(c + 1) * 4 * CH], raw_piece(m, c), ACT.Copy,
                                   bias=-MAGIC).then_inc(whole_done, 1)

            shift_back(0)
            quantise()
            act.wait_ge(whole_done, 4)
            shift_back(1)
            by_pairs(act, evac_xq, HT)
            act.wait_ge(wscale_done, 3)
            for c in range(DOWN_BY_POOL, 4):
                act.activation(raw_piece(2, c), raw_piece(2, c), ACT.Copy, scale=wscale[:, 2:3],
                               bias=MAGIC).then_inc(down_shifted, 1)
            with act.Fori(HT // 2, T // 2) as i:
                for j in range(2):
                    evac_xq(i * 2 + j, j)
            act.wait_ge(whole_done, 8)
            wait_down(act, 0)
            act.activation(whole[2][:, 0:4 * CH], raw_piece(2, 0), ACT.Copy, bias=-MAGIC).then_inc(whole_done, 1)

            def ffn(t, j, now, back1, back2):
                def silu(c):
                    if now:
                        act.wait_ge(gate_mm, t * NCH + c + 1)
                        alone(act)
                        act.activation(sg_buf[:, c % 2, :], bank[c % 2], ACT.Silu,
                                       scale=dq_gate[:, bass.ds(t, 1)]).then_inc(silu_done, 1)

                if now and isinstance(t, int) and t == 0:
                    act.wait_ge(wq_done, 2)
                silu(0)
                silu(1)
                if back2:
                    act.wait_ge(hq_tr, (t - 2) * 2 + 1)
                    act.activation(hqT[:, 0:IC // 2, :], bank[4].bitcast(BF16).rearrange("p (c n) -> p c n", n=P),
                                   ACT.Copy).then_inc(hqT_a, 1)
                silu(2)
                if back1:
                    act.wait_ge(s_h_done, t)
                    act.activation(hl_buf[:, 1 - j, :], hl_buf[:, 1 - j, :], ACT.Copy, bias=MAGIC,
                                   scale=s_h[:, 1 - j:2 - j]).then_inc(hs_done, 1)
                silu(3)
                if now:
                    act.wait_ge(h_done, t * NCH + NCH + 2)
                    act.activation(junk, h_buf[:, j, :], ACT.Square,
                                   accum_out=sumsq[:, j:j + 1]).then_inc(sq_done, 1)


            def router_high():
                act.wait_ge(rt_landed, 32)
                act.activation(rt_hi, rt_raw, ACT.Copy, scale=WSCALE).then_inc(rt_done, 1)

            def split_high(n):
                if n % NPC == 0:
                    act.wait_ge(w_landed[n // NPC], 48)
                    if n >= NPC:
                        wait_low(act, n)
                early = NPC <= n < EARLY
                if early:
                    act.activation(raw_piece_of(n), raw_piece_of(n), ACT.Copy, scale=WSCALE).then_inc(w_scaled, 1)
                    act.wait_ge(w_scaled, n - NPC + 1)
                act.activation(piece_of(n, 0), raw_piece_of(n), ACT.Copy, scale=1.0 if early else WSCALE)\
                   .then_inc(w_hi_done, 1)

            def attend(n, j, on):
                b = 1 - j
                if on(1):
                    act.wait_ge(xh_tr, n)
                    act.activation(xhT[:, b, :], bank[7 * b], ACT.Copy).then_inc(xhT_done, 1)
                if on(2):
                    act.wait_ge(prob_tr, n - 1)
                    act.activation(probT[:, j, :], bank[2][:, 0:P], ACT.Copy).then_inc(probT_done, 1)
                if on(4):
                    act.wait_ge(xn_tr, n - 3)
                    alone(act)
                    act.activation(xnT[:, :, bass.ds((n - 4) * P, P)],
                                   bank[5].bitcast(F16).rearrange("p (c n) -> p c n", c=2 * DC),
                                   ACT.Copy).then_inc(xnT_done, 1)
                if on(3):
                    act.wait_ge(xn_done, n - 2)
                    if not isinstance(n, int) or n - 3 >= 2:
                        act.wait_ge(xn_tr, n - 4)
                        act.wait_ge(xn_stored[b], (n - 3) // 2 * 16)
                    act.activation(xhl[:, b, 0:D], xn[:, b, :], ACT.Copy).then_inc(xhl_hi_done, 1)
                if on(1):
                    act.wait_ge(nmax_done, n)
                    act.activation(prob[:, b, :], smx[:, b, :], ACT.Exp, bias=nmax[:, b:b + 1],
                                   accum_out=rsum[:, b:b + 1]).then_inc(prob_done, 1)
                if isinstance(n, int) and T <= n < T + NPC:
                    split_high(n - T)

            pipelined(act, ffn, T, before_last=router_high)
            staged(act, attend, T, 5, first=1)

            def shared(v):
                for g in range(NG):
                    for c in range(HC):
                        m = (v * NG + g) * HC + c
                        act.wait_ge(s_gate_mm, m + 1)
                        if m >= 2:
                            act.wait_ge(s_lo, m - 1)
                        act.activation(sg_s[:, m % 2, :], bank[m % 2], ACT.Silu, scale=1.0 / WSCALE).then_inc(s_silu, 1)
                        if v == 0:
                            for n in splits_beside(m, 0):
                                split_high(n)
                        act.wait_ge(s_hid, m + 1)
                        if g >= 2:
                            act.wait_ge(s_down_mm, (v * NG + g - 1) * GT)
                        act.activation(hT_s[g % 2][:, 0, c, :], sg_s[:, m % 2, :], ACT.Copy).then_inc(s_hi, 1)
                        if v == 0:
                            for n in splits_beside(m, 1):
                                split_high(n)
                if v == 0:
                    routed(0, 0, True, False, False)

            for j in range(2):
                act.wait_ge(xn_stored[j], T // 2 * 16)

            def routed(t, j, now, back1, back2):
                b = 1 - j
                if back1:
                    act.wait_ge(gu_mm, t)
                    act.activation(sg_r[:, b, :], bank[b][:, 0:H], ACT.Silu, scale=1.0 / WSCALE).then_inc(silu_d, 1)
                if now:
                    act.wait_ge(xg_tr, t + 1)
                    act.activation(xgT[:, j, 0:D], bank[2].bitcast(F16)[:, 0:D], ACT.Copy).then_inc(xgT_hi, 1)
                if back1:
                    act.wait_ge(hd_done, t)
                    act.activation(h_hl[:, b, 0:H], sg_r[:, b, :], ACT.Copy).then_inc(hr_hi, 1)
                if isinstance(t, int) and t in (NBLK - 1, NBLK):
                    for n in ((0, 1), (2,))[t - NBLK + 1]:
                        split_high((NE + 1) * NPC + n)
                if back2:
                    act.wait_ge(dn_mm, t - 1)
                    if not isinstance(t, int) or t >= 4:
                        act.wait_ge(y_stored[j], slot_count(t - 2))
                    act.activation(y_out[:, j, :], bank[4 + j], ACT.Copy).then_inc(y_ready, 1)

            split_high(NPC)
            act.wait_ge(edif_done, 1)
            act.activation(e_pair, e_pair, ACT.Exp).then_inc(eexp_done, 1)
            shared(0)
            act.sem_inc(y_ready, 2)
            pipelined(act, routed, NBLK, first=1)
            for j in range(2):
                act.wait_ge(y_stored[j], (NBLK + 1 - j) // 2 * 16)
            shared(1)

        @block.tensor
        def _(pe):
            pe.wait_ge(consts_ready, 9)
            pe.wait_ge(geo_done, 1)
            pe.matmul(bank[0][:, 0:1], geo_row, ones_row[:, 0:1], start=True, stop=True).then_inc(wcol_mm, 1)
            pe.wait_ge(wcol_done, 1)
            for t in range(T):
                if t % (T // 4) == 0:
                    pe.wait_ge(ctx_landed[t // (T // 4)], 16)
                last = pe.matmul(bank[1][0:T, :], wcols[:, t, :], ctx_sb[:, t, :], start=(t == 0), stop=(t == T - 1))
            last.then_inc(chain_mm, 1)
            pe.wait_ge(chain_done, 1)
            for c in range(DC):
                last = pe.transpose(bank[0][:, 64 + c * T:64 + (c + 1) * T], cbar[:, c * P:(c + 1) * P], ident[0:T, 0:T])
            last.then_inc(chain_mm, 1)
            pe.wait_ge(chain_done, 2)
            pe.wait_ge(win_landed, 16)
            for c in range(DC):
                pe.matmul(bank[1][0:T, :], cbarT[:, c * T:(c + 1) * T], w_in_sb[:, c, :], start=(c == 0), stop=False)
            pe.matmul(bank[1][0:T, :], wsum16_row, b_in_row, start=False, stop=True).then_inc(chain_mm, 1)
            pe.wait_ge(chain_done, 3)
            for c in range(DC):
                last = pe.transpose(bank[0][:, 128 + c * T:128 + (c + 1) * T], y1[:, c * P:(c + 1) * P], ident[0:T, 0:T])
            last.then_inc(chain_mm, 1)
            pe.wait_ge(chain_done, 4)
            pe.wait_ge(wout_landed, 16)
            for c in range(DC):
                pe.matmul(bank[1][0:T, :], y1T[:, c * T:(c + 1) * T], w_out_sb[:, c, :], start=(c == 0), stop=False)
            pe.matmul(bank[1][0:T, :], ones_row[:, 0:T], b_out_row, start=False, stop=True).then_inc(chain_mm, 1)
            pe.wait_ge(chain_done, 6)
            for t in range(T):
                if t >= 4:
                    pe.wait_ge(bcast_used, t - 3)
                pe.matmul(bank[t % 4], pick[:, t:t + 1].to_broadcast([96, P]), sum_parts,
                          start=True, stop=True).then_inc(bcast_mm, 1)
            for m in range(3):
                pe.wait_ge(abs_done, 4 * m + 4)
                if m == 0:
                    pe.wait_ge(bcast_used, T)
                if m == 2:
                    pe.wait_ge(wscale_done, 1)
                pe.matmul(bank[m % 2][:, 256 + 4 * m:260 + 4 * m], ones, abs_part[:, 4 * m:4 * m + 4],
                          start=True, stop=True).then_inc(abs_mm, 1)

            def turn_xq(t, j):
                pe.wait_ge(xq_done, t + 1)
                if not isinstance(t, int):
                    pe.wait_ge(xqT_done, t - 1)
                for c in range(DC):
                    last = pe.transpose(bank[2 + j].bitcast(BF16)[:, c * P:(c + 1) * P],
                                        xq[:, j, c * P:(c + 1) * P], ident_h[:])
                last.then_inc(xq_tr, 1)

            by_pairs(pe, turn_xq, T)

            def ffn(t, j, now, back1, back2):
                def gate_up(c, parts=(0, 1)):
                    if not now:
                        return
                    if 0 in parts:
                        pe.wait_ge(h_done, t * NCH + c + 1)
                    for part in parts:
                        m, w, done = ((0, wq_gate, gate_mm), (2, wq_up, up_mm))[part]
                        for k in range(DC):
                            last = pe.matmul(bank[m + c % 2], xqT[:, k, bass.ds(t * P, P)],
                                             w[:, k, c * CH:(c + 1) * CH], start=(k == 0), stop=(k == DC - 1))
                        last.then_inc(done, 1)

                if now and isinstance(t, int) and t == 0:
                    pe.wait_ge(xqT_done, 1)
                    pe.wait_ge(wscale_done, 3)
                    pe.wait_ge(wq_done, 1)
                    gate_up(0, (0,))
                    gate_up(1, (0,))
                    pe.wait_ge(xqT_done, T)
                    pe.wait_ge(wq_done, 2)
                    gate_up(0, (1,))
                    gate_up(1, (1,))
                else:
                    gate_up(0)
                    gate_up(1)
                if back2:
                    pe.wait_ge(hq_done, t + 1)
                    for half, sem_h in ((0, hqT_a), (1, hqT_b)):
                        for c in range(IC // 2):
                            k = half * IC // 2 + c
                            last = pe.transpose(bank[4 + half].bitcast(BF16)[:, c * P:(c + 1) * P],
                                                hq[:, k * P:(k + 1) * P], ident_h[:])
                        last.then_inc(hq_tr, 1)
                gate_up(2)
                if back2:
                    if isinstance(t, int) and t == 2 or not isinstance(t, int):
                        pe.wait_ge(wq_done, 3)
                    pe.wait_ge(hqT_a, t - 1)
                    pe.wait_ge(hqT_b, t - 1)
                    for k in range(IC):
                        last = pe.matmul(bank[6 + j], hqT[:, k, :], wq_down[:, k, :],
                                         start=(k == 0), stop=(k == IC - 1))
                    last.then_inc(down_mm, 1)
                gate_up(3)

            pipelined(pe, ffn, T)

            pe.wait_ge(rt_done, 2)
            pe.wait_ge(ctx2_landed, 16)
            pe.wait_ge(ctxT_landed[0], 16 * DC)

            def attend(n, j, on):
                b = 1 - j
                if on(1):
                    pe.wait_ge(xh_done, n)
                    for c in range(DC):
                        last = pe.transpose(bank[7 * b][:, c * P:(c + 1) * P], xh[:, b, c * P:(c + 1) * P], ident[:])
                    last.then_inc(xh_tr, 1)
                if on(2):
                    pe.wait_ge(prob_done, n - 1)
                    pe.transpose(bank[2][:, 0:P], prob[:, j, :], ident[:]).then_inc(prob_tr, 1)
                if on(1):
                    if isinstance(n, int) and n == T // 4 + 1:
                        pe.wait_ge(ctxT_landed[1], 16 * DC)
                    pe.wait_ge(xhT_done, n)
                    for c in range(DC):
                        last = pe.matmul(bank[1][:, 0:P], xhT[:, b, c * P:(c + 1) * P],
                                         reg_b[:, bass.ds(ctxT_at(n - 1) + c * P, P)],
                                         start=(c == 0), stop=(c == DC - 1))
                    last.then_inc(score_mm, 1)
                if on(4):
                    pe.wait_ge(xhl_done, n - 3)
                    for c in range(2 * DC):
                        last = pe.transpose(bank[5].bitcast(F16)[:, c * P:(c + 1) * P],
                                            xhl[:, j, c * P:(c + 1) * P], ident16[:])
                    last.then_inc(xn_tr, 1)
                if on(5):
                    pe.wait_ge(xnT_done, n - 4)
                    if not isinstance(n, int) or n > 5:
                        pe.wait_ge(logit_done, n * 2 - 10)
                    i = 0
                    for part, ww in ((0, rt_hi), (0, rt_lo), (1, rt_hi)):
                        for c in range(DC):
                            last = pe.matmul(bank[6][:, 0:NE + 1], xnT[:, part * DC + c, bass.ds((n - 5) * P, P)],
                                             ww[:, c, :], start=(i == 0), stop=(i == 3 * DC - 1))
                            i += 1
                    last.then_inc(logit_mm, 1)
                if on(2):
                    pe.wait_ge(probT_done, n - 1)
                    pe.matmul(bank[3 + j], probT[:, j, :], ctx_sb[:, bass.ds(n - 2, 1), :]
                              .rearrange("p a d -> p (a d)"), start=True, stop=True).then_inc(read_mm, 1)

            staged(pe, attend, T, 5, first=1,
                   before={q * T // 4: lambda q=q: pe.wait_ge(ctxT_landed[q], 16 * DC) for q in (2, 3)})
            def rank():
                pe.wait_ge(hot_done, 1)
                pe.matmul(bank[6][:, 0:TE], lower_h, routed_h, start=True, stop=True)
                pe.matmul(bank[7][:, 0:TE], ones_h, routed_h, start=True, stop=True).then_inc(rank_mm, 1)

            def shared_down(v, g, dn):
                done = (v * NG + g) * HC
                for c in range(HC):
                    pe.wait_ge(s_hi, done + c + 1)
                    pe.wait_ge(s_lo, done + c + 1)
                    for k in range(GT):
                        n = (v * NG + g) * GT + k
                        if c == 0 and n == 0:
                            pe.wait_ge(rank_read, 1)
                        if c == 0 and n >= GT:
                            pe.wait_ge(acc_done, n - GT + 1)
                        for i, (part, ww) in enumerate(((0, 0), (0, 1), (1, 0))):
                            last = pe.matmul(bank[4 + k], hT_s[g % 2][:, part, c, k * P:(k + 1) * P], dn[ww][:, c, :],
                                             start=(c == 0 and i == 0), stop=(c == HC - 1 and i == 2))
                        if c == HC - 1:
                            last.then_inc(s_down_mm, 1)

            def shared(v):
                gu, dn = weights_of(0)
                wait_low(pe, NPC if v == 0 else (NE + 2) * NPC)
                for g in range(NG):
                    for c in range(HC):
                        m = (v * NG + g) * HC + c
                        if m >= 2:
                            pe.wait_ge(s_hid, m - 1)
                        for x_or_y, at, done in ((0, 0, s_gate_mm), (2, H, s_up_mm)):
                            i = 0
                            for part, ww in ((0, 0), (0, 1), (1, 0)):
                                for k in range(DC):
                                    last = pe.matmul(bank[x_or_y + m % 2],
                                                     gu[ww][:, k, at + c * P:at + (c + 1) * P],
                                                     xnT[:, part * DC + k, g * CH:(g + 1) * CH],
                                                     start=(i == 0), stop=(i == 3 * DC - 1))
                                    i += 1
                            last.then_inc(done, 1)
                        if m == 1:
                            rank()
                        if c == 0 and g:
                            shared_down(v, g - 1, dn)
                shared_down(v, NG - 1, dn)

            def weights_of(e):
                w = w_all[:, e, :] if isinstance(e, int) else w_all[:, bass.ds(e, 1), :].rearrange("p a w -> p (a w)")
                gu = [w[:, p * RAW:p * RAW + DC * 2 * H].rearrange("p (c i) -> p c i", c=DC) for p in range(2)]
                dn = [w[:, p * RAW + DC * 2 * H:(p + 1) * RAW].rearrange("p (c o) -> p c o", c=HC) for p in range(2)]
                return gu, dn

            def routed(t, j, now, back1, back2):
                b = 1 - j
                if isinstance(t, int) and t == 1:
                    wait_low(pe, (NE + 1) * NPC)
                    pe.wait_ge(experts_known, 1)
                    alone(pe)
                if back1:
                    gu, _ = weights_of(pe.value_load(expert_of[0:1, bass.ds(t - 1, 1)], min_val=1, max_val=NE))
                if back2:
                    _, dn = weights_of(pe.value_load(expert_of[0:1, bass.ds(t - 2, 1)], min_val=1, max_val=NE))
                if back1:
                    pe.wait_ge(xgT_hi, t)
                    if not isinstance(t, int) or t >= 3:
                        pe.wait_ge(hd_done, t - 2)
                    n = 0
                    for part, ww in ((0, 0), (0, 1), (1, 0)):
                        if part == 1:
                            pe.wait_ge(xgT_lo, t)
                        for c in range(DC):
                            at = (part * DC + c) * P
                            last = pe.matmul(bank[b], xgT[:, b, at:at + P], gu[ww][:, c, :],
                                             start=(n == 0), stop=(n == 3 * DC - 1))
                            n += 1
                        if n == DC and back2:
                            turn_hidden(t, j)
                    last.then_inc(gu_mm, 1)
                elif back2:
                    turn_hidden(t, j)
                if now:
                    pe.wait_ge(xg_landed[j], slot_count(t) + 16)
                    if not isinstance(t, int) or t >= 1:
                        pe.wait_ge(xgT_lo, t)
                        pe.wait_ge(xgT_hi, t)
                    for c in range(2 * DC):
                        last = pe.transpose(bank[2 + c // DC].bitcast(F16)[:, c % DC * P:(c % DC + 1) * P],
                                            xg[:, j, c * P:(c + 1) * P], ident16[:])
                    last.then_inc(xg_tr, 1)
                if back2:
                    pe.wait_ge(hT_done, t - 1)
                    pe.wait_ge(y_ready, t - 1)
                    n = 0
                    for part, ww in ((0, 0), (0, 1), (1, 0)):
                        for c in range(HC):
                            at = (part * HC + c) * P
                            last = pe.matmul(bank[4 + j], hT_r[:].bitcast(F16)[:, j, at:at + P], dn[ww][:, c, :],
                                             start=(n == 0), stop=(n == 3 * HC - 1))
                            n += 1
                    last.then_inc(dn_mm, 1)

            def turn_hidden(t, j):
                pe.wait_ge(hr_hi, t - 1)
                pe.wait_ge(hr_lo, t - 1)
                for c in range(2 * HC):
                    last = pe.transpose(bank[6 + j].bitcast(F16)[:, c * P:(c + 1) * P],
                                        h_hl[:, j, c * P:(c + 1) * P], ident16[:])
                last.then_inc(hd_tr, 1)

            pe.wait_ge(xnT_done, T)
            shared(0)

            pipelined(pe, routed, NBLK)
            shared(1)

        @block.vector
        def _(dve):
            dve.sem_inc(h_done, 2)
            dve.sem_inc(hq_done, 2)

            dve.wait_ge(consts_ready, 9)
            dve.wait_ge(keep_done, 1)
            dve.tensor_scalar(keep_row, keep_row, 0.5, 0.5, ALU.mult, ALU.add).then_inc(dve_a, 1)
            dve.wait_ge(dve_a, 1)
            dve.tensor_tensor_scan(geo_row[:, ::-1], keep_row.to_broadcast([1, S]), ones_row, 0.0,
                                   ALU.mult, ALU.add).then_inc(geo_done, 1)
            dve.wait_ge(geo_done, 1)
            dve.reduce_sum(wsum_row, geo_row, AX.X).then_inc(dve_a, 1)
            dve.wait_ge(dve_a, 2)
            dve.tensor_scalar(wsum16_row, ones_row[:, 0:T], wsum_row, 1.0 / S, ALU.mult, ALU.mult).then_inc(dve_a, 1)
            dve.wait_ge(wcol_mm, 1)
            dve.wait_ge(cols_cleared, 1)
            dve.tensor_scalar(extra[:, 0:T * T:T + 1], bank[0][:, 0:1].to_broadcast([P, T]), 1.0 / S, None, ALU.mult)\
               .then_inc(wcol_done, 1)
            count = [3]

            def step(ins, times=1):
                ins.then_inc(dve_a, 1)
                count[0] += times

            def settle():
                dve.wait_ge(dve_a, count[0])

            def stats_of(buf, h, halfway=None):
                for q in range(h * HT // 4, (h + 1) * HT // 4):
                    if halfway and q == h * HT // 4 + 1:
                        halfway()
                    with dve.Fori(q, q + 1) as i:
                        for t in (i * 4, i * 4 + 1, i * 4 + 2, i * 4 + 3):
                            ins = dve.bn_stats(stats[:, bass.ds(t, 1), :].rearrange("p a d -> p (a d)"), tile(buf, t))
                            ins.then_inc(dve_a, 1)
                count[0] += HT
                settle()
                r = slice(h * HT, (h + 1) * HT)
                step(dve.tensor_tensor(mean2[:, r], stats[:, r, 1], stats[:, r, 4], ALU.add))
                step(dve.tensor_tensor(tmp16[:, r], stats[:, r, 1], stats[:, r, 4], ALU.subtract))
                step(dve.tensor_tensor(vpe[:, r], stats[:, r, 2], stats[:, r, 5], ALU.add))
                settle()
                step(dve.scalar_tensor_tensor(tmp16[:, r], tmp16[:, r], 0.25, tmp16[:, r], ALU.mult, ALU.mult))
                step(dve.tensor_scalar(vpe[:, r], vpe[:, r], 1.0 / D, LN_EPS, ALU.mult, ALU.add))
                step(dve.tensor_scalar(neg_mean[:, r], mean2[:, r], -0.5, None, ALU.mult))
                settle()
                dve.tensor_tensor(vpe[:, r], vpe[:, r], tmp16[:, r], ALU.add).then_inc(var_ready, 1)

            def add_summary(h):
                with dve.Fori(h * HT // 4, (h + 1) * HT // 4) as i:
                    for t, k in ((i * 4, 0), (i * 4 + 1, 1), (i * 4 + 2, 2), (i * 4 + 3, 3)):
                        dve.wait_ge(normed, t + 1)
                        dve.wait_ge(bcast_mm, t + 1)
                        dve.tensor_tensor(tile(y_buf, t), tile(y_buf, t), bank[k], ALU.add).then_inc(bcast_used, 1)
                dve.wait_ge(bcast_used, (h + 1) * HT)

            def add_norm(h):
                with dve.Fori(h * HT // 4, (h + 1) * HT // 4) as i:
                    for t in (i * 4, i * 4 + 1, i * 4 + 2, i * 4 + 3):
                        dve.wait_ge(xb_done, t + 1)
                        dve.wait_ge(zg_done, t + 1)
                        ins = dve.tensor_tensor(tile(x_sb, t), tile(y_buf, t), tile(x_sb, t), ALU.add)
                        ins.then_inc(dve_a, 1)
                count[0] += HT
                settle()

            def norm_half():
                dve.wait_ge(rstd_ready, 5)
                with dve.Fori(0, HT // 4) as i:
                    for t in (i * 4, i * 4 + 1, i * 4 + 2, i * 4 + 3):
                        dve.tensor_scalar(tile(y_buf, t), tile(x_sb, t), neg_mean[:, bass.ds(t, 1)],
                                          rstd[:, bass.ds(t, 1)], ALU.add, ALU.mult).then_inc(dve_a, 1)
                count[0] += HT
                settle()

            def largest(t):
                dve.tensor_reduce(amax[:, bass.ds(t, 1)], tile(y_buf, t), AX.X, ALU.max,
                                  apply_absolute_value=True).then_inc(dve_a, 1)

            def token_scales(h):
                r = slice(h * HT, (h + 1) * HT)
                count[0] += HT
                settle()
                step(dve.tensor_scalar(amax[:, r], amax[:, r], QUANT_EPS, None, ALU.max))
                settle()
                step(dve.reciprocal(s_x[:, r], amax[:, r]))
                settle()
                dve.tensor_scalar(s_x[:, r], s_x[:, r], QMAX, None, ALU.mult).then_inc(quant_ready, 1)
                for m, dq in ((0, dq_gate), (1, dq_up)):
                    step(dve.tensor_scalar(dq[:, r], amax[:, r], wmean[:, m:m + 1], 1.0 / QMAX, ALU.mult, ALU.mult))

            def store_xq(t, j):
                dve.wait_ge(xq_tr, t + 1)
                dve.tensor_scalar(xq[:, j, :], tile(y_buf, t), MAGIC, None, ALU.subtract).then_inc(xq_done, 1)

            def weight_scale(m):
                dve.wait_ge(abs_mm, m + 1)
                step(dve.reduce_sum(wabs[:, m:m + 1], bank[m % 2][:, 256 + 4 * m:260 + 4 * m], AX.X))
                settle()
                step(dve.tensor_scalar(wmean[:, m:m + 1], wabs[:, m:m + 1], 1.0 / (I * D), QUANT_EPS, ALU.mult, ALU.max))
                settle()
                dve.reciprocal(wscale[:, m:m + 1], wmean[:, m:m + 1]).then_inc(wscale_done, 1)

            def hold(m):
                if m < 2:
                    dve.wait_ge(whole_done, 4 * m + 4)
                else:
                    dve.wait_ge(whole_done, 9)
                    dve.wait_ge(down_whole, 3)
                for c in range(4):
                    last = dve.tensor_scalar(wq[:, (4 * m + c) * 4 * CH:(4 * m + c + 1) * 4 * CH],
                                             whole[m][:, c * 4 * CH:(c + 1) * 4 * CH], 1.0, -1.0, ALU.min, ALU.max)
                last.then_inc(wq_done, 1)

            dve.sem_inc(xq_tr, 2)
            dve.wait_ge(x_landed[0], 16)
            stats_of(x_sb, 0)
            dve.wait_ge(x_landed[1], 16)
            stats_of(x_sb, 1, halfway=lambda: dve.wait_ge(x_landed[2], 16))
            dve.wait_ge(chain_mm, 3)
            step(dve.memset(sum_parts, 0.0))
            step(dve.tensor_tensor(pick, ident_h[0:96, 0:T], ident_h[0:96, 32:32 + T], ALU.add))
            settle()
            step(dve.tensor_tensor(pick, pick, ident_h[0:96, 64:64 + T], ALU.add))
            dve.wait_ge(chain_mm, 5)
            step(dve.tensor_copy(sum_f, bank[1][0:T, :]))
            settle()
            step(dve.tensor_copy(sum_parts[0:T], sum_f))
            settle()
            step(dve.tensor_tensor(sum_rest, sum_f, sum_parts[0:T], ALU.subtract))
            settle()
            step(dve.tensor_copy(sum_mid, sum_rest))
            settle()
            dve.tensor_copy(sum_parts[32:32 + T], sum_mid).then_inc(chain_done, 1)
            dve.tensor_tensor(sum_parts[64:64 + T], sum_rest, sum_mid, ALU.subtract).then_inc(chain_done, 1)
            for h in range(2):
                add_summary(h)
                stats_of(y_buf, h)
            weight_scale(0)
            add_norm(0)
            weight_scale(1)
            stats_of(x_sb, 0)
            norm_half()
            with dve.Fori(0, HT // 4) as i:
                for t in (i * 4, i * 4 + 1, i * 4 + 2, i * 4 + 3):
                    largest(t)
            token_scales(0)
            weight_scale(2)
            add_norm(1)
            stats_of(x_sb, 1)
            hold(0)
            with dve.Fori(0, HT // 2) as i:
                for j in range(2):
                    dve.wait_ge(xs_done, i * 2 + (j + 1))
                    store_xq(i * 2 + j, j)
                    dve.wait_ge(norm_done, i * 2 + (j + 1))
                    largest(i * 2 + (HT + j))
            token_scales(1)
            with dve.Fori(HT // 2, T // 2) as i:
                for j in range(2):
                    t = i * 2 + j
                    dve.wait_ge(xs_ready, t - (HT - 1))
                    store_xq(t, j)
            dve.wait_ge(xq_done, T)
            hold(1)
            step(dve.tensor_scalar(wmean[:, 0:1], wmean[:, 2:3], 1.0 / QMAX, None, ALU.mult))
            hold(2)
            dve.wait_ge(wq_done, 3)

            def ffn(t, j, now, back1, back2):
                def hidden(c):
                    if now:
                        dve.wait_ge(up_mm, t * NCH + c + 1)
                        dve.wait_ge(silu_done, t * NCH + c + 1)
                        dve.scalar_tensor_tensor(h_buf[:, j, c * CH:(c + 1) * CH], bank[2 + c % 2],
                                                 dq_up[:, bass.ds(t, 1)], sg_buf[:, c % 2, :],
                                                 ALU.mult, ALU.mult).then_inc(h_done, 1)

                b = 1 - j
                hidden(0)
                hidden(1)
                if back2:
                    dve.wait_ge(hq_tr, (t - 2) * 2 + 2)
                    dve.tensor_copy(hqT[:, IC // 2:, :], bank[5].bitcast(BF16).rearrange("p (c n) -> p c n", n=P))\
                       .then_inc(hqT_b, 1)
                    if isinstance(t, int) and t == T + 1:
                        attend(0, 0, lambda k: k == 0)
                if back1:
                    k = (t - 1) * 4
                    dve.wait_ge(hl_done, t * NCH)
                    dve.tensor_reduce(hmax[:, b:b + 1], hl_buf[:, b, :], AX.X, ALU.max,
                                      apply_absolute_value=True).then_inc(dve_b, 1)
                    dve.wait_ge(rinv_done, t)
                    dve.wait_ge(dve_b, k + 1)
                    dve.tensor_scalar(rlim[:, b:b + 1], hmax[:, b:b + 1], rinv[:, b:b + 1], QUANT_EPS,
                                      ALU.mult, ALU.max).then_inc(dve_b, 1)
                    dve.wait_ge(dve_b, k + 2)
                    dve.reciprocal(rrec[:, b:b + 1], rlim[:, b:b + 1]).then_inc(dve_b, 1)
                    dve.wait_ge(dve_b, k + 3)
                    dve.tensor_scalar(s_h[:, b:b + 1], rrec[:, b:b + 1], rinv[:, b:b + 1], QMAX,
                                      ALU.mult, ALU.mult).then_inc(s_h_done, 1)
                    dve.tensor_scalar(dq_h[:, b:b + 1], rlim[:, b:b + 1], wmean[:, 0:1], None,
                                      ALU.mult).then_inc(dve_b, 1)
                hidden(2)
                hidden(3)
                if back1:
                    dve.wait_ge(hs_done, t)
                    dve.tensor_scalar(hq, hl_buf[:, b, :], MAGIC, None, ALU.subtract).then_inc(hq_done, 1)
                if back2:
                    dve.wait_ge(down_mm, t - 1)
                    dve.scalar_tensor_tensor(tile(x_sb, t - 2), bank[6 + j], dq_h[:, j:j + 1], tile(x_sb, t - 2),
                                             ALU.mult, ALU.add).then_inc(x2_done, 1)


            def split_low(n):
                dve.wait_ge(w_hi_done, n + 1)
                dve.scalar_tensor_tensor(piece_of(n, 1), raw_piece_of(n), WSCALE, piece_of(n, 0),
                                         ALU.mult, ALU.subtract).then_inc(w_lo_done, 1)

            def attend(n, j, on):
                b = 1 - j
                lo, hi = norms_of(on)
                if on(0):
                    alone(dve)
                    dve.bn_stats(st[:, j, 0, :], tile(x_sb, n)).then_inc(stats_a, 1)
                if on(3):
                    dve.wait_ge(x3_done, n - 2)
                    alone(dve)
                    dve.bn_stats(st[:, j, 1, :], tile(x_sb, n - 3)).then_inc(stats_b, 1)
                if isinstance(n, int) and n == 0:
                    dve.wait_ge(mask_landed, 16)
                    dve.tensor_reduce(valid, mask_sb.rearrange("p (t m) -> p t m", t=T), AX.X, ALU.max)\
                       .then_inc(mask_done, 1)
                    dve.tensor_scalar(negb.rearrange("p t m -> p (t m)"), mask_sb, -1.0, -MASKED, ALU.add, ALU.mult)\
                       .then_inc(mask_done, 1)
                    dve.wait_ge(rt_done, 1)
                    dve.scalar_tensor_tensor(rt_lo, rt_raw, WSCALE, rt_hi, ALU.mult, ALU.subtract).then_inc(rt_done, 1)
                    dve.wait_ge(mask_done, 2)
                if on(0):
                    dve.wait_ge(stats_a, n * 2 + 1)
                    alone(dve)
                    dve.bn_aggr(mv[:, j, 0, :], st[:, j, 0, :]).then_inc(stats_a, 1)
                if on(2):
                    dve.wait_ge(prob_done, n - 1)
                    dve.reciprocal(rv[:, j:j + 1], rsum[:, j:j + 1]).then_inc(rv_done, 1)
                if on(3):
                    dve.wait_ge(stats_b, n * 2 - 5)
                    alone(dve)
                    dve.bn_aggr(mv[:, j, 1, :], st[:, j, 1, :]).then_inc(stats_b, 1)
                if lo < hi:
                    if on(0):
                        dve.wait_ge(stats_a, n * 2 + 2)
                    if on(3):
                        dve.wait_ge(stats_b, n * 2 - 4)
                    dve.tensor_scalar(ve[:, j, lo:hi], mv[:, j, lo:hi, 1], LN_EPS, None, ALU.add).then_inc(ve_done, 1)
                if on(1):
                    dve.wait_ge(score_mm, n)
                    dve.scalar_tensor_tensor(smx[:, b, :], bank[1][:, 0:P], ATT_SCALE, tile(negb, n - 1),
                                             ALU.mult, ALU.add).then_inc(smx_done, 1)
                if on(2):
                    dve.wait_ge(rv_done, n * 2 - 3)
                    dve.tensor_tensor(rv2[:, j:j + 1], rv[:, j:j + 1], valid[:, bass.ds(n - 2, 1)], ALU.mult)\
                       .then_inc(rv_done, 1)
                if on(1):
                    dve.wait_ge(smx_done, n)
                    dve.tensor_reduce(nmax[:, b:b + 1], smx[:, b, :], AX.X, ALU.max, negate=True)\
                       .then_inc(nmax_done, 1)
                if on(3):
                    dve.wait_ge(rs_done, n + 1)
                    dve.tensor_scalar(xn[:, b, :], tile(x_sb, n - 3), mv[:, j, 1, 0:1], rs[:, j, 1:2],
                                      ALU.subtract, ALU.mult).then_inc(xn_done, 1)
                if on(0):
                    dve.wait_ge(rs_done, n + 1)
                    dve.tensor_scalar(xh[:, j, :], tile(x_sb, n), mv[:, j, 0, 0:1], rs[:, j, 0:1],
                                      ALU.subtract, ALU.mult).then_inc(xh_done, 1)
                if isinstance(n, int) and T < n <= T + NPC:
                    for piece in TAIL_PIECES[n - T - 1]:
                        split_low(piece)
                if on(5):
                    dve.wait_ge(logit_mm, n - 4)
                    dve.tensor_scalar(tile(logit, n - 5), bank[6][:, 0:NE], 1.0 / WSCALE, None, ALU.mult)\
                       .then_inc(logit_done, 1)
                    dve.tensor_scalar(e_pair[:, 1, bass.ds(n - 5, 1)], bank[6][:, NE:NE + 1], -1.0 / WSCALE,
                                      None, ALU.mult).then_inc(logit_done, 1)
                if on(2):
                    dve.wait_ge(rv_done, n * 2 - 2)
                    dve.wait_ge(read_mm, n - 1)
                    dve.scalar_tensor_tensor(tile(x_sb, n - 2), bank[3 + j], rv2[:, j:j + 1], tile(x_sb, n - 2),
                                             ALU.mult, ALU.add).then_inc(x3_done, 1)

            pipelined(dve, ffn, T)
            dve.wait_ge(x2_done, T)
            staged(dve, attend, T, 5, first=1)

            n = 0
            dve.wait_ge(logit_done, 2 * T)
            dve.wait_ge(iota_done, 1)

            def wide(v):
                return v.unsqueeze(2).to_broadcast([P, T, NE])

            def step(ins):
                ins.then_inc(dve_d, 1)

            for a, (src, m, least, hot) in enumerate(((logit, m1, least1, first), (scr, m2, least2, second))):
                step(dve.tensor_reduce(m, src, AX.X, ALU.max))
                dve.wait_ge(dve_d, n + 1)
                step(dve.tensor_tensor(cand, src, wide(m), ALU.is_ge))
                dve.wait_ge(dve_d, n + 2)
                step(dve.scalar_tensor_tensor(cand, cand, -2.0 * NE, iota8, ALU.mult, ALU.add))
                dve.wait_ge(dve_d, n + 3)
                step(dve.tensor_reduce(least, cand, AX.X, ALU.min))
                dve.wait_ge(dve_d, n + 4)
                step(dve.tensor_tensor(hot, cand, wide(least), ALU.is_equal))
                dve.wait_ge(dve_d, n + 5)
                n += 5
                if a == 0:
                    step(dve.scalar_tensor_tensor(scr, first, MASKED, logit, ALU.mult, ALU.add))
                    dve.wait_ge(dve_d, n + 1)
                    n += 1
            dve.tensor_tensor(e_pair[:, 0, :], m2, m1, ALU.subtract).then_inc(edif_done, 1)
            dve.wait_ge(eexp_done, 1)
            step(dve.tensor_scalar(w1, e_pair[:, 0, :], 1.0, None, ALU.add))
            step(dve.tensor_scalar(w2, e_pair[:, 1, :], 1.0, None, ALU.add))
            dve.wait_ge(dve_d, n + 2)
            step(dve.reciprocal(w1, w1))
            step(dve.reciprocal(w2, w2))
            dve.wait_ge(dve_d, n + 4)
            step(dve.tensor_scalar(w1, w1, 1.0 / WSCALE, None, ALU.mult))
            step(dve.tensor_scalar(sgate, w2, 1.0 / WSCALE, None, ALU.mult))
            dve.wait_ge(dve_d, n + 6)
            step(dve.tensor_tensor(w2, e_pair[:, 0, :], w1, ALU.mult))
            dve.tensor_tensor(routed_h.rearrange("p (e t) -> p t e", e=NE), first, second, ALU.add).then_inc(hot_done, 1)
            step(dve.memset(carry.rearrange("p t e -> p (t e)"), 1.0))
            n += 8
            dve.wait_ge(dve_d, n)
            carry_v = carry.rearrange("p t e -> p (t e)").rearrange("p (e t) -> p e t", e=NE)
            step(dve.memset(carry_v[:, :, 0:1], 0.0))

            def split_pieces(m, part):
                for n in splits_beside(m, part):
                    if n >= EARLY:
                        split_low(n)

            def shared_hidden(v, m):
                g, c = m // HC % NG, m % HC
                dve.wait_ge(s_up_mm, m + 1)
                dve.wait_ge(s_silu, m + 1)
                dve.scalar_tensor_tensor(sg_s[:, m % 2, :], bank[2 + m % 2], 1.0 / WSCALE, sg_s[:, m % 2, :],
                                         ALU.mult, ALU.mult).then_inc(s_hid, 1)
                if v == 0 and 2 <= m:
                    split_pieces(m, 0)
                dve.wait_ge(s_hi, m + 1)
                dve.tensor_tensor(hT_s[g % 2][:, 1, c, :], sg_s[:, m % 2, :], hT_s[g % 2][:, 0, c, :],
                                  ALU.subtract).then_inc(s_lo, 1)

            shared_hidden(0, 0)
            shared_hidden(0, 1)
            dve.wait_ge(rank_mm, 1)
            flat = lambda v: v.rearrange("p t e -> p (t e)")
            step(dve.tensor_copy(flat(cand), bank[7][:, 0:TE]))
            dve.tensor_copy(flat(iota8), bank[6][:, 0:TE]).then_inc(rank_read, 1)
            dve.wait_ge(dve_d, n + 2)
            step(dve.tensor_tensor_scan(flat(scr), flat(carry), flat(cand), 0.0, ALU.mult, ALU.add))
            dve.wait_ge(dve_d, n + 3)
            n += 3
            total = flat(scr).rearrange("p (e t) -> p e t", e=NE)[:, :, T - 1:T].rearrange("p e t -> p (e t)")
            step(dve.tensor_scalar(blocks, total, 1.0 / P, 0.5 - 0.5 / P, ALU.mult, ALU.add))
            step(dve.tensor_tensor(flat(before), flat(scr), flat(cand), ALU.subtract))
            dve.wait_ge(dve_d, n + 2)
            step(dve.tensor_scalar(blocks, blocks, MAGIC, None, ALU.add))
            dve.wait_ge(rank_read, 1)
            step(dve.tensor_tensor(flat(before), flat(before), flat(iota8), ALU.add))
            dve.wait_ge(dve_d, n + 4)
            step(dve.tensor_scalar(blocks, blocks, MAGIC, None, ALU.subtract))
            dve.wait_ge(dve_d, n + 5)
            step(dve.tensor_tensor_scan(ends, ones8, blocks, 0.0, ALU.mult, ALU.add))
            dve.wait_ge(dve_d, n + 6)
            step(dve.tensor_tensor(begins, ends, blocks, ALU.subtract))
            dve.wait_ge(dve_d, n + 7)
            n += 7
            before_v = flat(before).rearrange("p (e t) -> p e t", e=NE)
            step(dve.scalar_tensor_tensor(before_v, begins.unsqueeze(2).to_broadcast([P, NE, T]), float(P), before_v,
                                          ALU.mult, ALU.add))
            dve.wait_ge(dve_d, n + 1)
            before_t = flat(before).rearrange("p (e t) -> p t e", e=NE)
            step(dve.tensor_tensor(first, first, before_t, ALU.mult))
            step(dve.tensor_tensor(second, second, before_t, ALU.mult))
            dve.wait_ge(dve_d, n + 3)
            step(dve.reduce_sum(slot[:, 0, :], first, AX.X))
            step(dve.reduce_sum(slot[:, 1, :], second, AX.X))
            dve.wait_ge(dve_d, n + 5)
            n += 5
            step(dve.tensor_scalar(place, slot, 1.0 / P, 0.5 / P - 0.5, ALU.mult, ALU.add))
            step(dve.tensor_copy(slot_u, slot))
            dve.wait_ge(dve_d, n + 2)
            step(dve.tensor_scalar(place, place, MAGIC, None, ALU.add))
            dve.wait_ge(dve_d, n + 3)
            step(dve.tensor_scalar(place, place, MAGIC, None, ALU.subtract))
            step(dve.tensor_scalar(slot, slot, float(NBLK), None, ALU.mult))
            dve.wait_ge(dve_d, n + 5)
            step(dve.scalar_tensor_tensor(place, place, 1.0 - NBLK * P, slot, ALU.mult, ALU.add))
            dve.wait_ge(dve_d, n + 6)
            dve.tensor_copy(place_u, place).then_inc(place_done, 1)
            n += 6
            step(dve.tensor_tensor(cmp_row, iota_n[0:1, :].unsqueeze(2).to_broadcast([1, NBLK, NE]),
                                   ends[0:1, :].unsqueeze(1).to_broadcast([1, NBLK, NE]), ALU.is_ge))
            dve.wait_ge(dve_d, n + 1)
            step(dve.reduce_sum(expert_f[0:1, :], cmp_row, AX.X))
            dve.wait_ge(dve_d, n + 2)
            dve.tensor_scalar(expert_of[0:1, :], expert_f[0:1, :], float(NE - 1), 1.0, ALU.min, ALU.add).then_inc(experts_known, 1)
            n += 2

            def shared_sum(v, g):
                for k in range(GT):
                    t = g * GT + k
                    m = v * T + t
                    dve.wait_ge(s_down_mm, m + 1)
                    if v:
                        dve.wait_ge(ya_used, 2 * t + 2)
                    dve.scalar_tensor_tensor(x_sb[:, t, :], bank[4 + k], sgate[:, t:t + 1], x_sb[:, t, :],
                                             ALU.mult, ALU.add).then_inc(acc_done, 1)

            def routed_sum(t):
                for a, w in ((0, w1), (1, w2)):
                    i = 2 * t + a
                    dve.wait_ge(ya_landed[i % (2 * NPC)], 16 * (i // (2 * NPC) + 1))
                    if a:
                        dve.wait_ge(ya_used, i)
                    dve.scalar_tensor_tensor(x_sb[:, t, :], ya[:, i % (2 * NPC), :], w[:, t:t + 1], x_sb[:, t, :],
                                             ALU.mult, ALU.add).then_inc(ya_used, 1)

            def shared(v):
                for g in range(NG):
                    for c in range(HC):
                        m = (v * NG + g) * HC + c
                        if v:
                            for t in range(SUMS[m - NG * HC], SUMS[m - NG * HC + 1]):
                                routed_sum(t)
                        if v or m >= 2:
                            shared_hidden(v, m)
                        if v == 0:
                            if m < 2:
                                split_pieces(m, 0)
                            split_pieces(m, 1)
                        if c == 0 and g:
                            shared_sum(v, g - 1)
                if v == 0:
                    routed(0, 0, True, False, False)
                shared_sum(v, NG - 1)

            def routed(t, j, now, back1, back2):
                b = 1 - j
                if back2:
                    dve.wait_ge(hd_tr, t - 1)
                    dve.tensor_copy(hT_r[:].bitcast(F16)[:, j, :], bank[6 + j].bitcast(F16)[:, 0:2 * H])\
                       .then_inc(hT_done, 1)
                if back1:
                    dve.wait_ge(silu_d, t)
                    dve.scalar_tensor_tensor(sg_r[:, b, :], bank[b][:, H:2 * H], 1.0 / WSCALE, sg_r[:, b, :],
                                             ALU.mult, ALU.mult).then_inc(hd_done, 1)
                if now:
                    dve.wait_ge(xg_tr, t + 1)
                    dve.tensor_copy(xgT[:, j, D:2 * D], bank[3].bitcast(F16)[:, 0:D]).then_inc(xgT_lo, 1)
                if back1:
                    dve.wait_ge(hr_hi, t)
                    dve.tensor_tensor(h_hl[:, b, H:2 * H], sg_r[:, b, :], h_hl[:, b, 0:H], ALU.subtract)\
                       .then_inc(hr_lo, 1)
                if isinstance(t, int) and t in (NBLK - 1, NBLK):
                    for n in ((0, 1), (2,))[t - NBLK + 1]:
                        split_low((NE + 1) * NPC + n)

            shared(0)
            pipelined(dve, routed, NBLK, first=1)
            shared(1)


def kernel(x, ctx_2048, mask_BxS2_bk0, L0_xattn_decay, L0_xattn_W_in, L0_xattn_b_in, L0_xattn_W_out, L0_xattn_b_out,
           L0_xattn_gamma, L0_xattn_beta, L0_ffn_w_gate, L0_ffn_w_up, L0_ffn_w_down, L0_ffn_ln_weight, L1_ffn_gate_w,
           L1_ffn_w_gate, L1_ffn_w_up, L1_ffn_w_down, L1_ffn_sh_gate, L1_ffn_sh_up, L1_ffn_sh_down, L1_ffn_se_gate_w):
    import concourse.bacc as bacc
    from concourse.bass_utils import run_bass_kernel_spmd

    def lay(a, *perm):
        a = np.asarray(a)
        return np.ascontiguousarray(a.transpose(perm) if perm else a)

    arrays = {
        "x": lay(x), "ctx": lay(ctx_2048), "ctxT": lay(ctx_2048, 0, 2, 1),
        "mask": lay(mask_BxS2_bk0).reshape(-1), "decay": lay(L0_xattn_decay).reshape(1, 1),
        "w_inT": lay(L0_xattn_W_in, 1, 0), "b_in": lay(L0_xattn_b_in),
        "w_outT": lay(L0_xattn_W_out, 1, 0), "b_out": lay(L0_xattn_b_out),
        "gamma": lay(L0_xattn_gamma), "beta": lay(L0_xattn_beta),
        "f_gateT": lay(L0_ffn_w_gate, 1, 0), "f_upT": lay(L0_ffn_w_up, 1, 0), "f_downT": lay(L0_ffn_w_down, 1, 0),
        "ln_weight": lay(L0_ffn_ln_weight), "routerT": lay(L1_ffn_gate_w, 1, 0),
        "e_gateT": lay(L1_ffn_w_gate, 0, 2, 1), "e_upT": lay(L1_ffn_w_up, 0, 2, 1),
        "e_downT": lay(L1_ffn_w_down, 0, 2, 1),
        "s_gateT": lay(L1_ffn_sh_gate, 1, 0), "s_upT": lay(L1_ffn_sh_up, 1, 0), "s_downT": lay(L1_ffn_sh_down, 1, 0),
        "se_gateT": lay(L1_ffn_se_gate_w, 1, 0),
    }
    nc = bacc.Bacc("TRN2", target_bir_lowering=False, num_devices=1)
    args = [nc.dram_tensor(f"in_{k}", a.shape, mybir.dt.from_np(a.dtype), kind="ExternalInput").ap()
            for k, a in arrays.items()]
    out = nc.dram_tensor("out_x", np.asarray(x).shape, F32, kind="ExternalOutput").ap()
    model_kernel(nc, *args, out)
    r = run_bass_kernel_spmd(nc, [{f"in_{k}": a for k, a in arrays.items()}], core_ids=[0])
    return r.results[0]["out_x"]
```
